# Optimizing a Trainium2 kernel written in Bass

```python
import numpy as np
import jax
import jax.numpy as jnp

def _softmax(x, axis=-1):
    return jax.nn.softmax(x, axis=axis)

def _gelu(x):
    return jax.nn.gelu(x, approximate=True)

def _silu(x):
    return jax.nn.silu(x)

def _sigmoid(x):
    return jax.nn.sigmoid(x)

def _layernorm(x, axis=-1, eps=1e-05):
    m = jnp.mean(x, axis=axis, keepdims=True)
    v = jnp.var(x, axis=axis, keepdims=True)
    return (x - m) / jnp.sqrt(v + eps)

def _scatter_add(tgt, idx, src, axis=0):
    return tgt.at[idx].add(src)

def _segment_sum(src, seg, n):
    return jax.ops.segment_sum(src, seg, n)
kernel_name = 'mk_vit_tower_d1_tok_img1024_r4_8304e5'

def setup_inputs(seed: int=0):
    np.random.seed(seed)
    _w = jnp.asarray

    def _rec_inputs():
        import jax
        import jax.numpy as jnp
        _rk = jax.random.key(seed)
        x = -0.000348323 + 0.999952 * jax.random.normal(jax.random.fold_in(_rk, 1), (32, 3, 128, 128), jnp.float32)
        return x
    x = _rec_inputs()

    def _L0_tok_setup():
        import jax, jax.numpy as jnp
        import numpy as np
        from jax import lax
        PATCH = 16
        key = jax.random.key(seed)
        k1, k2 = jax.random.split(key)
        B, C, IMG, HID = (32, 3, 96, 256)
        inputs = jax.random.normal(k1, (B, C, IMG, IMG), dtype=jnp.float32)
        flat = C * PATCH * PATCH
        W = jax.random.normal(k2, (flat, HID), dtype=jnp.float32) / np.sqrt(flat)
        return {'inputs': inputs, 'W': W}
    _L0_tok_all = _L0_tok_setup()
    _L0_tok_in = {k: v for k, v in _L0_tok_all.items() if k in ('W',)}
    del _L0_tok_all

    def _L0_attn_setup():
        import jax, jax.numpy as jnp
        import numpy as np
        D_MODEL, D_QKV, N_HEADS = (256, 64, 16)
        key = jax.random.key(seed)
        k_x, k_qkv, k_out = jax.random.split(key, 3)
        X = jax.random.normal(k_x, (2, 512, D_MODEL), dtype=jnp.float32)
        W_qkv = jax.random.normal(k_qkv, (D_MODEL, 3 * D_QKV * N_HEADS), dtype=jnp.float32) * D_MODEL ** (-0.5)
        W_out = jax.random.normal(k_out, (D_QKV * N_HEADS, D_MODEL), dtype=jnp.float32) * (D_QKV * N_HEADS) ** (-0.5)
        return {'X': X, 'W_qkv': W_qkv, 'W_out': W_out}
    _L0_attn_all = _L0_attn_setup()
    _L0_attn_in = {k: v for k, v in _L0_attn_all.items() if k in ('W_qkv', 'W_out')}
    del _L0_attn_all

    def _L0_ffn_setup():
        import jax, jax.numpy as jnp
        import numpy as np
        B, S, H, NH, E, F = (4, 256, 256, 16, 8, 1024)
        D = H // NH
        EPS = 1e-05

        def _layernorm(x, g, b):
            mu = jnp.mean(x, axis=-1, keepdims=True)
            var = jnp.var(x, axis=-1, keepdims=True)
            return (x - mu) * jax.lax.rsqrt(var + EPS) * g + b
        key = jax.random.key(seed)
        ks = jax.random.split(key, 16)
        s = 0.02
        return {'x': jax.random.normal(ks[0], (B, S, H), jnp.float32), 'ln1_g': jnp.ones((H,), jnp.float32), 'ln1_b': jnp.zeros((H,), jnp.float32), 'ln2_g': jnp.ones((H,), jnp.float32), 'ln2_b': jnp.zeros((H,), jnp.float32), 'wq': jax.random.normal(ks[1], (H, H), jnp.float32) * s, 'bq': jnp.zeros((H,), jnp.float32), 'wk': jax.random.normal(ks[2], (H, H), jnp.float32) * s, 'bk': jnp.zeros((H,), jnp.float32), 'wv': jax.random.normal(ks[3], (H, H), jnp.float32) * s, 'bv': jnp.zeros((H,), jnp.float32), 'wo': jax.random.normal(ks[4], (H, H), jnp.float32) * s, 'bo': jnp.zeros((H,), jnp.float32), 'gate_w': jax.random.normal(ks[5], (H, E), jnp.float32) * s, 'gate_b': jnp.zeros((E,), jnp.float32), 'w1': jax.random.normal(ks[6], (E, H, F), jnp.float32) * s, 'b1': jnp.zeros((E, F), jnp.float32), 'w2': jax.random.normal(ks[7], (E, F, H), jnp.float32) * s, 'b2': jnp.zeros((E, H), jnp.float32)}
    _L0_ffn_all = _L0_ffn_setup()
    _L0_ffn_in = {k: v for k, v in _L0_ffn_all.items() if k in ('ln1_g', 'ln1_b', 'ln2_g', 'ln2_b', 'wq', 'bq', 'wk', 'bk', 'wv', 'bv', 'wo', 'bo', 'gate_w', 'gate_b', 'w1', 'b1', 'w2', 'b2')}
    del _L0_ffn_all
    return {'x': x, 'L0_tok_W': _L0_tok_in['W'], 'L0_attn_W_qkv': _L0_attn_in['W_qkv'], 'L0_attn_W_out': _L0_attn_in['W_out'], 'L0_ffn_ln1_g': _L0_ffn_in['ln1_g'], 'L0_ffn_ln1_b': _L0_ffn_in['ln1_b'], 'L0_ffn_ln2_g': _L0_ffn_in['ln2_g'], 'L0_ffn_ln2_b': _L0_ffn_in['ln2_b'], 'L0_ffn_wq': _L0_ffn_in['wq'], 'L0_ffn_bq': _L0_ffn_in['bq'], 'L0_ffn_wk': _L0_ffn_in['wk'], 'L0_ffn_bk': _L0_ffn_in['bk'], 'L0_ffn_wv': _L0_ffn_in['wv'], 'L0_ffn_bv': _L0_ffn_in['bv'], 'L0_ffn_wo': _L0_ffn_in['wo'], 'L0_ffn_bo': _L0_ffn_in['bo'], 'L0_ffn_gate_w': _L0_ffn_in['gate_w'], 'L0_ffn_gate_b': _L0_ffn_in['gate_b'], 'L0_ffn_w1': _L0_ffn_in['w1'], 'L0_ffn_b1': _L0_ffn_in['b1'], 'L0_ffn_w2': _L0_ffn_in['w2'], 'L0_ffn_b2': _L0_ffn_in['b2']}

def reference(x, L0_tok_W, L0_attn_W_qkv, L0_attn_W_out, L0_ffn_ln1_g, L0_ffn_ln1_b, L0_ffn_ln2_g, L0_ffn_ln2_b, L0_ffn_wq, L0_ffn_bq, L0_ffn_wk, L0_ffn_bk, L0_ffn_wv, L0_ffn_bv, L0_ffn_wo, L0_ffn_bo, L0_ffn_gate_w, L0_ffn_gate_b, L0_ffn_w1, L0_ffn_b1, L0_ffn_w2, L0_ffn_b2):
    import jax
    import jax.numpy as jnp

    def _L0_tok_ref(inputs, W):
        import jax, jax.numpy as jnp
        import numpy as np
        from jax import lax
        PATCH = 16
        B, C, H, Wimg = inputs.shape
        patches = lax.conv_general_dilated_patches(inputs, filter_shape=[PATCH, PATCH], window_strides=[PATCH, PATCH], padding='VALID', dimension_numbers=('NCHW', 'HWIO', 'NCHW'))
        patches = patches.reshape(B, -1, C * PATCH * PATCH)
        return jnp.einsum('bnf,fh->bnh', patches, W)

    def _L0_attn_ref(X, W_qkv, W_out):
        import jax, jax.numpy as jnp
        import numpy as np
        D_MODEL, D_QKV, N_HEADS = (256, 64, 16)
        b, s, _ = X.shape
        h, d = (N_HEADS, D_QKV)
        scale = d ** 0.5
        qkv = X @ W_qkv
        qkv = qkv.reshape(b, s, h, d, 3)
        q, k, v = (qkv[..., 0], qkv[..., 1], qkv[..., 2])
        scores = jnp.einsum('bqhd,bkhd->bhqk', q, k) / scale
        weights = jax.nn.softmax(scores, axis=-1)
        attn = jnp.einsum('bhqk,bkhd->bqhd', weights, v)
        return attn.reshape(b, s, h * d) @ W_out

    def _L0_ffn_ref(x, ln1_g, ln1_b, ln2_g, ln2_b, wq, bq, wk, bk, wv, bv, wo, bo, gate_w, gate_b, w1, b1, w2, b2):
        import jax, jax.numpy as jnp
        import numpy as np
        B, S, H, NH, E, F = (4, 256, 256, 16, 8, 1024)
        D = H // NH
        EPS = 1e-05

        def _layernorm(x, g, b):
            mu = jnp.mean(x, axis=-1, keepdims=True)
            var = jnp.var(x, axis=-1, keepdims=True)
            return (x - mu) * jax.lax.rsqrt(var + EPS) * g + b
        b, s, h = x.shape
        hn = _layernorm(x, ln1_g, ln1_b)
        q = (hn @ wq + bq).reshape(b, s, NH, D).transpose(0, 2, 1, 3)
        k = (hn @ wk + bk).reshape(b, s, NH, D).transpose(0, 2, 1, 3)
        v = (hn @ wv + bv).reshape(b, s, NH, D).transpose(0, 2, 1, 3)
        scores = jnp.einsum('bhqd,bhkd->bhqk', q, k) / jnp.sqrt(jnp.float32(D))
        attn = jax.nn.softmax(scores, axis=-1)
        o = jnp.einsum('bhqk,bhkd->bhqd', attn, v)
        o = o.transpose(0, 2, 1, 3).reshape(b, s, h)
        x = x + (o @ wo + bo)
        hn2 = _layernorm(x, ln2_g, ln2_b).reshape(-1, h)
        logits = hn2 @ gate_w + gate_b
        idx = jnp.argmax(logits, axis=-1)
        mid = jax.nn.relu(jnp.einsum('th,ehf->etf', hn2, w1) + b1[:, None, :])
        y = jnp.einsum('etf,efh->eth', mid, w2) + b2[:, None, :]
        moe = y[idx, jnp.arange(hn2.shape[0])]
        return x + moe.reshape(b, s, h)
    h = _L0_tok_ref(x, L0_tok_W)
    h = h + _L0_attn_ref(_layernorm(h, axis=-1), L0_attn_W_qkv, L0_attn_W_out)
    h = h + _L0_ffn_ref(_layernorm(h, axis=-1), L0_ffn_ln1_g, L0_ffn_ln1_b, L0_ffn_ln2_g, L0_ffn_ln2_b, L0_ffn_wq, L0_ffn_bq, L0_ffn_wk, L0_ffn_bk, L0_ffn_wv, L0_ffn_bv, L0_ffn_wo, L0_ffn_bo, L0_ffn_gate_w, L0_ffn_gate_b, L0_ffn_w1, L0_ffn_b1, L0_ffn_w2, L0_ffn_b2)
    return h

_drawn_inputs = setup_inputs


def setup_inputs(seed=0):
    import zlib

    import numpy as np

    out = dict(_drawn_inputs(seed))
    spreads = {'L0_ffn_ln1_g': (1.0, 0.6),
     'L0_ffn_ln1_b': (0.0, 0.648),
     'L0_ffn_ln2_g': (1.0, 0.2),
     'L0_ffn_ln2_b': (0.0, 0.1),
     'L0_ffn_bq': (0.0, 0.8),
     'L0_ffn_bk': (0.0, 0.8),
     'L0_ffn_bv': (0.0, 0.358),
     'L0_ffn_bo': (0.0, 0.1),
     'L0_ffn_gate_b': (0.0, 0.1),
     'L0_ffn_b1': (0.0, 0.369),
     'L0_ffn_b2': (0.0, 0.1)}
    factors = {'L0_ffn_wq': 8.0, 'L0_ffn_wk': 8.0, 'L0_ffn_wv': 2.992}
    for name, (base, spread) in spreads.items():
        noise = np.random.default_rng([zlib.crc32(name.encode()), seed]).standard_normal(out[name].shape)
        drawn = base * np.exp(spread * noise) if base else spread * noise
        out[name] = jnp.asarray(drawn.astype(out[name].dtype))
    for name, factor in factors.items():
        out[name] = (out[name] * factor).astype(out[name].dtype)
    return out
```

```python
from contextlib import ExitStack

import concourse.bass as bass
from concourse import mybir
from concourse.alu_op_type import AluOpType as ALU

F32 = mybir.dt.float32
I32 = mybir.dt.int32
U32 = mybir.dt.uint32
ACT = mybir.ActivationFunctionType
AX_X = mybir.AxisListType.X

P = 128
IMAGES, CHANNELS, IMG, PATCH = 32, 3, 128, 16
GRID = IMG // PATCH
TOKENS = GRID * GRID
HID = 256
KH = HID // P
FEATURES = CHANNELS * PATCH * PATCH
FT = FEATURES // P
GROUP = 4
GROUPS = IMAGES // GROUP
GT = GROUP * TOKENS
FOLD = FEATURES // TOKENS
BANDS = GROUP * CHANNELS * GRID
TILES = IMAGES * TOKENS // P
HEADS, D1, D2 = 16, 64, 16
PAIRS = HEADS // 2
HD = HEADS * D1
KO = HD // P
EXPERTS, FFN = 8, 1024
KF = FFN // P
SLOT_TILES = TILES + EXPERTS - 1
EPS = 1e-5
COLUMNS = {"ln1_g": 0, "ln1_b": 2, "ln2_g": 4, "ln2_b": 6, "bq": 8, "bk": 10, "bv": 12, "b1": 14}
ROWS = 14 + EXPERTS * KF


class Part:

    def __init__(self, kind, i=None):
        self.kind = kind
        self.i = i
        self.c = {"first": 0, "body": None if i is None else i + 1, "last": None}[kind]
        self.f = {"first": None, "body": i, "last": GROUPS - 1}[kind]
        self.next_images = self.c is not None and not (isinstance(self.c, int) and self.c == GROUPS - 1)


class Ring:

    def __init__(self, nc, ctx, name, uses):
        self.banks = [ctx.enter_context(nc.psum_tensor(f"{name}{b}", [P, 512], F32)) for b in range(2)]
        self.full = [ctx.enter_context(nc.semaphore(f"{name}{b}_full")) for b in range(2)]
        self.emptied = [ctx.enter_context(nc.semaphore(f"{name}{b}_emptied")) for b in range(2)]
        self.uses = {
            "first": [u for u in uses if u[1] == "c"],
            "body": uses,
            "last": [u for u in uses if u[1] == "f"],
        }
        assert all(len(u) % 2 == 0 for u in self.uses.values())

    def _where(self, part, step):
        return [u[0] for u in self.uses[part.kind]].index(step)

    def _count(self, kind, b, n=None):
        mine = self.uses[kind][:n][b::2] if n is not None else self.uses[kind][b::2]
        return len(mine), sum(u[2] for u in mine)

    def _before(self, part, b, which):
        first, body = self._count("first", b)[which], self._count("body", b)[which]
        if part.kind == "first":
            return 0
        if part.kind == "body":
            return first + part.i * body
        return first + (GROUPS - 1) * body

    def _at(self, part, step, which, inclusive):
        n = self._where(part, step)
        return self._before(part, n % 2, which) + self._count(part.kind, n % 2, n + inclusive)[which]

    def bank(self, part, step):
        return self.banks[self._where(part, step) % 2]

    def wait_empty(self, engine, part, step):
        value = self._at(part, step, 1, 0)
        if not (isinstance(value, int) and value == 0):
            engine.wait_ge(self.emptied[self._where(part, step) % 2], value)

    def wait_full(self, engine, part, step):
        engine.wait_ge(self.full[self._where(part, step) % 2], self._at(part, step, 0, 1))

    def wait_read(self, engine, part, step):
        engine.wait_ge(self.emptied[self._where(part, step) % 2], self._at(part, step, 1, 1))

    def wait_read_before(self, engine, part, b):
        engine.wait_ge(self.emptied[b], self._before(part, b, 1))

    def full_of(self, part, step):
        return self.full[self._where(part, step) % 2]

    def emptied_of(self, part, step):
        return self.emptied[self._where(part, step) % 2]


def vit_tower(nc, x, tok_w, qkv_w, out_w, ln1_g, ln1_b, ln2_g, ln2_b, wq, bq, wk, bk, wv, bv, wo, bo,
              gate_w, gate_b, w1, b1, w2, b2, out):
    ctx = ExitStack()
    with ctx:
        def sb(name, shape, dt=F32, where=ctx):
            return where.enter_context(nc.sbuf_tensor(name, shape, dt))

        def sem(name):
            return ctx.enter_context(nc.semaphore(name))

        slot_rows = nc.dram_tensor("slot_rows", [SLOT_TILES * P, HID], F32, kind="Internal").ap()
        slot_outs = nc.dram_tensor("slot_outs", [SLOT_TILES * P, HID], F32, kind="Internal").ap()

        normed_all = sb("normed_all", [P, TILES, HID])
        residual_all = sb("residual_all", [P, TILES, HID])
        logits_all = sb("logits_all", [P, TILES, EXPERTS])
        bo_row = sb("bo_row", [P, HID])
        gate_b_row = sb("gate_b_row", [P, EXPERTS])
        columns = sb("columns", [P, ROWS])
        identity = sb("identity", [P, P])
        earlier = sb("earlier", [P, P])
        ones = sb("ones", [P, P])
        head_mask = sb("head_mask", [P, HEADS // KH])
        minus_half = sb("minus_half", [P, 2])
        eps = sb("eps", [P, 2])
        wait_carrier = sb("wait_carrier", [P, 1])
        iota_expert = sb("iota_expert", [P, EXPERTS])
        iota_tile = sb("iota_tile", [P, SLOT_TILES])
        iota_128 = sb("iota_128", [P, TILES])
        slot_of = sb("slot_of", [P, TILES], U32)
        expert_of = sb("expert_of", [P, SLOT_TILES], I32)
        gathered = normed_all

        def column(name, k, rows=slice(0, P)):
            return columns[rows, COLUMNS[name] + k:COLUMNS[name] + k + 1]

        tower = ExitStack()
        images_here = ExitStack()
        image_rows = sb("image_rows", [BANDS, PATCH, IMG], where=images_here)
        patch_rows = sb("patch_rows", [BANDS, GRID, PATCH, PATCH], where=images_here)
        images_here.close()
        fprobs = sb("fprobs", [P, 2, PAIRS, 2, TOKENS], where=tower)
        fq_heads = sb("fq_heads", [P, 2, KH, HEADS // KH, TOKENS], where=tower)
        features = sb("features", [P, GROUP * FEATURES + 2], where=tower)
        kT = sb("kT", [P, PAIRS, GT], where=tower)
        v_sb = sb("v_sb", [P, 2, HD], where=tower)
        probs = sb("probs", [P, 2, PAIRS, 2, TOKENS], where=tower)
        oT = sb("oT", [P, KO, P], where=tower)
        tok_w_sb = sb("tok_w_sb", [P, FT, HID], where=tower)
        qk_w = sb("qk_w", [P, KH, PAIRS, 2, P], where=tower)
        v_w = sb("v_w", [P, KH, HD], where=tower)
        out_w_sb = sb("out_w_sb", [P, KO, HID], where=tower)
        wq_sb = sb("wq_sb", [P, KH, HID], where=tower)
        wk_sb = sb("wk_sb", [P, KH, HID], where=tower)
        wv_sb = sb("wv_sb", [P, KH, HID], where=tower)
        wo_sb = sb("wo_sb", [P, KH, HID], where=tower)
        gate_w_sb = sb("gate_w_sb", [P, KH, EXPERTS], where=tower)
        h1 = sb("h1", [P, 2, HID], where=tower)
        z = sb("z", [P, 2, HID], where=tower)
        zT = sb("zT", [P, KH, GT], where=tower)
        raw_here = ExitStack()
        qkv_raw = sb("qkv_raw", [P, KH, 3 * HD], where=raw_here)
        raw_here.close()
        q_diag = sb("q_diag", [P, PAIRS, GROUP, P], where=tower)
        probsT = sb("probsT", [P, HEADS, P], where=tower)
        o_sb = sb("o_sb", [P, 2, HD], where=tower)
        vectors_here = ExitStack()
        vector_rows = sb("vector_rows", [ROWS, P], where=vectors_here)
        vectors_here.close()
        h2 = sb("h2", [P, 2, HID], where=tower)
        u = sb("u", [P, 2, HID], where=tower)
        u_bo = sb("u_bo", [P, 2, HID], where=tower)
        z1 = sb("z1", [P, 2, HID], where=tower)
        hnT = sb("hnT", [P, KH, GT], where=tower)
        hn2T = hnT
        fq = sb("fq", [P, KH, GT], where=tower)
        fkT = sb("fkT", [P, KH, GT], where=tower)
        fv = sb("fv", [P, 2, HID], where=tower)
        fprobsT = sb("fprobsT", [P, HEADS, P], where=tower)
        fo = sb("fo", [P, 2, HID], where=tower)
        foT = sb("foT", [P, 2, KH, P], where=tower)
        x2 = sb("x2", [P, 2, HID], where=tower)
        z2 = z1
        small = {}
        for n in ("a", "u", "1", "2"):
            small[n] = (sb(f"stats_{n}", [P, 2, 6], where=tower), sb(f"moments_{n}", [P, 2, 2], where=tower),
                        sb(f"var_eps_{n}", [P, 2], where=tower), sb(f"rstd_{n}", [P, 2], where=tower))
        soft = {}
        for n in ("c", "f"):
            soft[n] = tuple(sb(f"{what}_{n}", [P, GROUP, PAIRS], where=tower) for what in ("max", "sum", "rsum"))
        tower.close()

        experts = ExitStack()
        expert_w = sb("expert_w", [P, EXPERTS, KH * FFN + KF * HID], where=experts)
        b2_rows = sb("b2_rows", [P, EXPERTS * HID], where=experts)
        slot_in = sb("slot_in", [P, HID], where=experts)
        slot_inT = sb("slot_inT", [P, KH, P], where=experts)
        mid = sb("mid", [P, FFN], where=experts)
        midT = sb("midT", [P, KF, P], where=experts)
        b1_now = sb("b1_now", [P, KF], where=experts)
        slot_out = sb("slot_out", [P, HID], where=experts)
        r_max = sb("r_max", [P, TILES], where=experts)
        r_cand = sb("r_cand", [P, TILES, EXPERTS], where=experts)
        r_first = sb("r_first", [P, TILES], where=experts)
        chosen = sb("chosen", [P, EXPERTS, TILES], where=experts)
        r_incl = sb("r_incl", [P, EXPERTS, TILES], where=experts)
        r_excl = sb("r_excl", [P, EXPERTS, TILES], where=experts)
        r_work = sb("r_work", [P, EXPERTS, TILES], where=experts)
        r_count = sb("r_count", [P, EXPERTS], where=experts)
        r_tiles = sb("r_tiles", [P, EXPERTS], where=experts)
        r_end = sb("r_end", [P, EXPERTS], where=experts)
        r_shift = sb("r_shift", [P, EXPERTS], where=experts)
        r_slot = sb("r_slot", [P, TILES], where=experts)
        r_ended = sb("r_ended", [P, SLOT_TILES, EXPERTS - 1], where=experts)
        r_expert = sb("r_expert", [P, SLOT_TILES], where=experts)
        experts.close()

        turn = Ring(nc, ctx, "turn", [
            ("hnT", "f", 1), ("zT0", "c", 1), ("zT1", "c", 1), ("fpT00", "f", 2), ("fpT01", "f", 2), ("fpT10", "f", 2),
            ("fpT11", "f", 2), ("foT0", "f", 1), ("foT1", "f", 1), ("pT00", "c", 2), ("pT01", "c", 2),
            ("z2T", "f", 1), ("pT10", "c", 2), ("pT11", "c", 2), ("oT00", "c", 1), ("oT01", "c", 1),
            ("oT10", "c", 1), ("oT11", "c", 1)])
        proj = Ring(nc, ctx, "proj", [("tok0", "c", 1), ("tok1", "c", 1), ("fqk0", "f", 1), ("fqk1", "f", 1),
                                      ("fv", "f", 1)]
                    + [(f"qk{m}", "c", 1) for m in range(PAIRS)]
                    + [("v00", "c", 1), ("v01", "c", 1), ("wo0", "f", 1), ("wo1", "f", 1), ("v10", "c", 1),
                       ("v11", "c", 1), ("gate", "f", 1), ("out0", "c", 1), ("out1", "c", 1)])
        score = Ring(nc, ctx, "score", [("fs0", "f", 1), ("fs1", "f", 1), ("fs2", "f", 1), ("fs3", "f", 1),
                                        ("s0", "c", 1), ("s1", "c", 1), ("s2", "c", 1), ("s3", "c", 1)])
        mix = Ring(nc, ctx, "mix", [("fo0", "f", 1), ("fo1", "f", 1), ("o00", "c", 1), ("o01", "c", 1),
                                    ("o10", "c", 1), ("o11", "c", 1)])

        consts_made = sem("consts_made")
        vectors_landed = sem("vectors_landed")
        columns_ready = sem("columns_ready")
        columns_turned = sem("columns_turned")
        rows_landed = sem("rows_landed")
        tok_w_landed = sem("tok_w_landed")
        qkv_landed = sem("qkv_landed")
        qkv_sorted = sem("qkv_sorted")
        out_w_landed = sem("out_w_landed")
        small_w_landed = sem("small_w_landed")
        image_landed = sem("image_landed")
        image_used = sem("image_used")
        blocks_zero = sem("blocks_zero")
        fprobsT_zero = sem("fprobsT_zero")
        patch_rows_ready = sem("patch_rows_ready")
        features_landed = sem("features_landed")
        slots_cleared = sem("slots_cleared")
        norm = {n: {s: sem(f"norm_{n}_{s}") for s in ("stats", "moments", "var_eps", "rstd", "out")}
                for n in ("a", "u", "1", "2")}
        u_bo_ready = sem("u_bo_ready")
        fq_heads_ready = sem("fq_heads_ready")
        softmax = {n: {s: sem(f"softmax_{n}_{s}") for s in ("max", "exp", "sum", "rsum", "probs")}
                   for n in ("c", "f")}
        residual_kept = sem("residual_kept")
        normed_kept = sem("normed_kept")
        route = sem("route")
        chosen_ready = sem("chosen_ready")
        ranks_ready = sem("ranks_ready")
        slots_ready = sem("slots_ready")
        scattered = sem("scattered")
        expert_landed = [sem(f"expert_landed{e}") for e in range(EXPERTS)]
        experts_resident = sem("experts_resident")
        slot_in_landed = sem("slot_in_landed")
        slot_inT_full = sem("slot_inT_full")
        slot_inT_ready = sem("slot_inT_ready")
        mid_full = [sem(f"mid_full{n}") for n in range(2)]
        mid_ready = [sem(f"mid_ready{n}") for n in range(2)]
        midT_full = [sem(f"midT_full{n}") for n in range(2)]
        midT_ready = [sem(f"midT_ready{n}") for n in range(2)]
        b1_ready = sem("b1_ready")
        slot_out_full = sem("slot_out_full")
        slot_out_ready = sem("slot_out_ready")
        slot_out_stored = sem("slot_out_stored")
        gather_landed = [sem(f"gather_landed{n}") for n in range(4)]
        sums_ready = sem("sums_ready")
        out_stored = sem("out_stored")

        expert_w1 = expert_w[:, :, 0:KH * FFN].rearrange("p e (k f) -> p e k f", k=KH)
        expert_w2 = expert_w[:, :, KH * FFN:].rearrange("p e (c h) -> p e c h", c=KF)
        by_token = features[:, 1:1 + GROUP * FEATURES].rearrange("p (n a) -> p n a", a=FOLD)

        def of_image(tile, b):
            return tile[:, b // 2, :, b % 2]

        def per_group(per, group, done):
            return group * per + done

        block = ctx.enter_context(nc.Block())

        @block.sync
        def _(sync):
            def load_images(g):
                src = x[bass.ds(g * GROUP, GROUP)].rearrange("b c (i r) w -> (b c i) r w", i=GRID)
                sync.dma_start(image_rows[:], src).then_inc(image_landed, 16)

            def load_features(g):
                sync.wait_ge(patch_rows_ready, g + 1)
                rows = patch_rows[:].rearrange("p j r w -> p j (r w)")
                for n in range(GROUP * CHANNELS):
                    for half in range(2):
                        at = n * PATCH * PATCH + 1 - half
                        sync.dma_start(features[half * TOKENS:(half + 1) * TOKENS, at:at + PATCH * PATCH],
                                       rows[n * GRID:(n + 1) * GRID]).then_inc(features_landed, 16)

            load_images(0)
            sync.dma_start(tok_w_sb[:], tok_w.rearrange("(t p) h -> p t h", p=P)).then_inc(tok_w_landed, 16)
            for k in range(KH):
                sync.dma_start(qkv_raw[:, k, :], qkv_w[k * P:(k + 1) * P, :]).then_inc(qkv_landed, 16)
            load_features(0)
            sync.dma_start(out_w_sb[:], out_w.rearrange("(c p) h -> p c h", p=P)).then_inc(out_w_landed, 16)
            sync.wait_ge(fprobsT_zero, 1)
            sync.dma_start(slot_rows.rearrange("(s p) h -> p s h", p=P),
                           fprobsT[:, 0:HID // P].rearrange("p a b -> p (a b)").unsqueeze(1)
                           .broadcast_to([P, SLOT_TILES, HID])).then_inc(slots_cleared, 16)
            with sync.Fori(1, GROUPS) as g:
                sync.wait_ge(image_used, g)
                load_images(g)
                load_features(g)
            proj.wait_read(sync, Part("last"), "gate")
            sync.wait_ge(normed_kept, TILES)
            for e in range(EXPERTS):
                sync.dma_start(expert_w1[:, e], w1[e].rearrange("(k p) f -> p k f", p=P))\
                    .then_inc(expert_landed[e], 16)
                sync.dma_start(expert_w2[:, e], w2[e].rearrange("(c p) h -> p c h", p=P))\
                    .then_inc(expert_landed[e], 16)
                if e == 0:
                    sync.dma_start(b2_rows[:], b2.rearrange("e h -> (e h)").partition_broadcast(P))\
                        .then_inc(expert_landed[0], 16)
            for e in range(EXPERTS):
                sync.wait_ge(expert_landed[e], 48 if e == 0 else 32)
                sync.sem_inc(experts_resident, 1)
            out_rows = out.rearrange("b t h -> (b t) h").rearrange("(t p) h -> p t h", p=P)
            for n in range(4):
                sync.wait_ge(sums_ready, n + 1)
                sync.dma_start(out_rows[:, 4 * n:4 * n + 4], gathered[:, 4 * n:4 * n + 4]).then_inc(out_stored, 16)
            sync.wait_ge(out_stored, 64)

        @block.gpsimd
        def _(pool):
            pool.memset(identity[:], 0.0)
            pool.memset(earlier[:], 1.0)
            pool.memset(head_mask[:], 1.0)
            pool.memset(minus_half[:], -0.5)
            pool.memset(eps[:], EPS)
            pool.memset(ones[:], 1.0)
            pool.iota(iota_expert[:], pattern=[[1, EXPERTS]], base=0, channel_multiplier=0,
                      allow_small_or_imprecise_dtypes=True)
            pool.iota(iota_tile[:], pattern=[[1, SLOT_TILES]], base=0, channel_multiplier=0,
                      allow_small_or_imprecise_dtypes=True)
            pool.iota(iota_128[:], pattern=[[P, TILES]], base=0, channel_multiplier=0,
                      allow_small_or_imprecise_dtypes=True).then_inc(consts_made, 1)
            pool.wait_ge(consts_made, 1)
            pool.affine_select(out=identity[:], in_=identity[:], compare_op=ALU.not_equal, fill=1.0, base=0,
                               pattern=[[-1, P]], channel_multiplier=1)
            pool.affine_select(out=earlier[:], in_=earlier[:], compare_op=ALU.is_gt, fill=0.0, base=0,
                               pattern=[[1, P]], channel_multiplier=-1)
            pool.affine_select(out=head_mask[:], in_=head_mask[:], compare_op=ALU.is_ge, fill=0.0, base=0,
                               pattern=[[-D2, HEADS // KH]], channel_multiplier=1).then_inc(consts_made, 1)
            pool.wait_ge(consts_made, 2)
            pool.affine_select(out=head_mask[:], in_=head_mask[:], compare_op=ALU.is_ge, fill=0.0, base=D2 - 1,
                               pattern=[[D2, HEADS // KH]], channel_multiplier=-1).then_inc(consts_made, 1)
            pool.memset(fprobsT[:], 0.0).then_inc(fprobsT_zero, 1)

            for name, src in (("ln1_g", ln1_g), ("ln1_b", ln1_b), ("ln2_g", ln2_g), ("ln2_b", ln2_b),
                              ("bq", bq), ("bk", bk), ("bv", bv)):
                pool.dma_start(vector_rows[COLUMNS[name]:COLUMNS[name] + KH],
                               src.rearrange("(k p) -> k p", p=P)).then_inc(vectors_landed, 16)
            pool.dma_start(vector_rows[COLUMNS["b1"]:ROWS], b1.rearrange("e (c p) -> (e c) p", p=P))\
                .then_inc(vectors_landed, 16)
            pool.dma_start(bo_row[:], bo.partition_broadcast(P)).then_inc(rows_landed, 16)
            pool.dma_start(gate_b_row[:], gate_b.partition_broadcast(P)).then_inc(rows_landed, 16)
            for tile, src in ((wq_sb, wq), (wk_sb, wk), (wv_sb, wv), (wo_sb, wo), (gate_w_sb, gate_w)):
                pool.dma_start(tile[:], src.rearrange("(k p) h -> p k h", p=P)).then_inc(small_w_landed, 16)

            pool.wait_ge(qkv_landed, 32)
            by_kind = qkv_raw[:].rearrange("p k (m c s) -> p k s m c", m=PAIRS, s=3)
            pool.tensor_copy(v_w[:, 1].rearrange("p (m c) -> p m c", m=PAIRS), by_kind[:, 1, 2]).then_inc(qkv_sorted, 1)
            pool.wait_ge(qkv_sorted, 3)
            pool.memset(probsT[:], 0.0).then_inc(blocks_zero, 1)

            def root(n, group):
                _, moments, var_eps, rstd = small[n]
                pool.wait_ge(norm[n]["moments"], per_group(2, group, 2))
                pool.tensor_tensor(var_eps[:], moments[:, :, 1], eps[:], ALU.add).then_inc(norm[n]["var_eps"], 1)
                pool.wait_ge(norm[n]["var_eps"], per_group(1, group, 1))
                pool.tensor_tensor(rstd[:], var_eps[:], minus_half[:], ALU.pow).then_inc(norm[n]["rstd"], 1)

            def scale_probs(n, tile, b, group):
                pool.wait_ge(softmax[n]["rsum"], per_group(GROUP, group, b + 1))
                rows = of_image(tile, b)
                pool.tensor_tensor(rows, rows, soft[n][2][:, b].unsqueeze(2).broadcast_to([P, PAIRS, TOKENS]),
                                   ALU.mult).then_inc(softmax[n]["probs"], 1)

            def bo_to_u(part):
                pool.wait_ge(norm["u"]["out"], per_group(2, part.f, 2))
                for j in range(2):
                    pool.tensor_tensor(u_bo[:, j], u[:, j], bo_row[:], ALU.add).then_inc(u_bo_ready, 1)

            def queries_by_head(part):
                for m in range(KH):
                    proj.wait_read(pool, part, f"fqk{m}")
                for b in range(GROUP):
                    if b >= 2:
                        score.wait_full(pool, part, f"fs{b - 2}")
                    for m in range(KH):
                        pool.tensor_tensor(
                            fq_heads[:, b % 2, m],
                            fq[:, m, b * TOKENS:(b + 1) * TOKENS].unsqueeze(1).broadcast_to([P, HEADS // KH, TOKENS]),
                            head_mask[:].unsqueeze(2).broadcast_to([P, HEADS // KH, TOKENS]),
                            ALU.mult).then_inc(fq_heads_ready, 1)

            def keep_residual(part):
                for j in range(2):
                    proj.wait_read(pool, part, f"wo{j}")
                    pool.tensor_tensor(residual_all[:, bass.ds(part.f * 2 + j, 1)], h2[:, j:j + 1], x2[:, j:j + 1],
                                       ALU.add)\
                        .then_inc(residual_kept, 1)

            def keep_normed(part):
                for j in range(2):
                    pool.wait_ge(norm["2"]["out"], per_group(2, part.f, j + 1))
                    pool.tensor_copy(normed_all[:, bass.ds(part.f * 2 + j, 1)], z2[:, j:j + 1]).then_inc(normed_kept, 1)

            def work(part):
                c, f = part.c, part.f
                if f is not None:
                    root("u", f)
                    bo_to_u(part)
                    root("1", f)
                if c is not None:
                    root("a", c)
                if f is not None:
                    queries_by_head(part)
                    for b in range(GROUP):
                        scale_probs("f", fprobs, b, f)
                if c is not None:
                    scale_probs("c", probs, 0, c)
                    scale_probs("c", probs, 1, c)
                if f is not None:
                    keep_residual(part)
                    root("2", f)
                if c is not None:
                    scale_probs("c", probs, 2, c)
                    scale_probs("c", probs, 3, c)
                if f is not None:
                    keep_normed(part)

            pool.wait_ge(rows_landed, 32)
            work(Part("first"))
            with pool.Fori(0, GROUPS - 2) as i:
                work(Part("body", i))
            work(Part("body", GROUPS - 2))
            work(Part("last"))

            pool.wait_ge(slots_cleared, 16)
            pool.wait_ge(slots_ready, 1)
            pool.wait_ge(normed_kept, TILES)
            for t in range(TILES):
                pool.indirect_dma_start(out=slot_rows, out_offset=bass.IndirectOffsetOnAxis(ap=slot_of[:, t:t + 1], axis=0),
                                        in_=normed_all[:, t], in_offset=None).then_inc(scattered, 16)
            pool.wait_ge(scattered, 16 * TILES)

            def load_slot_tile(s):
                pool.dma_start(slot_in[:], slot_rows[bass.ds(s * P, P), :]).then_inc(slot_in_landed, 16)

            def store_slot_tile(s):
                pool.wait_ge(slot_out_ready, s + 1)
                pool.dma_start(slot_outs[bass.ds(s * P, P), :], slot_out[:]).then_inc(slot_out_stored, 16)

            load_slot_tile(0)
            with pool.Fori(0, SLOT_TILES - 1) as s:
                pool.wait_ge(slot_inT_full, s + 1)
                load_slot_tile(s + 1)
                store_slot_tile(s)
            store_slot_tile(SLOT_TILES - 1)

            pool.wait_ge(slot_out_stored, 16 * SLOT_TILES)
            for t in range(TILES):
                pool.indirect_dma_start(out=gathered[:, t], out_offset=None, in_=slot_outs,
                                        in_offset=bass.IndirectOffsetOnAxis(ap=slot_of[:, t:t + 1], axis=0))\
                    .then_inc(gather_landed[t // 4], 16)

        @block.vector
        def _(dve):
            def stats(n, tile, j):
                dve.bn_stats(small[n][0][:, j], tile[:, j]).then_inc(norm[n]["stats"], 1)

            def moments(n, group):
                dve.wait_ge(norm[n]["stats"], per_group(2, group, 2))
                dve.memset(wait_carrier[:], 0.0)
                for j in range(2):
                    dve.bn_aggr(small[n][1][:, j], small[n][0][:, j]).then_inc(norm[n]["moments"], 1)

            def normed(n, dst, src, group):
                dve.wait_ge(norm[n]["rstd"], per_group(1, group, 1))
                for j in range(2):
                    dve.tensor_scalar(dst[:, j], src[:, j], small[n][1][:, j, 0:1], small[n][3][:, j:j + 1],
                                      ALU.subtract, ALU.mult).then_inc(norm[n]["out"], 1)

            def minus_max(n, tile, b, part, step, group):
                score.wait_full(dve, part, step)
                scores = score.bank(part, step)[:].rearrange("p (h t) -> p h t", h=PAIRS)
                dve.tensor_reduce(soft[n][0][:, b], scores, AX_X, ALU.max).then_inc(softmax[n]["max"], 1)
                dve.wait_ge(softmax[n]["max"], per_group(GROUP, group, b + 1))
                dve.tensor_tensor(of_image(tile, b), scores,
                                  soft[n][0][:, b].unsqueeze(2).broadcast_to([P, PAIRS, TOKENS]), ALU.subtract)\
                    .then_inc(score.emptied_of(part, step), 1)

            def row_sums(n, tile, b, group):
                dve.wait_ge(softmax[n]["exp"], per_group(GROUP, group, b + 1))
                dve.tensor_reduce(soft[n][1][:, b], of_image(tile, b), AX_X, ALU.add)\
                    .then_inc(softmax[n]["sum"], 1)
                dve.wait_ge(softmax[n]["sum"], per_group(GROUP, group, b + 1))
                dve.reciprocal(soft[n][2][:, b], soft[n][1][:, b]).then_inc(softmax[n]["rsum"], 1)

            def from_ring(ring, part, step, dst, src):
                ring.wait_full(dve, part, step)
                dve.tensor_copy(dst, src(ring.bank(part, step))).then_inc(ring.emptied_of(part, step), 1)

            def odd_image_blocks(part, steps, dst):
                for g, step in enumerate(steps):
                    turn.wait_full(dve, part, step)
                    src = turn.bank(part, step)[TOKENS:P].rearrange("p (h t) -> p h t", h=8)
                    dve.tensor_copy(dst[TOKENS:P, 8 * g:8 * g + 8, TOKENS:P], src)\
                        .then_inc(turn.emptied_of(part, step), 1)

            def by_patch(g):
                dve.wait_ge(image_landed, 16 * (g + 1))
                dve.tensor_copy(patch_rows[:], image_rows[:].rearrange("p r (j w) -> p j r w", j=GRID))\
                    .then_inc(patch_rows_ready, 1)

            def qk_out(part, m):
                step = f"qk{m}"
                proj.wait_full(dve, part, step)
                bank = proj.bank(part, step)
                for half in range(2):
                    rows = slice(half * D1, (half + 1) * D1)
                    dve.tensor_copy(q_diag[rows, m, :, rows], bank[rows, 0:GT].rearrange("p (b t) -> p b t", b=GROUP))
                dve.tensor_copy(kT[:, m], bank[:, GT:2 * GT]).then_inc(proj.emptied_of(part, step), 1)

            def work(part):
                c, f = part.c, part.f
                if f is not None:
                    for b in range(2):
                        proj.wait_read_before(dve, part, b)
                    for j in range(2):
                        stats("u", h2, j)
                    moments("u", f)
                    normed("u", u, h2, f)
                    dve.wait_ge(norm["u"]["out"], per_group(2, f, 2))
                    for j in range(2):
                        stats("1", u, j)
                    moments("1", f)
                    normed("1", z1, u, f)
                if c is not None:
                    from_ring(proj, part, "tok1", h1[:, 1], lambda bank: bank[:, 0:HID])
                    proj.wait_read(dve, part, "tok0")
                    stats("a", h1, 0)
                    proj.wait_read(dve, part, "tok1")
                    stats("a", h1, 1)
                    moments("a", c)
                if f is not None:
                    proj.wait_full(dve, part, "fqk1")
                    bank = proj.bank(part, "fqk1")
                    dve.tensor_scalar(fq[:, 1], bank[:, 0:GT], column("bq", 1), None, ALU.add)
                    dve.tensor_scalar(fkT[:, 1], bank[:, GT:2 * GT], column("bk", 1), None, ALU.add)\
                        .then_inc(proj.emptied_of(part, "fqk1"), 1)
                if c is not None:
                    normed("a", z, h1, c)
                    from_ring(turn, part, "zT1", zT[:, :, P:], lambda bank: bank[:, 0:HID].rearrange("p (k t) -> p k t", k=KH))
                if f is not None:
                    minus_max("f", fprobs, 0, part, "fs0", f)
                    minus_max("f", fprobs, 1, part, "fs1", f)
                if c is not None:
                    qk_out(part, 1)
                if f is not None:
                    row_sums("f", fprobs, 0, f)
                    row_sums("f", fprobs, 1, f)
                if c is not None:
                    qk_out(part, 3)
                if f is not None:
                    odd_image_blocks(part, ("fpT00", "fpT01"), fprobsT)
                    minus_max("f", fprobs, 2, part, "fs2", f)
                    minus_max("f", fprobs, 3, part, "fs3", f)
                if c is not None:
                    qk_out(part, 5)
                if f is not None:
                    row_sums("f", fprobs, 2, f)
                    row_sums("f", fprobs, 3, f)
                if c is not None:
                    qk_out(part, 7)
                if f is not None:
                    odd_image_blocks(part, ("fpT10", "fpT11"), fprobsT)
                    from_ring(mix, part, "fo1", fo[:, 1], lambda bank: bank[:, 0:HID])
                if c is not None:
                    minus_max("c", probs, 0, part, "s0", c)
                    minus_max("c", probs, 1, part, "s1", c)
                    from_ring(proj, part, "v01", v_sb[:, 0, 512:], lambda bank: bank[:])
                if f is not None:
                    turn.wait_full(dve, part, "foT1")
                    bank = turn.bank(part, "foT1")
                    for k in range(KH):
                        ins = dve.tensor_scalar(foT[:, 1, k], bank[:, k * P:(k + 1) * P], column("bv", k), None, ALU.add)
                    ins.then_inc(turn.emptied_of(part, "foT1"), 1)
                if c is not None:
                    row_sums("c", probs, 0, c)
                    row_sums("c", probs, 1, c)
                    minus_max("c", probs, 2, part, "s2", c)
                    minus_max("c", probs, 3, part, "s3", c)
                if f is not None:
                    for j in range(2):
                        dve.wait_ge(u_bo_ready, per_group(2, f, j + 1))
                        proj.wait_full(dve, part, f"wo{j}")
                        dve.tensor_tensor(x2[:, j], proj.bank(part, f"wo{j}")[:, 0:HID], u_bo[:, j], ALU.add)\
                            .then_inc(proj.emptied_of(part, f"wo{j}"), 1)
                    for j in range(2):
                        proj.wait_read(dve, part, f"wo{j}")
                        stats("2", x2, j)
                    moments("2", f)
                if c is not None:
                    from_ring(proj, part, "v11", v_sb[:, 1, 512:], lambda bank: bank[:])
                    row_sums("c", probs, 2, c)
                    row_sums("c", probs, 3, c)
                if part.next_images:
                    by_patch(c + 1)
                if f is not None:
                    normed("2", z2, x2, f)
                if c is not None:
                    odd_image_blocks(part, ("pT00", "pT01"), probsT)
                    from_ring(mix, part, "o01", o_sb[:, 0, 512:], lambda bank: bank[:])
                    odd_image_blocks(part, ("pT10", "pT11"), probsT)
                if f is not None:
                    proj.wait_full(dve, part, "gate")
                    logits = proj.bank(part, "gate")[:, 0:2 * EXPERTS].rearrange("p (j e) -> p j e", j=2)
                    dve.tensor_tensor(logits_all[:, bass.ds(f * 2, 2)], logits,
                                      gate_b_row[:].unsqueeze(1).broadcast_to([P, 2, EXPERTS]), ALU.add)\
                        .then_inc(proj.emptied_of(part, "gate"), 1)
                if c is not None:
                    from_ring(mix, part, "o11", o_sb[:, 1, 512:], lambda bank: bank[:])
                    for j in range(2):
                        from_ring(turn, part, f"oT{j}1", oT[:, KO // 2:],
                                  lambda bank: bank[:].rearrange("p (a t) -> p a t", t=P))
                        proj.wait_full(dve, part, f"out{j}")
                        dve.tensor_tensor(h2[:, j], proj.bank(part, f"out{j}")[:, 0:HID], h1[:, j], ALU.add)\
                            .then_inc(proj.emptied_of(part, f"out{j}"), 1)

            by_patch(0)
            dve.wait_ge(columns_turned, 1)
            dve.tensor_copy(columns[:], turn.banks[0][:, 0:ROWS]).then_inc(columns_ready, 1)
            dve.wait_ge(qkv_landed, 32)
            by_kind = qkv_raw[:].rearrange("p k (m c s) -> p k s m c", m=PAIRS, s=3)
            for s in range(2):
                dve.tensor_copy(qk_w[:, 0, :, s], by_kind[:, 0, s])
            dve.tensor_copy(v_w[:, 0].rearrange("p (m c) -> p m c", m=PAIRS), by_kind[:, 0, 2]).then_inc(qkv_sorted, 1)
            dve.wait_ge(qkv_sorted, 3)
            dve.memset(q_diag[:], 0.0).then_inc(blocks_zero, 1)
            dve.wait_ge(blocks_zero, 2)
            dve.wait_ge(columns_ready, 1)
            dve.wait_ge(rows_landed, 32)
            work(Part("first"))
            dve.wait_ge(slots_cleared, 16)
            with dve.Fori(0, GROUPS - 2) as i:
                work(Part("body", i))
            work(Part("body", GROUPS - 2))
            work(Part("last"))

            steps = [0]

            def then(ins):
                steps[0] += 1
                ins.then_inc(route, 1)
                dve.wait_ge(route, steps[0])

            last = Part("last")
            proj.wait_read(dve, last, "gate")
            dve.wait_ge(normed_kept, TILES)
            by_tile = [P, TILES, EXPERTS]
            ranks_of = iota_expert[:].unsqueeze(1).broadcast_to(by_tile)
            then(dve.tensor_reduce(r_max[:], logits_all[:], AX_X, ALU.max))
            then(dve.tensor_tensor(r_cand[:], logits_all[:], r_max[:].unsqueeze(2).broadcast_to(by_tile), ALU.is_lt))
            then(dve.scalar_tensor_tensor(r_cand[:], r_cand[:], float(EXPERTS), ranks_of, ALU.mult, ALU.add))
            then(dve.tensor_reduce(r_first[:], r_cand[:], AX_X, ALU.min))
            dve.tensor_tensor(chosen[:].rearrange("p e t -> p t e"), r_first[:].unsqueeze(2).broadcast_to(by_tile),
                              ranks_of, ALU.is_equal).then_inc(chosen_ready, 1)
            dve.wait_ge(ranks_ready, 2)
            ranks = score.banks[0][:, 0:EXPERTS * TILES].rearrange("p (e t) -> p e t", e=EXPERTS)
            totals = score.banks[1][:, 0:EXPERTS * TILES]
            totals_3d = totals.rearrange("p (e t) -> p e t", e=EXPERTS)
            flat = lambda tile: tile[:].rearrange("p e t -> p (e t)")
            then(dve.tensor_tensor_scan(flat(r_incl), ones[:], totals, 0.0, ALU.mult, ALU.add))
            then(dve.tensor_tensor(r_excl[:], r_incl[:], totals_3d, ALU.subtract))
            then(dve.tensor_reduce(r_count[:], totals_3d, AX_X, ALU.add))
            by_expert = [P, EXPERTS, TILES]
            then(dve.tensor_tensor(r_work[:], r_count[:].unsqueeze(2).broadcast_to(by_expert),
                                   iota_128[:].unsqueeze(1).broadcast_to(by_expert), ALU.is_gt))
            then(dve.tensor_reduce(r_tiles[:], r_work[:], AX_X, ALU.add))
            then(dve.tensor_tensor_scan(r_end[:], ones[:, 0:EXPERTS], r_tiles[:], 0.0, ALU.mult, ALU.add))
            then(dve.tensor_tensor(r_shift[:], r_end[:], r_tiles[:], ALU.subtract))
            then(dve.scalar_tensor_tensor(r_shift[:], r_shift[:], float(P), r_excl[:, :, 0], ALU.mult, ALU.subtract))
            then(dve.tensor_tensor(r_work[:], ranks, r_excl[:], ALU.add))
            then(dve.tensor_tensor(r_work[:], r_work[:], r_shift[:].unsqueeze(2).broadcast_to(by_expert), ALU.add))
            then(dve.tensor_tensor(r_work[:], r_work[:], chosen[:], ALU.mult))
            then(dve.tensor_reduce(r_slot[:], r_work[:].rearrange("p e t -> p t e"), AX_X, ALU.add))
            dve.tensor_copy(slot_of[:], r_slot[:]).then_inc(slots_ready, 1)
            by_slot = [P, SLOT_TILES, EXPERTS - 1]
            then(dve.tensor_tensor(r_ended[:], iota_tile[:].unsqueeze(2).broadcast_to(by_slot),
                                   r_end[:, 0:EXPERTS - 1].unsqueeze(1).broadcast_to(by_slot), ALU.is_ge))
            then(dve.tensor_reduce(r_expert[:], r_ended[:], AX_X, ALU.add))
            dve.tensor_copy(expert_of[:], r_expert[:]).then_inc(slots_ready, 1)
            dve.wait_ge(slots_ready, 2)
            dve.wait_ge(experts_resident, 1)

            def expert(s):
                return dve.value_load(expert_of[0:1, bass.ds(s, 1)], min_val=0, max_val=EXPERTS - 1)

            def rows_in(s):
                turn_bank = turn.banks[0]
                dve.wait_ge(slot_inT_full, s + 1)
                for k in range(KH):
                    ins = dve.tensor_scalar(slot_inT[:, k], turn_bank[:, k * P:(k + 1) * P], column("ln2_g", k),
                                            column("ln2_b", k), ALU.mult, ALU.add)
                ins.then_inc(slot_inT_ready, 1)

            def mid_half(s):
                dve.wait_ge(mid_full[1], s + 1)
                dve.tensor_copy(mid[:, 512:], proj.banks[1][:]).then_inc(mid_ready[1], 1)

            def biases(s):
                dve.tensor_copy(b1_now[:], columns[:, bass.ds(expert(s) * KF + COLUMNS["b1"], KF)]).then_inc(b1_ready, 1)

            def midT_half(s):
                dve.wait_ge(midT_full[1], s + 1)
                dve.wait_ge(b1_ready, s + 1)
                for n in range(KF // 2):
                    c = KF // 2 + n
                    ins = dve.tensor_scalar(midT[:, c], score.banks[1][:, n * P:(n + 1) * P], b1_now[:, c:c + 1], 0.0,
                                            ALU.add, ALU.max)
                ins.then_inc(midT_ready[1], 1)

            def rows_out(s, first=False):
                dve.wait_ge(slot_out_full, s + 1)
                if not first:
                    dve.wait_ge(slot_out_stored, s * 16)
                e = expert(s)
                dve.tensor_tensor(slot_out[:], mix.banks[0][:, 0:HID], b2_rows[:, bass.ds(e * HID, HID)], ALU.add)\
                    .then_inc(slot_out_ready, 1)

            rows_in(0)
            biases(0)
            mid_half(0)
            rows_in(1)
            midT_half(0)
            dve.wait_ge(midT_ready[0], 1)
            dve.wait_ge(midT_ready[1], 1)
            biases(1)
            mid_half(1)
            rows_out(0, True)
            with dve.Fori(1, SLOT_TILES - 1) as s:
                rows_in(s + 1)
                midT_half(s)
                dve.wait_ge(midT_ready[0], s + 1)
                dve.wait_ge(midT_ready[1], s + 1)
                biases(s + 1)
                mid_half(s + 1)
                rows_out(s)
            midT_half(SLOT_TILES - 1)
            rows_out(SLOT_TILES - 1)
            for n in range(4):
                dve.wait_ge(gather_landed[n], 64)
                part_of = gathered[:, 4 * n:4 * n + 4]
                dve.tensor_tensor(part_of, part_of, residual_all[:, 4 * n:4 * n + 4], ALU.add).then_inc(sums_ready, 1)

        @block.scalar
        def _(act):
            def from_ring(ring, part, step, dst, src):
                ring.wait_full(act, part, step)
                act.activation(dst, src(ring.bank(part, step)), ACT.Copy).then_inc(ring.emptied_of(part, step), 1)

            def exps(n, tile, b, part, step, scale):
                score.wait_read(act, part, step)
                act.activation(of_image(tile, b), of_image(tile, b), ACT.Exp, scale=scale).then_inc(softmax[n]["exp"], 1)

            def even_image_blocks(part, steps, dst):
                for g, step in enumerate(steps):
                    turn.wait_full(act, part, step)
                    src = turn.bank(part, step)[0:TOKENS].rearrange("p (h t) -> p h t", h=8)
                    act.activation(dst[0:TOKENS, 8 * g:8 * g + 8, 0:TOKENS], src, ACT.Copy)\
                        .then_inc(turn.emptied_of(part, step), 1)

            def qk_out(part, m):
                step = f"qk{m}"
                proj.wait_full(act, part, step)
                bank = proj.bank(part, step)
                for half in range(2):
                    rows = slice(half * D1, (half + 1) * D1)
                    act.activation(q_diag[rows, m, :, rows],
                                   bank[rows, 0:GT].rearrange("p (b t) -> p b t", b=GROUP), ACT.Copy)
                act.activation(kT[:, m], bank[:, GT:2 * GT], ACT.Copy).then_inc(proj.emptied_of(part, step), 1)

            def work(part):
                c, f = part.c, part.f
                if c is not None:
                    from_ring(proj, part, "tok0", h1[:, 0], lambda bank: bank[:, 0:HID])
                if f is not None:
                    turn.wait_full(act, part, "hnT")
                    for k in range(KH):
                        ins = act.activation(hnT[:, k], turn.bank(part, "hnT")[:, k * GT:(k + 1) * GT], ACT.Identity,
                                             scale=column("ln1_g", k), bias=column("ln1_b", k))
                    ins.then_inc(turn.emptied_of(part, "hnT"), 1)
                    proj.wait_full(act, part, "fqk0")
                    bank = proj.bank(part, "fqk0")
                    act.activation(fq[:, 0], bank[:, 0:GT], ACT.Identity, bias=column("bq", 0))
                    act.activation(fkT[:, 0], bank[:, GT:2 * GT], ACT.Identity, bias=column("bk", 0))\
                        .then_inc(proj.emptied_of(part, "fqk0"), 1)
                    from_ring(proj, part, "fv", fv[:].rearrange("p j h -> p (j h)"), lambda bank: bank[:])
                if c is not None:
                    from_ring(turn, part, "zT0", zT[:, :, 0:P], lambda bank: bank[:, 0:HID].rearrange("p (k t) -> p k t", k=KH))
                    qk_out(part, 0)
                if f is not None:
                    exps("f", fprobs, 0, part, "fs0", D2 ** -0.5)
                    exps("f", fprobs, 1, part, "fs1", D2 ** -0.5)
                if c is not None:
                    qk_out(part, 2)
                if f is not None:
                    even_image_blocks(part, ("fpT00", "fpT01"), fprobsT)
                if c is not None:
                    qk_out(part, 4)
                if f is not None:
                    exps("f", fprobs, 2, part, "fs2", D2 ** -0.5)
                    exps("f", fprobs, 3, part, "fs3", D2 ** -0.5)
                    from_ring(mix, part, "fo0", fo[:, 0], lambda bank: bank[:, 0:HID])
                if c is not None:
                    qk_out(part, 6)
                if f is not None:
                    even_image_blocks(part, ("fpT10", "fpT11"), fprobsT)
                if c is not None:
                    exps("c", probs, 0, part, "s0", D1 ** -0.5)
                    exps("c", probs, 1, part, "s1", D1 ** -0.5)
                    from_ring(proj, part, "v00", v_sb[:, 0, 0:512], lambda bank: bank[:])
                if f is not None:
                    turn.wait_full(act, part, "foT0")
                    bank = turn.bank(part, "foT0")
                    for k in range(KH):
                        ins = act.activation(foT[:, 0, k], bank[:, k * P:(k + 1) * P], ACT.Identity, bias=column("bv", k))
                    ins.then_inc(turn.emptied_of(part, "foT0"), 1)
                if c is not None:
                    exps("c", probs, 2, part, "s2", D1 ** -0.5)
                    exps("c", probs, 3, part, "s3", D1 ** -0.5)
                    from_ring(proj, part, "v10", v_sb[:, 1, 0:512], lambda bank: bank[:])
                    even_image_blocks(part, ("pT00", "pT01"), probsT)
                    from_ring(mix, part, "o00", o_sb[:, 0, 0:512], lambda bank: bank[:])
                if f is not None:
                    turn.wait_full(act, part, "z2T")
                    for k in range(KH):
                        ins = act.activation(hn2T[:, k], turn.bank(part, "z2T")[:, k * GT:(k + 1) * GT], ACT.Identity,
                                             scale=column("ln2_g", k), bias=column("ln2_b", k))
                    ins.then_inc(turn.emptied_of(part, "z2T"), 1)
                if c is not None:
                    even_image_blocks(part, ("pT10", "pT11"), probsT)
                    from_ring(mix, part, "o10", o_sb[:, 1, 0:512], lambda bank: bank[:])
                    for j in range(2):
                        from_ring(turn, part, f"oT{j}0", oT[:, 0:KO // 2],
                                  lambda bank: bank[:].rearrange("p (a t) -> p a t", t=P))

            act.wait_ge(qkv_landed, 32)
            by_kind = qkv_raw[:].rearrange("p k (m c s) -> p k s m c", m=PAIRS, s=3)
            act.activation(qk_w[:, 1, :, 0], by_kind[:, 1, 0], ACT.Copy)
            act.activation(qk_w[:, 1, :, 1], by_kind[:, 1, 1], ACT.Copy).then_inc(qkv_sorted, 1)
            act.wait_ge(columns_ready, 1)
            act.wait_ge(blocks_zero, 2)
            work(Part("first"))
            act.wait_ge(slots_cleared, 16)
            with act.Fori(0, GROUPS - 2) as i:
                work(Part("body", i))
            work(Part("body", GROUPS - 2))
            work(Part("last"))

            def mid_half(s):
                act.wait_ge(mid_full[0], s + 1)
                act.activation(mid[:, 0:512], proj.banks[0][:], ACT.Copy).then_inc(mid_ready[0], 1)

            def midT_half(s):
                act.wait_ge(midT_full[0], s + 1)
                act.wait_ge(b1_ready, s + 1)
                for c in range(KF // 2):
                    ins = act.activation(midT[:, c], score.banks[0][:, c * P:(c + 1) * P], ACT.Relu, bias=b1_now[:, c:c + 1])
                ins.then_inc(midT_ready[0], 1)

            mid_half(0)
            with act.Fori(0, SLOT_TILES - 1) as s:
                midT_half(s)
                mid_half(s + 1)
            midT_half(SLOT_TILES - 1)

        @block.tensor
        def _(pe):
            def group_of(out_ap, pairs):
                for n, (lhsT, rhs) in enumerate(pairs):
                    ins = pe.matmul(out_ap, lhsT, rhs, start=(n == 0), stop=(n == len(pairs) - 1))
                return ins

            def tokens(part):
                pe.wait_ge(features_landed, per_group(16 * GROUP * CHANNELS * 2, part.c, 16 * GROUP * CHANNELS * 2))
                for j in range(2):
                    proj.wait_empty(pe, part, f"tok{j}")
                    group_of(proj.bank(part, f"tok{j}")[:, 0:HID],
                             [(by_token[:, j * P:(j + 1) * P, 2 * t], tok_w_sb[:, t]) for t in range(FT)])\
                        .then_inc(proj.full_of(part, f"tok{j}"), 1)

            def turn_rows(part, step, rows, ready, count):
                turn.wait_empty(pe, part, step)
                for j in range(2):
                    pe.wait_ge(ready, per_group(2, count, j + 1))
                    for k in range(KH):
                        ins = pe.transpose(turn.bank(part, step)[:, k * GT + j * P:k * GT + (j + 1) * P],
                                           rows[:, j, k * P:(k + 1) * P], identity[:])
                ins.then_inc(turn.full_of(part, step), 1)

            def turn_z(part):
                for j in range(2):
                    pe.wait_ge(norm["a"]["out"], per_group(2, part.c, j + 1))
                    turn.wait_empty(pe, part, f"zT{j}")
                    for k in range(KH):
                        ins = pe.transpose(turn.bank(part, f"zT{j}")[:, k * P:(k + 1) * P], z[:, j, k * P:(k + 1) * P],
                                           identity[:])
                    ins.then_inc(turn.full_of(part, f"zT{j}"), 1)

            def qk(part, m):
                step = f"qk{m}"
                if m == 0:
                    for j in range(2):
                        turn.wait_read(pe, part, f"zT{j}")
                proj.wait_empty(pe, part, step)
                for s in range(2):
                    ins = group_of(proj.bank(part, step)[:, s * GT:(s + 1) * GT],
                                   [(qk_w[:, k, m, s], zT[:, k]) for k in range(KH)])
                ins.then_inc(proj.full_of(part, step), 1)

            def values(part, j):
                for half in range(2):
                    step = f"v{j}{half}"
                    proj.wait_empty(pe, part, step)
                    for k in range(KH):
                        ins = pe.matmul(proj.bank(part, step)[:], zT[:, k, j * P:(j + 1) * P],
                                        v_w[:, k, half * 512:(half + 1) * 512], start=(k == 0), stop=(k == KH - 1))
                        if (j, half, k) == (0, 0, 0):
                            ins.then_inc(image_used, 1)
                    ins.then_inc(proj.full_of(part, step), 1)

            def scores(part, b):
                if b == 0:
                    proj.wait_read(pe, part, "qk6")
                    proj.wait_read(pe, part, "qk7")
                step = f"s{b}"
                score.wait_empty(pe, part, step)
                for m in range(PAIRS):
                    ins = pe.matmul(score.bank(part, step)[:, m * TOKENS:(m + 1) * TOKENS], q_diag[:, m, b],
                                    kT[:, m, b * TOKENS:(b + 1) * TOKENS], start=True, stop=True)
                ins.then_inc(score.full_of(part, step), 1)

            def fscores(part, b):
                pe.wait_ge(fq_heads_ready, per_group(GROUP * KH, part.f, KH * (b + 1)))
                step = f"fs{b}"
                score.wait_empty(pe, part, step)
                for m in range(KH):
                    for g in range(PAIRS // KH):
                        at = (m * PAIRS // KH + g) * TOKENS
                        ins = pe.matmul(score.bank(part, step)[:, at:at + TOKENS],
                                        fq_heads[:, b % 2, m, 2 * g:2 * g + 2].rearrange("p h t -> p (h t)"),
                                        fkT[:, m, b * TOKENS:(b + 1) * TOKENS], start=True, stop=True)
                ins.then_inc(score.full_of(part, step), 1)

            def turn_probs(part, n, tile, j, group):
                pe.wait_ge(softmax[n]["probs"], per_group(GROUP, group, 2 * j + 2))
                for g in range(2):
                    step = f"{'f' if n == 'f' else ''}pT{j}{g}"
                    turn.wait_empty(pe, part, step)
                    for q in range(4):
                        m = 4 * g + q
                        ins = pe.transpose(turn.bank(part, step)[:, q * P:(q + 1) * P],
                                           tile[:, j, m].rearrange("p b t -> p (b t)"), identity[:])
                    ins.then_inc(turn.full_of(part, step), 1)

            def mix_values(part, j):
                for g in range(2):
                    turn.wait_read(pe, part, f"pT{j}{g}")
                    proj.wait_read(pe, part, f"v{j}{g}")
                for g in range(2):
                    step = f"o{j}{g}"
                    mix.wait_empty(pe, part, step)
                    for n in range(8):
                        h = 8 * g + n
                        ins = pe.matmul(mix.bank(part, step)[:, n * D1:(n + 1) * D1], probsT[:, h],
                                        v_sb[:, j, h * D1:(h + 1) * D1], start=True, stop=True)
                    ins.then_inc(mix.full_of(part, step), 1)

            def fmix_values(part, j):
                for g in range(2):
                    turn.wait_read(pe, part, f"fpT{j}{g}")
                proj.wait_read(pe, part, "fv")
                step = f"fo{j}"
                mix.wait_empty(pe, part, step)
                for h in range(HEADS):
                    ins = pe.matmul(mix.bank(part, step)[:, h * D2:(h + 1) * D2], fprobsT[:, h],
                                    fv[:, j, h * D2:(h + 1) * D2], start=True, stop=True)
                ins.then_inc(mix.full_of(part, step), 1)

            def turn_fo(part, j):
                mix.wait_read(pe, part, f"fo{j}")
                turn.wait_empty(pe, part, f"foT{j}")
                for k in range(KH):
                    ins = pe.transpose(turn.bank(part, f"foT{j}")[:, k * P:(k + 1) * P], fo[:, j, k * P:(k + 1) * P],
                                       identity[:])
                ins.then_inc(turn.full_of(part, f"foT{j}"), 1)

            def fout(part, j):
                turn.wait_read(pe, part, f"foT{j}")
                proj.wait_empty(pe, part, f"wo{j}")
                group_of(proj.bank(part, f"wo{j}")[:, 0:HID], [(foT[:, j, k], wo_sb[:, k]) for k in range(KH)])\
                    .then_inc(proj.full_of(part, f"wo{j}"), 1)

            def out_proj(part, j):
                for g in range(2):
                    mix.wait_read(pe, part, f"o{j}{g}")
                    turn.wait_empty(pe, part, f"oT{j}{g}")
                    for q in range(KO // 2):
                        at = (g * KO // 2 + q) * P
                        ins = pe.transpose(turn.bank(part, f"oT{j}{g}")[:, q * P:(q + 1) * P], o_sb[:, j, at:at + P],
                                           identity[:])
                    ins.then_inc(turn.full_of(part, f"oT{j}{g}"), 1)
                for g in range(2):
                    turn.wait_read(pe, part, f"oT{j}{g}")
                proj.wait_empty(pe, part, f"out{j}")
                group_of(proj.bank(part, f"out{j}")[:, 0:HID], [(oT[:, k], out_w_sb[:, k]) for k in range(KO)])\
                    .then_inc(proj.full_of(part, f"out{j}"), 1)

            def fqkv(part):
                turn.wait_read(pe, part, "hnT")
                for m in range(KH):
                    proj.wait_empty(pe, part, f"fqk{m}")
                    for s, weights in enumerate((wq_sb, wk_sb)):
                        ins = group_of(proj.bank(part, f"fqk{m}")[:, s * GT:(s + 1) * GT],
                                       [(weights[:, k, m * P:(m + 1) * P], hnT[:, k]) for k in range(KH)])
                    ins.then_inc(proj.full_of(part, f"fqk{m}"), 1)
                proj.wait_empty(pe, part, "fv")
                for j in range(2):
                    ins = group_of(proj.bank(part, "fv")[:, j * HID:(j + 1) * HID],
                                   [(hnT[:, k, j * P:(j + 1) * P], wv_sb[:, k]) for k in range(KH)])
                ins.then_inc(proj.full_of(part, "fv"), 1)

            def gate(part):
                turn.wait_read(pe, part, "z2T")
                proj.wait_empty(pe, part, "gate")
                for j in range(2):
                    ins = group_of(proj.bank(part, "gate")[:, j * EXPERTS:(j + 1) * EXPERTS],
                                   [(hn2T[:, k, j * P:(j + 1) * P], gate_w_sb[:, k]) for k in range(KH)])
                ins.then_inc(proj.full_of(part, "gate"), 1)

            def work(part):
                c, f = part.c, part.f
                if c is not None:
                    tokens(part)
                if f is not None:
                    turn_rows(part, "hnT", z1, norm["1"]["out"], f)
                    fqkv(part)
                if c is not None:
                    turn_z(part)
                    if part.kind == "first":
                        pe.wait_ge(qkv_sorted, 3)
                if f is not None:
                    for m in range(KH):
                        proj.wait_read(pe, part, f"fqk{m}")
                    fscores(part, 0)
                    fscores(part, 1)
                if c is not None:
                    for m in range(4):
                        qk(part, m)
                if f is not None:
                    turn_probs(part, "f", fprobs, 0, f)
                    fscores(part, 2)
                    fscores(part, 3)
                if c is not None:
                    qk(part, 4)
                    qk(part, 5)
                if f is not None:
                    fmix_values(part, 0)
                if c is not None:
                    qk(part, 6)
                    qk(part, 7)
                if f is not None:
                    turn_probs(part, "f", fprobs, 1, f)
                    fmix_values(part, 1)
                if c is not None:
                    scores(part, 0)
                    scores(part, 1)
                    values(part, 0)
                if f is not None:
                    turn_fo(part, 0)
                    turn_fo(part, 1)
                if c is not None:
                    scores(part, 2)
                    scores(part, 3)
                if f is not None:
                    fout(part, 0)
                    fout(part, 1)
                if c is not None:
                    values(part, 1)
                    turn_probs(part, "c", probs, 0, c)
                    mix_values(part, 0)
                if f is not None:
                    turn_rows(part, "z2T", z2, norm["2"]["out"], f)
                if c is not None:
                    turn_probs(part, "c", probs, 1, c)
                if f is not None:
                    gate(part)
                if c is not None:
                    mix_values(part, 1)
                    if part.kind == "first":
                        pe.wait_ge(out_w_landed, 16)
                    out_proj(part, 0)
                    out_proj(part, 1)

            pe.wait_ge(consts_made, 3)
            pe.wait_ge(vectors_landed, 128)
            pe.transpose(turn.banks[0][:, 0:ROWS], vector_rows[:], identity[0:ROWS, 0:ROWS]).then_inc(columns_turned, 1)
            pe.wait_ge(columns_ready, 1)
            pe.wait_ge(tok_w_landed, 16)
            work(Part("first"))
            pe.wait_ge(small_w_landed, 80)
            with pe.Fori(0, GROUPS - 2) as i:
                work(Part("body", i))
            work(Part("body", GROUPS - 2))
            work(Part("last"))

            pe.wait_ge(chosen_ready, 1)
            flat = chosen[:].rearrange("p e t -> p (e t)")
            pe.matmul(score.banks[0][:, 0:EXPERTS * TILES], earlier[:], flat, start=True, stop=True).then_inc(ranks_ready, 1)
            pe.matmul(score.banks[1][:, 0:EXPERTS * TILES], ones[:], flat, start=True, stop=True).then_inc(ranks_ready, 1)
            pe.wait_ge(slots_ready, 2)

            def expert(s):
                return pe.value_load(expert_of[0:1, bass.ds(s, 1)], min_val=0, max_val=EXPERTS - 1)

            def turn_in(s):
                pe.wait_ge(slot_in_landed, (s + 1) * 16)
                for k in range(KH):
                    ins = pe.transpose(turn.banks[0][:, k * P:(k + 1) * P], slot_in[:, k * P:(k + 1) * P], identity[:])
                ins.then_inc(slot_inT_full, 1)

            def up(s, e):
                pe.wait_ge(experts_resident, e + 1)
                pe.wait_ge(slot_inT_ready, s + 1)
                for half in range(2):
                    group_of(proj.banks[half][:],
                             [(slot_inT[:, k], expert_w[:, bass.ds(e, 1), k * FFN + half * 512:k * FFN + (half + 1) * 512])
                              for k in range(KH)]).then_inc(mid_full[half], 1)

            def turn_mid(s):
                for half in range(2):
                    pe.wait_ge(mid_ready[half], s + 1)
                    for n in range(KF // 2):
                        at = (half * KF // 2 + n) * P
                        ins = pe.transpose(score.banks[half][:, n * P:(n + 1) * P], mid[:, at:at + P], identity[:])
                    ins.then_inc(midT_full[half], 1)

            def down(s, e):
                for half in range(2):
                    pe.wait_ge(midT_ready[half], s + 1)
                group_of(mix.banks[0][:, 0:HID],
                         [(midT[:, c], expert_w[:, bass.ds(e, 1), KH * FFN + c * HID:KH * FFN + (c + 1) * HID])
                          for c in range(KF)]).then_inc(slot_out_full, 1)

            turn_in(0)
            up(0, expert(0))
            with pe.Fori(0, SLOT_TILES - 1) as s:
                turn_in(s + 1)
                turn_mid(s)
                up(s + 1, expert(s + 1))
                down(s, expert(s))
            turn_mid(SLOT_TILES - 1)
            down(SLOT_TILES - 1, expert(SLOT_TILES - 1))


_INS = ["x", "L0_tok_W", "L0_attn_W_qkv", "L0_attn_W_out", "L0_ffn_ln1_g", "L0_ffn_ln1_b", "L0_ffn_ln2_g",
        "L0_ffn_ln2_b", "L0_ffn_wq", "L0_ffn_bq", "L0_ffn_wk", "L0_ffn_bk", "L0_ffn_wv", "L0_ffn_bv", "L0_ffn_wo",
        "L0_ffn_bo", "L0_ffn_gate_w", "L0_ffn_gate_b", "L0_ffn_w1", "L0_ffn_b1", "L0_ffn_w2", "L0_ffn_b2"]


def kernel(**inputs):
    import numpy as np
    import concourse.bacc as bacc
    from concourse.bass_utils import run_bass_kernel_spmd

    nc = bacc.Bacc("TRN2", target_bir_lowering=False, num_devices=1)
    arrays, args = {}, []
    for name in _INS:
        a = np.ascontiguousarray(inputs[name])
        arrays[f"in_{name}"] = a
        args.append(nc.dram_tensor(f"in_{name}", a.shape, mybir.dt.from_np(a.dtype), kind="ExternalInput").ap())
    args.append(nc.dram_tensor("tower_out", (IMAGES, TOKENS, HID), F32, kind="ExternalOutput").ap())
    vit_tower(nc, *args)
    r = run_bass_kernel_spmd(nc, [arrays], core_ids=[0])
    return r.results[0]["tower_out"]
```

```python
from contextlib import ExitStack

import concourse.bass as bass
from concourse import mybir
from concourse.alu_op_type import AluOpType as ALU

F32 = mybir.dt.float32
I32 = mybir.dt.int32
U32 = mybir.dt.uint32
ACT = mybir.ActivationFunctionType
AX_X = mybir.AxisListType.X

P = 128
IMAGES, CHANNELS, IMG, PATCH = 32, 3, 128, 16
GRID = IMG // PATCH
TOKENS = GRID * GRID
HID = 256
KH = HID // P
FEATURES = CHANNELS * PATCH * PATCH
FT = FEATURES // P
GROUP = 4
GROUPS = IMAGES // GROUP
GT = GROUP * TOKENS
FOLD = FEATURES // TOKENS
BANDS = GROUP * CHANNELS * GRID
FEATURE_LOADS = 16 * 2 * GROUP * CHANNELS
TILES = IMAGES * TOKENS // P
HEADS, D1, D2 = 16, 64, 16
PAIRS = HEADS // 2
HD = HEADS * D1
KO = HD // P
EXPERTS, FFN = 8, 1024
KF = FFN // P
SLOT_TILES = TILES + EXPERTS - 1
EPS = 1e-5
COLUMNS = {"ln1_g": 0, "ln1_b": 2, "ln2_g": 4, "ln2_b": 6, "bq": 8, "bk": 10, "bv": 12, "b1": 14}
ROWS = 14 + EXPERTS * KF


class Part:

    PHASES = {"start": "n", "first": "cn", "body": "cfn", "final": "cf", "last": "f"}

    def __init__(self, kind, i=None):
        self.kind = kind
        self.i = i
        phases = self.PHASES[kind]
        at = {"start": -1, "first": 0, "body": None if i is None else i + 1, "final": GROUPS - 1, "last": GROUPS}[kind]
        self.c = at if "c" in phases else None
        self.f = at - 1 if "f" in phases else None
        self.n = at + 1 if "n" in phases else None


class Ring:

    def __init__(self, nc, ctx, name, uses):
        self.banks = [ctx.enter_context(nc.psum_tensor(f"{name}{b}", [P, 512], F32)) for b in range(2)]
        self.full = [ctx.enter_context(nc.semaphore(f"{name}{b}_full")) for b in range(2)]
        self.emptied = [ctx.enter_context(nc.semaphore(f"{name}{b}_emptied")) for b in range(2)]
        self.uses = {kind: [u for u in uses if u[1] in phases] for kind, phases in Part.PHASES.items()}
        assert all(len(u) % 2 == 0 for u in self.uses.values())

    def _where(self, kind, step):
        return [u[0] for u in self.uses[kind]].index(step)

    def _count(self, kind, b, n=None):
        mine = self.uses[kind][:n][b::2] if n is not None else self.uses[kind][b::2]
        return len(mine), sum(u[2] for u in mine)

    def _before(self, part, b, which):
        start, first, body, final = (self._count(kind, b)[which] for kind in ("start", "first", "body", "final"))
        return {
            "start": 0,
            "first": start,
            "body": start + first + (0 if part.i is None else part.i) * body,
            "final": start + first + (GROUPS - 2) * body,
            "last": start + first + (GROUPS - 2) * body + final,
        }[part.kind]

    def _at(self, part, step, which, inclusive):
        n = self._where(part.kind, step)
        return self._before(part, n % 2, which) + self._count(part.kind, n % 2, n + inclusive)[which]

    def bank(self, part, step):
        return self.banks[self._where(part.kind, step) % 2]

    def wait_empty(self, engine, part, step):
        value = self._at(part, step, 1, 0)
        if not (isinstance(value, int) and value == 0):
            engine.wait_ge(self.emptied[self._where(part.kind, step) % 2], value)

    def wait_full(self, engine, part, step):
        engine.wait_ge(self.full[self._where(part.kind, step) % 2], self._at(part, step, 0, 1))

    def wait_read(self, engine, part, step):
        engine.wait_ge(self.emptied[self._where(part.kind, step) % 2], self._at(part, step, 1, 1))

    def wait_read_in_previous(self, engine, part, step):
        tails = set()
        for kind in {"body": ("first", "body"), "final": ("body",), "last": ("final",)}[part.kind]:
            n = self._where(kind, step)
            tails.add((n % 2, self._count(kind, n % 2)[1] - self._count(kind, n % 2, n + 1)[1]))
        (b, tail), = tails
        engine.wait_ge(self.emptied[b], self._before(part, b, 1) - tail)

    def full_of(self, part, step):
        return self.full[self._where(part.kind, step) % 2]

    def emptied_of(self, part, step):
        return self.emptied[self._where(part.kind, step) % 2]


def vit_tower(nc, x, tok_w, qkv_w, out_w, ln1_g, ln1_b, ln2_g, ln2_b, wq, bq, wk, bk, wv, bv, wo, bo,
              gate_w, gate_b, w1, b1, w2, b2, out):
    ctx = ExitStack()
    with ctx:
        def sb(name, shape, dt=F32, where=ctx):
            return where.enter_context(nc.sbuf_tensor(name, shape, dt))

        def sem(name):
            return ctx.enter_context(nc.semaphore(name))

        slot_rows = nc.dram_tensor("slot_rows", [SLOT_TILES * P, HID], F32, kind="Internal").ap()
        slot_outs = nc.dram_tensor("slot_outs", [SLOT_TILES * P, HID], F32, kind="Internal").ap()

        normed_all = sb("normed_all", [P, TILES, HID])
        residual_all = sb("residual_all", [P, TILES, HID])
        logits_all = sb("logits_all", [P, TILES, EXPERTS])
        bo_row = sb("bo_row", [P, HID])
        gate_b_row = sb("gate_b_row", [P, EXPERTS])
        columns = sb("columns", [P, ROWS])
        identity = sb("identity", [P, P])
        earlier = sb("earlier", [P, P])
        ones = sb("ones", [P, P])
        head_mask = sb("head_mask", [P, HEADS // KH])
        minus_half = sb("minus_half", [P, 2])
        eps = sb("eps", [P, 2])
        wait_carrier = sb("wait_carrier", [P, 1])
        iota_expert = sb("iota_expert", [P, EXPERTS])
        iota_tile = sb("iota_tile", [P, SLOT_TILES])
        iota_128 = sb("iota_128", [P, TILES])
        slot_of = sb("slot_of", [P, TILES], U32)
        expert_of = sb("expert_of", [P, SLOT_TILES], I32)
        gathered = normed_all

        def column(name, k, rows=slice(0, P)):
            return columns[rows, COLUMNS[name] + k:COLUMNS[name] + k + 1]

        tower = ExitStack()
        images_here = ExitStack()
        image_rows = sb("image_rows", [BANDS, PATCH, IMG], where=images_here)
        patch_rows = sb("patch_rows", [BANDS, GRID, PATCH, PATCH], where=images_here)
        images_here.close()
        o_sb = sb("o_sb", [P, 2, HD], where=tower)
        probs = sb("probs", [P, 2, PAIRS, 2, TOKENS], where=tower)
        features = sb("features", [P, GROUP * FEATURES + 2], where=tower)
        kT = sb("kT", [P, PAIRS, GT], where=tower)
        v_sb = sb("v_sb", [P, 2, HD], where=tower)
        oT = sb("oT", [P, KO, P], where=tower)
        tok_w_sb = sb("tok_w_sb", [P, FT, HID], where=tower)
        qk_w = sb("qk_w", [P, KH, PAIRS, 2, P], where=tower)
        v_w = sb("v_w", [P, KH, HD], where=tower)
        out_w_sb = sb("out_w_sb", [P, KO, HID], where=tower)
        raw_here = ExitStack()
        qkv_raw = sb("qkv_raw", [P, KH, 3 * HD], where=raw_here)
        raw_here.close()
        q_diag = sb("q_diag", [P, PAIRS, GROUP, P], where=tower)
        probsT = sb("probsT", [P, HEADS, P], where=tower)
        h1 = sb("h1", [P, 2, HID], where=tower)
        z = sb("z", [P, 2, HID], where=tower)
        zT = sb("zT", [P, KH, GT], where=tower)
        vectors_here = ExitStack()
        vector_rows = sb("vector_rows", [ROWS, P], where=vectors_here)
        vectors_here.close()
        h2 = sb("h2", [P, 2, HID], where=tower)
        fprobs = sb("fprobs", [P, 2, PAIRS, 2, TOKENS], where=tower)
        fq_heads = sb("fq_heads", [P, 2, KH, HEADS // KH, TOKENS], where=tower)
        wq_sb = sb("wq_sb", [P, KH, HID], where=tower)
        wk_sb = sb("wk_sb", [P, KH, HID], where=tower)
        wv_sb = sb("wv_sb", [P, KH, HID], where=tower)
        wo_sb = sb("wo_sb", [P, KH, HID], where=tower)
        gate_w_sb = sb("gate_w_sb", [P, KH, EXPERTS], where=tower)
        u = sb("u", [P, 2, HID], where=tower)
        u_bo = sb("u_bo", [P, 2, HID], where=tower)
        z1 = sb("z1", [P, 2, HID], where=tower)
        z2 = z1
        hnT = sb("hnT", [P, KH, GT], where=tower)
        hn2T = hnT
        fq = sb("fq", [P, KH, GT], where=tower)
        fkT = sb("fkT", [P, KH, GT], where=tower)
        fv = sb("fv", [P, 2, HID], where=tower)
        fprobsT = sb("fprobsT", [P, HEADS, P], where=tower)
        fo = sb("fo", [P, 2, HID], where=tower)
        foT = sb("foT", [P, 2, KH, P], where=tower)
        x2 = sb("x2", [P, 2, HID], where=tower)
        small = {}
        for n in ("a", "u", "1", "2"):
            small[n] = (sb(f"stats_{n}", [P, 2, 6], where=tower), sb(f"moments_{n}", [P, 2, 2], where=tower),
                        sb(f"var_eps_{n}", [P, 2], where=tower), sb(f"rstd_{n}", [P, 2], where=tower))
        soft = {}
        for n in ("c", "f"):
            soft[n] = tuple(sb(f"{what}_{n}", [P, GROUP, PAIRS], where=tower) for what in ("max", "sum", "rsum"))
        tower.close()

        experts = ExitStack()
        expert_w = sb("expert_w", [P, EXPERTS, KH * FFN + KF * HID], where=experts)
        b2_rows = sb("b2_rows", [P, EXPERTS * HID], where=experts)
        slot_in = sb("slot_in", [P, 2, HID], where=experts)
        slot_inT = sb("slot_inT", [P, KH, P], where=experts)
        mid = sb("mid", [P, FFN], where=experts)
        midT = sb("midT", [P, KF, P], where=experts)
        b1_now = sb("b1_now", [P, KF], where=experts)
        slot_out = sb("slot_out", [P, HID], where=experts)
        r_max = sb("r_max", [P, TILES], where=experts)
        r_cand = sb("r_cand", [P, TILES, EXPERTS], where=experts)
        r_first = sb("r_first", [P, TILES], where=experts)
        chosen = sb("chosen", [P, EXPERTS, TILES], where=experts)
        r_incl = sb("r_incl", [P, EXPERTS, TILES], where=experts)
        r_excl = sb("r_excl", [P, EXPERTS, TILES], where=experts)
        r_work = sb("r_work", [P, EXPERTS, TILES], where=experts)
        r_count = sb("r_count", [P, EXPERTS], where=experts)
        r_tiles = sb("r_tiles", [P, EXPERTS], where=experts)
        r_end = sb("r_end", [P, EXPERTS], where=experts)
        r_shift = sb("r_shift", [P, EXPERTS], where=experts)
        r_slot = sb("r_slot", [P, TILES], where=experts)
        r_ended = sb("r_ended", [P, SLOT_TILES, EXPERTS - 1], where=experts)
        r_expert = sb("r_expert", [P, SLOT_TILES], where=experts)
        experts.close()

        turn = Ring(nc, ctx, "turn", [
            ("zT0", "c", 1), ("zT1", "c", 1), ("hnT", "f", 1), ("fpT00", "f", 2), ("fpT01", "f", 2),
            ("fpT10", "f", 2), ("fpT11", "f", 2), ("pT00", "c", 2), ("pT01", "c", 2), ("foT0", "f", 1),
            ("foT1", "f", 1), ("pT10", "c", 2), ("pT11", "c", 2), ("oT00", "c", 1), ("oT01", "c", 1),
            ("z2T", "f", 1), ("oT10", "c", 1), ("oT11", "c", 1)])
        proj = Ring(nc, ctx, "proj", [
            ("qk0", "c", 1), ("qk1", "c", 1), ("qk2", "c", 1), ("qk3", "c", 1), ("fqk0", "f", 1), ("fqk1", "f", 1),
            ("fv0", "f", 1), ("fv1", "f", 1), ("qk4", "c", 1), ("qk5", "c", 1), ("qk6", "c", 1), ("qk7", "c", 1), ("v00", "c", 1),
            ("v01", "c", 1), ("v10", "c", 1), ("v11", "c", 1), ("wo0", "f", 1), ("wo1", "f", 1), ("out0", "c", 1),
            ("gate0", "f", 1), ("gate1", "f", 1), ("tok0", "n", 1), ("tok1", "n", 1), ("out1", "c", 1)])
        score = Ring(nc, ctx, "score", [("fs0", "f", 1), ("fs1", "f", 1), ("fs2", "f", 1), ("fs3", "f", 1),
                                        ("s0", "c", 1), ("s1", "c", 1), ("s2", "c", 1), ("s3", "c", 1)])
        mix = Ring(nc, ctx, "mix", [("fo0", "f", 1), ("fo1", "f", 1), ("o00", "c", 1), ("o01", "c", 1),
                                    ("o10", "c", 1), ("o11", "c", 1)])

        consts_made = sem("consts_made")
        vectors_landed = sem("vectors_landed")
        columns_ready = sem("columns_ready")
        columns_turned = sem("columns_turned")
        rows_landed = sem("rows_landed")
        tok_w_landed = sem("tok_w_landed")
        qkv_landed = sem("qkv_landed")
        qkv_sorted = sem("qkv_sorted")
        out_w_landed = sem("out_w_landed")
        small_w_landed = sem("small_w_landed")
        image_landed = sem("image_landed")
        image_used = sem("image_used")
        blocks_zero = sem("blocks_zero")
        fprobsT_zero = sem("fprobsT_zero")
        patch_rows_ready = sem("patch_rows_ready")
        features_landed = sem("features_landed")
        slots_cleared = sem("slots_cleared")
        norm = {n: {s: sem(f"norm_{n}_{s}") for s in ("stats", "moments", "var_eps", "rstd", "out")}
                for n in ("a", "u", "1", "2")}
        u_bo_ready = sem("u_bo_ready")
        h1_moved = sem("h1_moved")
        fq_heads_ready = sem("fq_heads_ready")
        softmax = {n: {s: sem(f"softmax_{n}_{s}") for s in ("max", "exp", "sum", "rsum", "probs")}
                   for n in ("c", "f")}
        residual_kept = sem("residual_kept")
        normed_kept = sem("normed_kept")
        route = sem("route")
        chosen_ready = sem("chosen_ready")
        ranks_ready = sem("ranks_ready")
        slots_ready = sem("slots_ready")
        scattered = sem("scattered")
        expert_landed = [sem(f"expert_landed{e}") for e in range(EXPERTS)]
        b2_landed = sem("b2_landed")
        experts_resident = sem("experts_resident")
        slot_in_landed = [sem(f"slot_in_landed{n}") for n in range(2)]
        slot_inT_full = sem("slot_inT_full")
        slot_inT_ready = sem("slot_inT_ready")
        mid_full = [sem(f"mid_full{n}") for n in range(2)]
        mid_ready = [sem(f"mid_ready{n}") for n in range(2)]
        midT_full = [sem(f"midT_full{n}") for n in range(2)]
        midT_ready = [sem(f"midT_ready{n}") for n in range(2)]
        b1_ready = sem("b1_ready")
        slot_out_full = sem("slot_out_full")
        slot_out_ready = sem("slot_out_ready")
        slot_out_stored = sem("slot_out_stored")
        gather_landed = [sem(f"gather_landed{n}") for n in range(4)]
        sums_ready = sem("sums_ready")
        out_stored = sem("out_stored")

        expert_w1 = expert_w[:, :, 0:KH * FFN].rearrange("p e (k f) -> p e k f", k=KH)
        expert_w2 = expert_w[:, :, KH * FFN:].rearrange("p e (c h) -> p e c h", c=KF)
        by_token = features[:, 1:1 + GROUP * FEATURES].rearrange("p (n a) -> p n a", a=FOLD)

        def of_image(tile, b):
            return tile[:, b // 2, :, b % 2]

        def per_group(per, group, done):
            return group * per + done

        block = ctx.enter_context(nc.Block())

        @block.sync
        def _(sync):
            def load_images(g):
                src = x[bass.ds(g * GROUP, GROUP)].rearrange("b c (i r) w -> (b c i) r w", i=GRID)
                sync.dma_start(image_rows[:], src).then_inc(image_landed, 16)

            def load_features(g):
                sync.wait_ge(patch_rows_ready, g + 1)
                rows = patch_rows[:].rearrange("p j r w -> p j (r w)")
                for n in range(GROUP * CHANNELS):
                    for half in range(2):
                        at = n * PATCH * PATCH + 1 - half
                        sync.dma_start(features[half * TOKENS:(half + 1) * TOKENS, at:at + PATCH * PATCH],
                                       rows[n * GRID:(n + 1) * GRID]).then_inc(features_landed, 16)

            load_images(0)
            sync.dma_start(tok_w_sb[:], tok_w.rearrange("(t p) h -> p t h", p=P)).then_inc(tok_w_landed, 16)
            for k in range(KH):
                sync.dma_start(qkv_raw[:, k, :], qkv_w[k * P:(k + 1) * P, :]).then_inc(qkv_landed, 16)
            load_features(0)
            sync.dma_start(out_w_sb[:], out_w.rearrange("(c p) h -> p c h", p=P)).then_inc(out_w_landed, 16)
            sync.wait_ge(fprobsT_zero, 1)
            sync.dma_start(slot_rows.rearrange("(s p) h -> p s h", p=P),
                           fprobsT[:, 0:HID // P].rearrange("p a b -> p (a b)").unsqueeze(1)
                           .broadcast_to([P, SLOT_TILES, HID])).then_inc(slots_cleared, 16)
            with sync.Fori(1, GROUPS) as g:
                sync.wait_ge(image_used, g)
                load_images(g)
                load_features(g)
            def load_expert(e):
                sync.dma_start(expert_w1[:, e], w1[e].rearrange("(k p) f -> p k f", p=P))\
                    .then_inc(expert_landed[e], 16)
                sync.dma_start(expert_w2[:, e], w2[e].rearrange("(c p) h -> p c h", p=P))\
                    .then_inc(expert_landed[e], 16)

            proj.wait_read(sync, Part("final"), "out1")
            for e in range(EXPERTS - 1):
                load_expert(e)
            for j in range(2):
                proj.wait_read(sync, Part("last"), f"gate{j}")
            sync.wait_ge(normed_kept, TILES)

            def load_slot_tile(s, buffer):
                sync.dma_start(slot_in[:, buffer], slot_rows[bass.ds(s * P, P), :]).then_inc(slot_in_landed[buffer], 16)

            def store_slot_tile(s):
                sync.wait_ge(slot_out_ready, s + 1)
                sync.dma_start(slot_outs[bass.ds(s * P, P), :], slot_out[:]).then_inc(slot_out_stored, 16)

            def slot_tile(s, buffer, load=True):
                if load:
                    sync.wait_ge(slot_inT_full, s + 1)
                    load_slot_tile(s + 2, buffer)
                store_slot_tile(s)

            sync.wait_ge(scattered, 16 * TILES)
            load_slot_tile(0, 0)
            sync.dma_start(b2_rows[:], b2.rearrange("e h -> (e h)").partition_broadcast(P)).then_inc(b2_landed, 16)
            load_slot_tile(1, 1)
            load_expert(EXPERTS - 1)
            with sync.Fori(0, (SLOT_TILES - 3) // 2) as pair:
                slot_tile(2 * pair, 0)
                slot_tile(2 * pair + 1, 1)
            slot_tile(SLOT_TILES - 3, 0)
            slot_tile(SLOT_TILES - 2, 1, load=False)
            slot_tile(SLOT_TILES - 1, 0, load=False)
            out_rows = out.rearrange("b t h -> (b t) h").rearrange("(t p) h -> p t h", p=P)
            for n in range(4):
                sync.wait_ge(sums_ready, n + 1)
                sync.dma_start(out_rows[:, 4 * n:4 * n + 4], gathered[:, 4 * n:4 * n + 4]).then_inc(out_stored, 16)
            sync.wait_ge(out_stored, 64)

        @block.gpsimd
        def _(pool):
            pool.memset(identity[:], 0.0)
            pool.memset(earlier[:], 1.0)
            pool.memset(head_mask[:], 1.0)
            pool.memset(minus_half[:], -0.5)
            pool.memset(eps[:], EPS)
            pool.memset(ones[:], 1.0)
            pool.iota(iota_expert[:], pattern=[[1, EXPERTS]], base=0, channel_multiplier=0,
                      allow_small_or_imprecise_dtypes=True)
            pool.iota(iota_tile[:], pattern=[[1, SLOT_TILES]], base=0, channel_multiplier=0,
                      allow_small_or_imprecise_dtypes=True)
            pool.iota(iota_128[:], pattern=[[P, TILES]], base=0, channel_multiplier=0,
                      allow_small_or_imprecise_dtypes=True).then_inc(consts_made, 1)
            pool.wait_ge(consts_made, 1)
            pool.affine_select(out=identity[:], in_=identity[:], compare_op=ALU.not_equal, fill=1.0, base=0,
                               pattern=[[-1, P]], channel_multiplier=1)
            pool.affine_select(out=earlier[:], in_=earlier[:], compare_op=ALU.is_gt, fill=0.0, base=0,
                               pattern=[[1, P]], channel_multiplier=-1)
            pool.affine_select(out=head_mask[:], in_=head_mask[:], compare_op=ALU.is_ge, fill=0.0, base=0,
                               pattern=[[-D2, HEADS // KH]], channel_multiplier=1).then_inc(consts_made, 1)
            pool.wait_ge(consts_made, 2)
            pool.affine_select(out=head_mask[:], in_=head_mask[:], compare_op=ALU.is_ge, fill=0.0, base=D2 - 1,
                               pattern=[[D2, HEADS // KH]], channel_multiplier=-1).then_inc(consts_made, 1)
            pool.memset(fprobsT[:], 0.0).then_inc(fprobsT_zero, 1)

            for name, src in (("ln1_g", ln1_g), ("ln1_b", ln1_b), ("ln2_g", ln2_g), ("ln2_b", ln2_b),
                              ("bq", bq), ("bk", bk), ("bv", bv)):
                pool.dma_start(vector_rows[COLUMNS[name]:COLUMNS[name] + KH],
                               src.rearrange("(k p) -> k p", p=P)).then_inc(vectors_landed, 16)
            pool.dma_start(vector_rows[COLUMNS["b1"]:ROWS], b1.rearrange("e (c p) -> (e c) p", p=P))\
                .then_inc(vectors_landed, 16)
            pool.dma_start(bo_row[:], bo.partition_broadcast(P)).then_inc(rows_landed, 16)
            pool.dma_start(gate_b_row[:], gate_b.partition_broadcast(P)).then_inc(rows_landed, 16)
            for tile, src in ((wq_sb, wq), (wk_sb, wk), (wv_sb, wv), (wo_sb, wo), (gate_w_sb, gate_w)):
                pool.dma_start(tile[:], src.rearrange("(k p) h -> p k h", p=P)).then_inc(small_w_landed, 16)

            pool.wait_ge(qkv_landed, 32)
            by_kind = qkv_raw[:].rearrange("p k (m c s) -> p k s m c", m=PAIRS, s=3)
            pool.tensor_copy(v_w[:, 1].rearrange("p (m c) -> p m c", m=PAIRS), by_kind[:, 1, 2]).then_inc(qkv_sorted, 1)
            pool.wait_ge(qkv_sorted, 3)
            pool.memset(probsT[:], 0.0).then_inc(blocks_zero, 1)

            def root(n, group):
                _, moments, var_eps, rstd = small[n]
                pool.wait_ge(norm[n]["moments"], per_group(2, group, 2))
                pool.tensor_tensor(var_eps[:], moments[:, :, 1], eps[:], ALU.add).then_inc(norm[n]["var_eps"], 1)
                pool.wait_ge(norm[n]["var_eps"], per_group(1, group, 1))
                pool.tensor_tensor(rstd[:], var_eps[:], minus_half[:], ALU.pow).then_inc(norm[n]["rstd"], 1)

            def scale_probs(n, tile, b, group):
                pool.wait_ge(softmax[n]["rsum"], per_group(GROUP, group, b + 1))
                rows = of_image(tile, b)
                pool.tensor_tensor(rows, rows, soft[n][2][:, b].unsqueeze(2).broadcast_to([P, PAIRS, TOKENS]),
                                   ALU.mult).then_inc(softmax[n]["probs"], 1)

            def bo_to_u(part):
                pool.wait_ge(norm["u"]["out"], per_group(2, part.f, 2))
                for j in range(2):
                    pool.tensor_tensor(u_bo[:, j], u[:, j], bo_row[:], ALU.add).then_inc(u_bo_ready, 1)

            def queries_by_head(part, images):
                for m in range(KH):
                    proj.wait_read(pool, part, f"fqk{m}")
                for b in images:
                    if b >= 2:
                        score.wait_full(pool, part, f"fs{b - 2}")
                    for m in range(KH):
                        pool.tensor_tensor(
                            fq_heads[:, b % 2, m],
                            fq[:, m, b * TOKENS:(b + 1) * TOKENS].unsqueeze(1).broadcast_to([P, HEADS // KH, TOKENS]),
                            head_mask[:].unsqueeze(2).broadcast_to([P, HEADS // KH, TOKENS]),
                            ALU.mult).then_inc(fq_heads_ready, 1)

            def keep_residual(part):
                for j in range(2):
                    proj.wait_read(pool, part, f"wo{j}")
                    pool.tensor_tensor(residual_all[:, bass.ds(part.f * 2 + j, 1)], h2[:, j:j + 1], x2[:, j:j + 1],
                                       ALU.add)\
                        .then_inc(residual_kept, 1)

            def keep_normed(part):
                for j in range(2):
                    pool.wait_ge(norm["2"]["out"], per_group(2, part.f, j + 1))
                    pool.tensor_copy(normed_all[:, bass.ds(part.f * 2 + j, 1)], z2[:, j:j + 1]).then_inc(normed_kept, 1)

            def work(part):
                c, f, n = part.c, part.f, part.n
                if f is not None:
                    root("u", f)
                    root("1", f)
                    queries_by_head(part, (0, 1, 2))
                    scale_probs("f", fprobs, 0, f)
                    queries_by_head(part, (3,))
                    scale_probs("f", fprobs, 1, f)
                    bo_to_u(part)
                    scale_probs("f", fprobs, 2, f)
                    scale_probs("f", fprobs, 3, f)
                if c is not None:
                    for b in range(GROUP):
                        scale_probs("c", probs, b, c)
                if f is not None:
                    root("2", f)
                    keep_residual(part)
                    keep_normed(part)
                if n is not None:
                    root("a", n)

            pool.wait_ge(rows_landed, 32)
            work(Part("start"))
            work(Part("first"))
            with pool.Fori(0, GROUPS - 2) as i:
                work(Part("body", i))
            work(Part("final"))
            work(Part("last"))

            pool.wait_ge(slots_cleared, 16)
            pool.wait_ge(slots_ready, 1)
            pool.wait_ge(normed_kept, TILES)
            for t in range(TILES):
                pool.indirect_dma_start(out=slot_rows, out_offset=bass.IndirectOffsetOnAxis(ap=slot_of[:, t:t + 1], axis=0),
                                        in_=normed_all[:, t], in_offset=None).then_inc(scattered, 16)

            for e in range(EXPERTS):
                pool.wait_ge(expert_landed[e], 32)
                pool.sem_inc(experts_resident, 1)

            pool.wait_ge(slot_out_stored, 16 * SLOT_TILES)
            for t in range(TILES):
                pool.indirect_dma_start(out=gathered[:, t], out_offset=None, in_=slot_outs,
                                        in_offset=bass.IndirectOffsetOnAxis(ap=slot_of[:, t:t + 1], axis=0))\
                    .then_inc(gather_landed[t // 4], 16)

        @block.vector
        def _(dve):
            def stats(n, tile, j):
                dve.bn_stats(small[n][0][:, j], tile[:, j]).then_inc(norm[n]["stats"], 1)

            def moments(n, group):
                dve.wait_ge(norm[n]["stats"], per_group(2, group, 2))
                dve.memset(wait_carrier[:], 0.0)
                for j in range(2):
                    dve.bn_aggr(small[n][1][:, j], small[n][0][:, j]).then_inc(norm[n]["moments"], 1)

            def normed(n, dst, src, group):
                dve.wait_ge(norm[n]["rstd"], per_group(1, group, 1))
                for j in range(2):
                    dve.tensor_scalar(dst[:, j], src[:, j], small[n][1][:, j, 0:1], small[n][3][:, j:j + 1],
                                      ALU.subtract, ALU.mult).then_inc(norm[n]["out"], 1)

            def minus_max(n, tile, b, part, step, group):
                score.wait_full(dve, part, step)
                scores = score.bank(part, step)[:].rearrange("p (h t) -> p h t", h=PAIRS)
                dve.tensor_reduce(soft[n][0][:, b], scores, AX_X, ALU.max).then_inc(softmax[n]["max"], 1)
                dve.wait_ge(softmax[n]["max"], per_group(GROUP, group, b + 1))
                dve.tensor_tensor(of_image(tile, b), scores,
                                  soft[n][0][:, b].unsqueeze(2).broadcast_to([P, PAIRS, TOKENS]), ALU.subtract)\
                    .then_inc(score.emptied_of(part, step), 1)

            def row_sums(n, tile, b, group):
                dve.wait_ge(softmax[n]["exp"], per_group(GROUP, group, b + 1))
                dve.tensor_reduce(soft[n][1][:, b], of_image(tile, b), AX_X, ALU.add)\
                    .then_inc(softmax[n]["sum"], 1)
                dve.wait_ge(softmax[n]["sum"], per_group(GROUP, group, b + 1))
                dve.reciprocal(soft[n][2][:, b], soft[n][1][:, b]).then_inc(softmax[n]["rsum"], 1)

            def from_ring(ring, part, step, dst, src):
                ring.wait_full(dve, part, step)
                dve.tensor_copy(dst, src(ring.bank(part, step))).then_inc(ring.emptied_of(part, step), 1)

            def odd_image_blocks(part, steps, dst):
                for g, step in enumerate(steps):
                    turn.wait_full(dve, part, step)
                    src = turn.bank(part, step)[TOKENS:P].rearrange("p (h t) -> p h t", h=8)
                    dve.tensor_copy(dst[TOKENS:P, 8 * g:8 * g + 8, TOKENS:P], src)\
                        .then_inc(turn.emptied_of(part, step), 1)

            def by_patch(g):
                dve.wait_ge(image_landed, 16 * (g + 1))
                dve.tensor_copy(patch_rows[:], image_rows[:].rearrange("p r (j w) -> p j r w", j=GRID))\
                    .then_inc(patch_rows_ready, 1)

            def qk_out(part, m):
                step = f"qk{m}"
                proj.wait_full(dve, part, step)
                bank = proj.bank(part, step)
                for half in range(2):
                    rows = slice(half * D1, (half + 1) * D1)
                    dve.tensor_copy(q_diag[rows, m, :, rows], bank[rows, 0:GT].rearrange("p (b t) -> p b t", b=GROUP))
                dve.tensor_copy(kT[:, m], bank[:, GT:2 * GT]).then_inc(proj.emptied_of(part, step), 1)

            def h2_out(part, j):
                proj.wait_full(dve, part, f"out{j}")
                dve.wait_ge(h1_moved, per_group(1, part.c, 1))
                dve.tensor_tensor(h2[:, j], proj.bank(part, f"out{j}")[:, 0:HID], h2[:, j], ALU.add)\
                    .then_inc(proj.emptied_of(part, f"out{j}"), 1)

            def work(part):
                c, f, n = part.c, part.f, part.n
                if f is not None:
                    proj.wait_read_in_previous(dve, part, "out1")
                    for j in range(2):
                        stats("u", h2, j)
                    moments("u", f)
                    normed("u", u, h2, f)
                    dve.wait_ge(norm["u"]["out"], per_group(2, f, 2))
                    for j in range(2):
                        stats("1", u, j)
                    moments("1", f)
                if c is not None:
                    qk_out(part, 1)
                if f is not None:
                    normed("1", z1, u, f)
                if c is not None:
                    if n is not None:
                        by_patch(n)
                    qk_out(part, 3)
                if f is not None:
                    proj.wait_full(dve, part, "fqk1")
                    bank = proj.bank(part, "fqk1")
                    dve.tensor_scalar(fq[:, 1], bank[:, 0:GT], column("bq", 1), None, ALU.add)
                    dve.tensor_scalar(fkT[:, 1], bank[:, GT:2 * GT], column("bk", 1), None, ALU.add)\
                        .then_inc(proj.emptied_of(part, "fqk1"), 1)
                    minus_max("f", fprobs, 0, part, "fs0", f)
                if c is not None:
                    qk_out(part, 5)
                if f is not None:
                    minus_max("f", fprobs, 1, part, "fs1", f)
                    row_sums("f", fprobs, 0, f)
                if c is not None:
                    qk_out(part, 7)
                if f is not None:
                    row_sums("f", fprobs, 1, f)
                if c is not None:
                    from_ring(proj, part, "v01", v_sb[:, 0, 512:], lambda bank: bank[:])
                if f is not None:
                    odd_image_blocks(part, ("fpT00", "fpT01"), fprobsT)
                    minus_max("f", fprobs, 2, part, "fs2", f)
                    minus_max("f", fprobs, 3, part, "fs3", f)
                if c is not None:
                    if n is not None:
                        dve.wait_ge(features_landed, per_group(FEATURE_LOADS, n, FEATURE_LOADS))
                    minus_max("c", probs, 0, part, "s0", c)
                    minus_max("c", probs, 1, part, "s1", c)
                if f is not None:
                    row_sums("f", fprobs, 2, f)
                    row_sums("f", fprobs, 3, f)
                if c is not None:
                    row_sums("c", probs, 0, c)
                    row_sums("c", probs, 1, c)
                    from_ring(proj, part, "v11", v_sb[:, 1, 512:], lambda bank: bank[:])
                if f is not None:
                    odd_image_blocks(part, ("fpT10", "fpT11"), fprobsT)
                if c is not None:
                    minus_max("c", probs, 2, part, "s2", c)
                    minus_max("c", probs, 3, part, "s3", c)
                    row_sums("c", probs, 2, c)
                if f is not None:
                    from_ring(mix, part, "fo1", fo[:, 1], lambda bank: bank[:, 0:HID])
                if c is not None:
                    row_sums("c", probs, 3, c)
                    odd_image_blocks(part, ("pT00", "pT01"), probsT)
                    from_ring(mix, part, "o01", o_sb[:, 0, 512:], lambda bank: bank[:])
                if f is not None:
                    for j in range(2):
                        dve.wait_ge(u_bo_ready, per_group(2, f, j + 1))
                        proj.wait_full(dve, part, f"wo{j}")
                        dve.tensor_tensor(x2[:, j], proj.bank(part, f"wo{j}")[:, 0:HID], u_bo[:, j], ALU.add)\
                            .then_inc(proj.emptied_of(part, f"wo{j}"), 1)
                    for j in range(2):
                        proj.wait_read(dve, part, f"wo{j}")
                        stats("2", x2, j)
                    moments("2", f)
                if c is not None:
                    odd_image_blocks(part, ("pT10", "pT11"), probsT)
                if f is not None:
                    normed("2", z2, x2, f)
                if c is not None:
                    from_ring(turn, part, "oT01", oT[:, KO // 2:], lambda bank: bank[:].rearrange("p (a t) -> p a t", t=P))
                    from_ring(mix, part, "o11", o_sb[:, 1, 512:], lambda bank: bank[:])
                    h2_out(part, 0)
                if f is not None:
                    for j in range(2):
                        proj.wait_full(dve, part, f"gate{j}")
                        dve.tensor_tensor(logits_all[:, bass.ds(f * 2 + j, 1)],
                                          proj.bank(part, f"gate{j}")[:, 0:EXPERTS].unsqueeze(1),
                                          gate_b_row[:].unsqueeze(1), ALU.add)\
                            .then_inc(proj.emptied_of(part, f"gate{j}"), 1)
                if c is not None:
                    from_ring(turn, part, "oT11", oT[:, KO // 2:], lambda bank: bank[:].rearrange("p (a t) -> p a t", t=P))
                if n is not None:
                    if c is not None:
                        dve.wait_ge(h1_moved, per_group(1, c, 1))
                    from_ring(proj, part, "tok1", h1[:, 1], lambda bank: bank[:, 0:HID])
                    for j in range(2):
                        proj.wait_read(dve, part, f"tok{j}")
                        stats("a", h1, j)
                    moments("a", n)
                    normed("a", z, h1, n)
                if c is not None:
                    h2_out(part, 1)

            by_patch(0)
            dve.wait_ge(columns_turned, 1)
            dve.tensor_copy(columns[:], turn.banks[0][:, 0:ROWS]).then_inc(columns_ready, 1)
            dve.wait_ge(qkv_landed, 32)
            by_kind = qkv_raw[:].rearrange("p k (m c s) -> p k s m c", m=PAIRS, s=3)
            for s in range(2):
                dve.tensor_copy(qk_w[:, 0, :, s], by_kind[:, 0, s])
            dve.tensor_copy(v_w[:, 0].rearrange("p (m c) -> p m c", m=PAIRS), by_kind[:, 0, 2]).then_inc(qkv_sorted, 1)
            dve.wait_ge(qkv_sorted, 3)
            dve.memset(q_diag[:], 0.0).then_inc(blocks_zero, 1)
            work(Part("start"))
            dve.wait_ge(blocks_zero, 2)
            dve.wait_ge(columns_ready, 1)
            dve.wait_ge(rows_landed, 32)
            work(Part("first"))
            dve.wait_ge(slots_cleared, 16)
            with dve.Fori(0, GROUPS - 2) as i:
                work(Part("body", i))
            work(Part("final"))
            work(Part("last"))

            steps = [0]

            def then(ins):
                steps[0] += 1
                ins.then_inc(route, 1)
                dve.wait_ge(route, steps[0])

            last = Part("last")
            for j in range(2):
                proj.wait_read(dve, last, f"gate{j}")
            dve.wait_ge(normed_kept, TILES)
            by_tile = [P, TILES, EXPERTS]
            ranks_of = iota_expert[:].unsqueeze(1).broadcast_to(by_tile)
            then(dve.tensor_reduce(r_max[:], logits_all[:], AX_X, ALU.max))
            then(dve.tensor_tensor(r_cand[:], logits_all[:], r_max[:].unsqueeze(2).broadcast_to(by_tile), ALU.is_lt))
            then(dve.scalar_tensor_tensor(r_cand[:], r_cand[:], float(EXPERTS), ranks_of, ALU.mult, ALU.add))
            then(dve.tensor_reduce(r_first[:], r_cand[:], AX_X, ALU.min))
            dve.tensor_tensor(chosen[:].rearrange("p e t -> p t e"), r_first[:].unsqueeze(2).broadcast_to(by_tile),
                              ranks_of, ALU.is_equal).then_inc(chosen_ready, 1)
            dve.wait_ge(ranks_ready, 2)
            ranks = score.banks[0][:, 0:EXPERTS * TILES].rearrange("p (e t) -> p e t", e=EXPERTS)
            totals = score.banks[1][:, 0:EXPERTS * TILES]
            totals_3d = totals.rearrange("p (e t) -> p e t", e=EXPERTS)
            flat = lambda tile: tile[:].rearrange("p e t -> p (e t)")
            then(dve.tensor_tensor_scan(flat(r_incl), ones[:], totals, 0.0, ALU.mult, ALU.add))
            then(dve.tensor_tensor(r_excl[:], r_incl[:], totals_3d, ALU.subtract))
            then(dve.tensor_reduce(r_count[:], totals_3d, AX_X, ALU.add))
            by_expert = [P, EXPERTS, TILES]
            then(dve.tensor_tensor(r_work[:], r_count[:].unsqueeze(2).broadcast_to(by_expert),
                                   iota_128[:].unsqueeze(1).broadcast_to(by_expert), ALU.is_gt))
            then(dve.tensor_reduce(r_tiles[:], r_work[:], AX_X, ALU.add))
            then(dve.tensor_tensor_scan(r_end[:], ones[:, 0:EXPERTS], r_tiles[:], 0.0, ALU.mult, ALU.add))
            then(dve.tensor_tensor(r_shift[:], r_end[:], r_tiles[:], ALU.subtract))
            then(dve.scalar_tensor_tensor(r_shift[:], r_shift[:], float(P), r_excl[:, :, 0], ALU.mult, ALU.subtract))
            then(dve.tensor_tensor(r_work[:], ranks, r_excl[:], ALU.add))
            then(dve.tensor_tensor(r_work[:], r_work[:], r_shift[:].unsqueeze(2).broadcast_to(by_expert), ALU.add))
            then(dve.tensor_tensor(r_work[:], r_work[:], chosen[:], ALU.mult))
            then(dve.tensor_reduce(r_slot[:], r_work[:].rearrange("p e t -> p t e"), AX_X, ALU.add))
            dve.tensor_copy(slot_of[:], r_slot[:]).then_inc(slots_ready, 1)
            by_slot = [P, SLOT_TILES, EXPERTS - 1]
            then(dve.tensor_tensor(r_ended[:], iota_tile[:].unsqueeze(2).broadcast_to(by_slot),
                                   r_end[:, 0:EXPERTS - 1].unsqueeze(1).broadcast_to(by_slot), ALU.is_ge))
            then(dve.tensor_reduce(r_expert[:], r_ended[:], AX_X, ALU.add))
            dve.tensor_copy(expert_of[:], r_expert[:]).then_inc(slots_ready, 1)
            dve.wait_ge(slots_ready, 2)

            def expert(s):
                return dve.value_load(expert_of[0:1, bass.ds(s, 1)], min_val=0, max_val=EXPERTS - 1)

            def rows_in(s):
                turn_bank = turn.banks[0]
                dve.wait_ge(slot_inT_full, s + 1)
                for k in range(KH):
                    ins = dve.tensor_scalar(slot_inT[:, k], turn_bank[:, k * P:(k + 1) * P], column("ln2_g", k),
                                            column("ln2_b", k), ALU.mult, ALU.add)
                ins.then_inc(slot_inT_ready, 1)

            def mid_half(s):
                dve.wait_ge(mid_full[1], s + 1)
                dve.tensor_copy(mid[:, 512:], proj.banks[1][:]).then_inc(mid_ready[1], 1)

            def biases(s):
                dve.tensor_copy(b1_now[:], columns[:, bass.ds(expert(s) * KF + COLUMNS["b1"], KF)]).then_inc(b1_ready, 1)

            def midT_half(s):
                dve.wait_ge(midT_full[1], s + 1)
                dve.wait_ge(b1_ready, s + 1)
                for n in range(KF // 2):
                    c = KF // 2 + n
                    ins = dve.tensor_scalar(midT[:, c], score.banks[1][:, n * P:(n + 1) * P], b1_now[:, c:c + 1], 0.0,
                                            ALU.add, ALU.max)
                ins.then_inc(midT_ready[1], 1)

            def rows_out(s, first=False):
                dve.wait_ge(slot_out_full, s + 1)
                if first:
                    dve.wait_ge(b2_landed, 16)
                else:
                    dve.wait_ge(slot_out_stored, s * 16)
                e = expert(s)
                dve.tensor_tensor(slot_out[:], mix.banks[0][:, 0:HID], b2_rows[:, bass.ds(e * HID, HID)], ALU.add)\
                    .then_inc(slot_out_ready, 1)

            rows_in(0)
            biases(0)
            mid_half(0)
            rows_in(1)
            midT_half(0)
            dve.wait_ge(midT_ready[0], 1)
            dve.wait_ge(midT_ready[1], 1)
            biases(1)
            mid_half(1)
            rows_out(0, True)
            with dve.Fori(1, SLOT_TILES - 1) as s:
                rows_in(s + 1)
                midT_half(s)
                dve.wait_ge(midT_ready[0], s + 1)
                dve.wait_ge(midT_ready[1], s + 1)
                biases(s + 1)
                mid_half(s + 1)
                rows_out(s)
            midT_half(SLOT_TILES - 1)
            rows_out(SLOT_TILES - 1)
            for n in range(4):
                dve.wait_ge(gather_landed[n], 64)
                part_of = gathered[:, 4 * n:4 * n + 4]
                dve.tensor_tensor(part_of, part_of, residual_all[:, 4 * n:4 * n + 4], ALU.add).then_inc(sums_ready, 1)

        @block.scalar
        def _(act):
            def from_ring(ring, part, step, dst, src):
                ring.wait_full(act, part, step)
                act.activation(dst, src(ring.bank(part, step)), ACT.Copy).then_inc(ring.emptied_of(part, step), 1)

            def exps(n, tile, b, part, step, scale):
                score.wait_read(act, part, step)
                act.activation(of_image(tile, b), of_image(tile, b), ACT.Exp, scale=scale).then_inc(softmax[n]["exp"], 1)

            def even_image_blocks(part, steps, dst):
                for g, step in enumerate(steps):
                    turn.wait_full(act, part, step)
                    src = turn.bank(part, step)[0:TOKENS].rearrange("p (h t) -> p h t", h=8)
                    act.activation(dst[0:TOKENS, 8 * g:8 * g + 8, 0:TOKENS], src, ACT.Copy)\
                        .then_inc(turn.emptied_of(part, step), 1)

            def qk_out(part, m):
                step = f"qk{m}"
                proj.wait_full(act, part, step)
                bank = proj.bank(part, step)
                for half in range(2):
                    rows = slice(half * D1, (half + 1) * D1)
                    act.activation(q_diag[rows, m, :, rows],
                                   bank[rows, 0:GT].rearrange("p (b t) -> p b t", b=GROUP), ACT.Copy)
                act.activation(kT[:, m], bank[:, GT:2 * GT], ACT.Copy).then_inc(proj.emptied_of(part, step), 1)

            def columns_of_fo(part, j):
                turn.wait_full(act, part, f"foT{j}")
                bank = turn.bank(part, f"foT{j}")
                for k in range(KH):
                    ins = act.activation(foT[:, j, k], bank[:, k * P:(k + 1) * P], ACT.Identity, bias=column("bv", k))
                ins.then_inc(turn.emptied_of(part, f"foT{j}"), 1)

            def work(part):
                c, f, n = part.c, part.f, part.n
                if c is not None:
                    for j in range(2):
                        from_ring(turn, part, f"zT{j}", zT[:, :, j * P:(j + 1) * P],
                                  lambda bank: bank[:, 0:HID].rearrange("p (k t) -> p k t", k=KH))
                    qk_out(part, 0)
                    qk_out(part, 2)
                if f is not None:
                    turn.wait_full(act, part, "hnT")
                    for k in range(KH):
                        ins = act.activation(hnT[:, k], turn.bank(part, "hnT")[:, k * GT:(k + 1) * GT], ACT.Identity,
                                             scale=column("ln1_g", k), bias=column("ln1_b", k))
                    ins.then_inc(turn.emptied_of(part, "hnT"), 1)
                    proj.wait_full(act, part, "fqk0")
                    bank = proj.bank(part, "fqk0")
                    act.activation(fq[:, 0], bank[:, 0:GT], ACT.Identity, bias=column("bq", 0))
                    act.activation(fkT[:, 0], bank[:, GT:2 * GT], ACT.Identity, bias=column("bk", 0))\
                        .then_inc(proj.emptied_of(part, "fqk0"), 1)
                    for j in range(2):
                        from_ring(proj, part, f"fv{j}", fv[:, j], lambda bank: bank[:, 0:HID])
                if c is not None:
                    qk_out(part, 4)
                if f is not None:
                    exps("f", fprobs, 0, part, "fs0", D2 ** -0.5)
                if c is not None:
                    qk_out(part, 6)
                if f is not None:
                    exps("f", fprobs, 1, part, "fs1", D2 ** -0.5)
                if c is not None:
                    from_ring(proj, part, "v00", v_sb[:, 0, 0:512], lambda bank: bank[:])
                if f is not None:
                    even_image_blocks(part, ("fpT00", "fpT01"), fprobsT)
                    exps("f", fprobs, 2, part, "fs2", D2 ** -0.5)
                    exps("f", fprobs, 3, part, "fs3", D2 ** -0.5)
                if c is not None:
                    exps("c", probs, 0, part, "s0", D1 ** -0.5)
                    exps("c", probs, 1, part, "s1", D1 ** -0.5)
                if f is not None:
                    from_ring(mix, part, "fo0", fo[:, 0], lambda bank: bank[:, 0:HID])
                if c is not None:
                    from_ring(proj, part, "v10", v_sb[:, 1, 0:512], lambda bank: bank[:])
                if f is not None:
                    even_image_blocks(part, ("fpT10", "fpT11"), fprobsT)
                if c is not None:
                    exps("c", probs, 2, part, "s2", D1 ** -0.5)
                    exps("c", probs, 3, part, "s3", D1 ** -0.5)
                    even_image_blocks(part, ("pT00", "pT01"), probsT)
                if f is not None:
                    columns_of_fo(part, 0)
                    columns_of_fo(part, 1)
                if c is not None:
                    from_ring(mix, part, "o00", o_sb[:, 0, 0:512], lambda bank: bank[:])
                    even_image_blocks(part, ("pT10", "pT11"), probsT)
                    from_ring(turn, part, "oT00", oT[:, 0:KO // 2], lambda bank: bank[:].rearrange("p (a t) -> p a t", t=P))
                    from_ring(mix, part, "o10", o_sb[:, 1, 0:512], lambda bank: bank[:])
                if f is not None:
                    turn.wait_full(act, part, "z2T")
                    for k in range(KH):
                        ins = act.activation(hn2T[:, k], turn.bank(part, "z2T")[:, k * GT:(k + 1) * GT], ACT.Identity,
                                             scale=column("ln2_g", k), bias=column("ln2_b", k))
                    ins.then_inc(turn.emptied_of(part, "z2T"), 1)
                if c is not None:
                    if f is not None:
                        act.wait_ge(residual_kept, per_group(2, f, 2))
                    act.activation(h2[:], h1[:], ACT.Copy).then_inc(h1_moved, 1)
                    from_ring(turn, part, "oT10", oT[:, 0:KO // 2], lambda bank: bank[:].rearrange("p (a t) -> p a t", t=P))
                if n is not None:
                    if c is not None:
                        act.wait_ge(h1_moved, per_group(1, c, 1))
                    from_ring(proj, part, "tok0", h1[:, 0], lambda bank: bank[:, 0:HID])

            act.wait_ge(qkv_landed, 32)
            by_kind = qkv_raw[:].rearrange("p k (m c s) -> p k s m c", m=PAIRS, s=3)
            act.activation(qk_w[:, 1, :, 0], by_kind[:, 1, 0], ACT.Copy)
            act.activation(qk_w[:, 1, :, 1], by_kind[:, 1, 1], ACT.Copy).then_inc(qkv_sorted, 1)
            act.wait_ge(columns_ready, 1)
            work(Part("start"))
            act.wait_ge(blocks_zero, 2)
            work(Part("first"))
            act.wait_ge(slots_cleared, 16)
            with act.Fori(0, GROUPS - 2) as i:
                work(Part("body", i))
            work(Part("final"))
            work(Part("last"))

            def mid_half(s):
                act.wait_ge(mid_full[0], s + 1)
                act.activation(mid[:, 0:512], proj.banks[0][:], ACT.Copy).then_inc(mid_ready[0], 1)

            def midT_half(s):
                act.wait_ge(midT_full[0], s + 1)
                act.wait_ge(b1_ready, s + 1)
                for c in range(KF // 2):
                    ins = act.activation(midT[:, c], score.banks[0][:, c * P:(c + 1) * P], ACT.Relu, bias=b1_now[:, c:c + 1])
                ins.then_inc(midT_ready[0], 1)

            mid_half(0)
            with act.Fori(0, SLOT_TILES - 1) as s:
                midT_half(s)
                mid_half(s + 1)
            midT_half(SLOT_TILES - 1)

        @block.tensor
        def _(pe):
            def group_of(out_ap, pairs):
                for n, (lhsT, rhs) in enumerate(pairs):
                    ins = pe.matmul(out_ap, lhsT, rhs, start=(n == 0), stop=(n == len(pairs) - 1))
                return ins

            def tokens(part):
                pe.wait_ge(features_landed, per_group(FEATURE_LOADS, part.n, FEATURE_LOADS))
                for j in range(2):
                    proj.wait_empty(pe, part, f"tok{j}")
                    group_of(proj.bank(part, f"tok{j}")[:, 0:HID],
                             [(by_token[:, j * P:(j + 1) * P, 2 * t], tok_w_sb[:, t]) for t in range(FT)])\
                        .then_inc(proj.full_of(part, f"tok{j}"), 1)

            def turn_rows(part, step, rows, ready, count):
                turn.wait_empty(pe, part, step)
                for j in range(2):
                    pe.wait_ge(ready, per_group(2, count, j + 1))
                    for k in range(KH):
                        ins = pe.transpose(turn.bank(part, step)[:, k * GT + j * P:k * GT + (j + 1) * P],
                                           rows[:, j, k * P:(k + 1) * P], identity[:])
                ins.then_inc(turn.full_of(part, step), 1)

            def turn_z(part):
                for j in range(2):
                    pe.wait_ge(norm["a"]["out"], per_group(2, part.c, j + 1))
                    turn.wait_empty(pe, part, f"zT{j}")
                    for k in range(KH):
                        ins = pe.transpose(turn.bank(part, f"zT{j}")[:, k * P:(k + 1) * P], z[:, j, k * P:(k + 1) * P],
                                           identity[:])
                    ins.then_inc(turn.full_of(part, f"zT{j}"), 1)

            def qk(part, m):
                step = f"qk{m}"
                if m == 0:
                    for j in range(2):
                        turn.wait_read(pe, part, f"zT{j}")
                proj.wait_empty(pe, part, step)
                for s in range(2):
                    ins = group_of(proj.bank(part, step)[:, s * GT:(s + 1) * GT],
                                   [(qk_w[:, k, m, s], zT[:, k]) for k in range(KH)])
                ins.then_inc(proj.full_of(part, step), 1)

            def values(part, j):
                for half in range(2):
                    step = f"v{j}{half}"
                    proj.wait_empty(pe, part, step)
                    for k in range(KH):
                        ins = pe.matmul(proj.bank(part, step)[:], zT[:, k, j * P:(j + 1) * P],
                                        v_w[:, k, half * 512:(half + 1) * 512], start=(k == 0), stop=(k == KH - 1))
                    ins.then_inc(proj.full_of(part, step), 1)

            def scores(part, b):
                if b == 0:
                    proj.wait_read(pe, part, "qk6")
                    proj.wait_read(pe, part, "qk7")
                step = f"s{b}"
                score.wait_empty(pe, part, step)
                for m in range(PAIRS):
                    ins = pe.matmul(score.bank(part, step)[:, m * TOKENS:(m + 1) * TOKENS], q_diag[:, m, b],
                                    kT[:, m, b * TOKENS:(b + 1) * TOKENS], start=True, stop=True)
                ins.then_inc(score.full_of(part, step), 1)

            def fscores(part, b):
                pe.wait_ge(fq_heads_ready, per_group(GROUP * KH, part.f, KH * (b + 1)))
                step = f"fs{b}"
                score.wait_empty(pe, part, step)
                for m in range(KH):
                    for g in range(PAIRS // KH):
                        at = (m * PAIRS // KH + g) * TOKENS
                        ins = pe.matmul(score.bank(part, step)[:, at:at + TOKENS],
                                        fq_heads[:, b % 2, m, 2 * g:2 * g + 2].rearrange("p h t -> p (h t)"),
                                        fkT[:, m, b * TOKENS:(b + 1) * TOKENS], start=True, stop=True)
                ins.then_inc(score.full_of(part, step), 1)

            def turn_probs(part, n, tile, j, group):
                pe.wait_ge(softmax[n]["probs"], per_group(GROUP, group, 2 * j + 2))
                for g in range(2):
                    step = f"{'f' if n == 'f' else ''}pT{j}{g}"
                    turn.wait_empty(pe, part, step)
                    for q in range(4):
                        m = 4 * g + q
                        ins = pe.transpose(turn.bank(part, step)[:, q * P:(q + 1) * P],
                                           tile[:, j, m].rearrange("p b t -> p (b t)"), identity[:])
                    ins.then_inc(turn.full_of(part, step), 1)

            def mix_values(part, j):
                for g in range(2):
                    turn.wait_read(pe, part, f"pT{j}{g}")
                    proj.wait_read(pe, part, f"v{j}{g}")
                for g in range(2):
                    step = f"o{j}{g}"
                    mix.wait_empty(pe, part, step)
                    for n in range(8):
                        h = 8 * g + n
                        ins = pe.matmul(mix.bank(part, step)[:, n * D1:(n + 1) * D1], probsT[:, h],
                                        v_sb[:, j, h * D1:(h + 1) * D1], start=True, stop=True)
                    ins.then_inc(mix.full_of(part, step), 1)

            def fmix_values(part, j):
                for g in range(2):
                    turn.wait_read(pe, part, f"fpT{j}{g}")
                proj.wait_read(pe, part, f"fv{j}")
                step = f"fo{j}"
                mix.wait_empty(pe, part, step)
                for h in range(HEADS):
                    ins = pe.matmul(mix.bank(part, step)[:, h * D2:(h + 1) * D2], fprobsT[:, h],
                                    fv[:, j, h * D2:(h + 1) * D2], start=True, stop=True)
                ins.then_inc(mix.full_of(part, step), 1)

            def turn_fo(part, j):
                mix.wait_read(pe, part, f"fo{j}")
                turn.wait_empty(pe, part, f"foT{j}")
                for k in range(KH):
                    ins = pe.transpose(turn.bank(part, f"foT{j}")[:, k * P:(k + 1) * P], fo[:, j, k * P:(k + 1) * P],
                                       identity[:])
                ins.then_inc(turn.full_of(part, f"foT{j}"), 1)

            def fout(part, j):
                turn.wait_read(pe, part, f"foT{j}")
                proj.wait_empty(pe, part, f"wo{j}")
                group_of(proj.bank(part, f"wo{j}")[:, 0:HID], [(foT[:, j, k], wo_sb[:, k]) for k in range(KH)])\
                    .then_inc(proj.full_of(part, f"wo{j}"), 1)

            def turn_o(part, j):
                for g in range(2):
                    mix.wait_read(pe, part, f"o{j}{g}")
                    turn.wait_empty(pe, part, f"oT{j}{g}")
                    for q in range(KO // 2):
                        at = (g * KO // 2 + q) * P
                        ins = pe.transpose(turn.bank(part, f"oT{j}{g}")[:, q * P:(q + 1) * P], o_sb[:, j, at:at + P],
                                           identity[:])
                    ins.then_inc(turn.full_of(part, f"oT{j}{g}"), 1)

            def out_proj(part, j):
                for g in range(2):
                    turn.wait_read(pe, part, f"oT{j}{g}")
                proj.wait_empty(pe, part, f"out{j}")
                for k in range(KO):
                    ins = pe.matmul(proj.bank(part, f"out{j}")[:, 0:HID], oT[:, k], out_w_sb[:, k],
                                    start=(k == 0), stop=(k == KO - 1))
                    if (j, k) == (1, 0):
                        ins.then_inc(image_used, 1)
                ins.then_inc(proj.full_of(part, f"out{j}"), 1)

            def fqkv(part):
                turn.wait_read(pe, part, "hnT")
                for m in range(KH):
                    proj.wait_empty(pe, part, f"fqk{m}")
                    for s, weights in enumerate((wq_sb, wk_sb)):
                        ins = group_of(proj.bank(part, f"fqk{m}")[:, s * GT:(s + 1) * GT],
                                       [(weights[:, k, m * P:(m + 1) * P], hnT[:, k]) for k in range(KH)])
                    ins.then_inc(proj.full_of(part, f"fqk{m}"), 1)
                for j in range(2):
                    proj.wait_empty(pe, part, f"fv{j}")
                    group_of(proj.bank(part, f"fv{j}")[:, 0:HID],
                             [(hnT[:, k, j * P:(j + 1) * P], wv_sb[:, k]) for k in range(KH)])\
                        .then_inc(proj.full_of(part, f"fv{j}"), 1)

            def gate(part):
                turn.wait_read(pe, part, "z2T")
                for j in range(2):
                    proj.wait_empty(pe, part, f"gate{j}")
                    group_of(proj.bank(part, f"gate{j}")[:, 0:EXPERTS],
                             [(hn2T[:, k, j * P:(j + 1) * P], gate_w_sb[:, k]) for k in range(KH)])\
                        .then_inc(proj.full_of(part, f"gate{j}"), 1)

            def work(part):
                c, f, n = part.c, part.f, part.n
                if c is not None:
                    turn_z(part)
                    for m in range(3):
                        qk(part, m)
                if f is not None:
                    turn_rows(part, "hnT", z1, norm["1"]["out"], f)
                if c is not None:
                    qk(part, 3)
                if f is not None:
                    fqkv(part)
                if c is not None:
                    qk(part, 4)
                if f is not None:
                    for m in range(KH):
                        proj.wait_read(pe, part, f"fqk{m}")
                    fscores(part, 0)
                if c is not None:
                    qk(part, 5)
                if f is not None:
                    fscores(part, 1)
                if c is not None:
                    qk(part, 6)
                    qk(part, 7)
                    values(part, 0)
                if f is not None:
                    turn_probs(part, "f", fprobs, 0, f)
                    fscores(part, 2)
                    fscores(part, 3)
                if c is not None:
                    scores(part, 0)
                    scores(part, 1)
                if f is not None:
                    fmix_values(part, 0)
                if c is not None:
                    values(part, 1)
                if f is not None:
                    turn_probs(part, "f", fprobs, 1, f)
                if c is not None:
                    scores(part, 2)
                    scores(part, 3)
                if f is not None:
                    fmix_values(part, 1)
                if c is not None:
                    turn_probs(part, "c", probs, 0, c)
                if f is not None:
                    turn_fo(part, 0)
                    turn_fo(part, 1)
                if c is not None:
                    mix_values(part, 0)
                if f is not None:
                    fout(part, 0)
                    fout(part, 1)
                if c is not None:
                    turn_probs(part, "c", probs, 1, c)
                    turn_o(part, 0)
                    mix_values(part, 1)
                if f is not None:
                    turn_rows(part, "z2T", z2, norm["2"]["out"], f)
                if c is not None:
                    if part.kind == "first":
                        pe.wait_ge(out_w_landed, 16)
                    out_proj(part, 0)
                if f is not None:
                    gate(part)
                if c is not None:
                    turn_o(part, 1)
                if n is not None:
                    tokens(part)
                if c is not None:
                    out_proj(part, 1)

            pe.wait_ge(consts_made, 3)
            pe.wait_ge(vectors_landed, 128)
            pe.transpose(turn.banks[0][:, 0:ROWS], vector_rows[:], identity[0:ROWS, 0:ROWS]).then_inc(columns_turned, 1)
            pe.wait_ge(columns_ready, 1)
            pe.wait_ge(tok_w_landed, 16)
            work(Part("start"))
            pe.sem_inc(image_used, 1)
            pe.wait_ge(qkv_sorted, 3)
            work(Part("first"))
            pe.wait_ge(small_w_landed, 80)
            with pe.Fori(0, GROUPS - 2) as i:
                work(Part("body", i))
            work(Part("final"))
            work(Part("last"))

            pe.wait_ge(chosen_ready, 1)
            flat = chosen[:].rearrange("p e t -> p (e t)")
            pe.matmul(score.banks[0][:, 0:EXPERTS * TILES], earlier[:], flat, start=True, stop=True).then_inc(ranks_ready, 1)
            pe.matmul(score.banks[1][:, 0:EXPERTS * TILES], ones[:], flat, start=True, stop=True).then_inc(ranks_ready, 1)
            pe.wait_ge(slots_ready, 2)

            def expert(s):
                return pe.value_load(expert_of[0:1, bass.ds(s, 1)], min_val=0, max_val=EXPERTS - 1)

            def turn_in(s, buffer, pair):
                pe.wait_ge(slot_in_landed[buffer], (pair + 1) * 16)
                for k in range(KH):
                    ins = pe.transpose(turn.banks[0][:, k * P:(k + 1) * P], slot_in[:, buffer, k * P:(k + 1) * P],
                                       identity[:])
                ins.then_inc(slot_inT_full, 1)

            def up(s, e):
                pe.wait_ge(experts_resident, e + 1)
                pe.wait_ge(slot_inT_ready, s + 1)
                for half in range(2):
                    group_of(proj.banks[half][:],
                             [(slot_inT[:, k], expert_w[:, bass.ds(e, 1), k * FFN + half * 512:k * FFN + (half + 1) * 512])
                              for k in range(KH)]).then_inc(mid_full[half], 1)

            def turn_mid(s):
                for half in range(2):
                    pe.wait_ge(mid_ready[half], s + 1)
                    for n in range(KF // 2):
                        at = (half * KF // 2 + n) * P
                        ins = pe.transpose(score.banks[half][:, n * P:(n + 1) * P], mid[:, at:at + P], identity[:])
                    ins.then_inc(midT_full[half], 1)

            def down(s, e):
                for half in range(2):
                    pe.wait_ge(midT_ready[half], s + 1)
                group_of(mix.banks[0][:, 0:HID],
                         [(midT[:, c], expert_w[:, bass.ds(e, 1), KH * FFN + c * HID:KH * FFN + (c + 1) * HID])
                          for c in range(KF)]).then_inc(slot_out_full, 1)

            turn_in(0, 0, 0)
            up(0, expert(0))
            with pe.Fori(0, (SLOT_TILES - 1) // 2) as pair:
                for half in range(2):
                    s = 2 * pair + half
                    turn_in(s + 1, 1 - half, pair + half)
                    turn_mid(s)
                    up(s + 1, expert(s + 1))
                    down(s, expert(s))
            turn_mid(SLOT_TILES - 1)
            down(SLOT_TILES - 1, expert(SLOT_TILES - 1))


_INS = ["x", "L0_tok_W", "L0_attn_W_qkv", "L0_attn_W_out", "L0_ffn_ln1_g", "L0_ffn_ln1_b", "L0_ffn_ln2_g",
        "L0_ffn_ln2_b", "L0_ffn_wq", "L0_ffn_bq", "L0_ffn_wk", "L0_ffn_bk", "L0_ffn_wv", "L0_ffn_bv", "L0_ffn_wo",
        "L0_ffn_bo", "L0_ffn_gate_w", "L0_ffn_gate_b", "L0_ffn_w1", "L0_ffn_b1", "L0_ffn_w2", "L0_ffn_b2"]


def kernel(**inputs):
    import numpy as np
    import concourse.bacc as bacc
    from concourse.bass_utils import run_bass_kernel_spmd

    nc = bacc.Bacc("TRN2", target_bir_lowering=False, num_devices=1)
    arrays, args = {}, []
    for name in _INS:
        a = np.ascontiguousarray(inputs[name])
        arrays[f"in_{name}"] = a
        args.append(nc.dram_tensor(f"in_{name}", a.shape, mybir.dt.from_np(a.dtype), kind="ExternalInput").ap())
    args.append(nc.dram_tensor("tower_out", (IMAGES, TOKENS, HID), F32, kind="ExternalOutput").ap())
    vit_tower(nc, *args)
    r = run_bass_kernel_spmd(nc, [arrays], core_ids=[0])
    return r.results[0]["tower_out"]
```

```python
from contextlib import ExitStack

import concourse.bass as bass
from concourse import mybir
from concourse.alu_op_type import AluOpType as ALU

F32 = mybir.dt.float32
I32 = mybir.dt.int32
U32 = mybir.dt.uint32
ACT = mybir.ActivationFunctionType
AX_X = mybir.AxisListType.X

P = 128
IMAGES, CHANNELS, IMG, PATCH = 32, 3, 128, 16
GRID = IMG // PATCH
TOKENS = GRID * GRID
HID = 256
KH = HID // P
FEATURES = CHANNELS * PATCH * PATCH
FT = FEATURES // P
GROUP = 4
GROUPS = IMAGES // GROUP
GT = GROUP * TOKENS
FOLD = FEATURES // TOKENS
BANDS = GROUP * CHANNELS * GRID
FEATURE_LOADS = 16 * 2 * GROUP * CHANNELS
TILES = IMAGES * TOKENS // P
HEADS, D1, D2 = 16, 64, 16
PAIRS = HEADS // 2
HD = HEADS * D1
KO = HD // P
EXPERTS, FFN = 8, 1024
KF = FFN // P
SLOT_TILES = TILES + EXPERTS - 1
EPS = 1e-5
KEPT = 2 * HID + 1
NOBODY = 2 * IMAGES * TOKENS
COLUMNS = {"ln1_g": 0, "ln1_b": 2, "ln2_g": 4, "ln2_b": 6, "bq": 8, "bk": 10, "bv": 12, "b1": 14}
ROWS = 14 + EXPERTS * KF


class Part:

    PHASES = {"start": "n", "first": "cn", "body": "cfn", "final": "cf", "last": "f"}

    def __init__(self, kind, i=None):
        self.kind = kind
        self.i = i
        phases = self.PHASES[kind]
        at = {"start": -1, "first": 0, "body": None if i is None else i + 1, "final": GROUPS - 1, "last": GROUPS}[kind]
        self.c = at if "c" in phases else None
        self.f = at - 1 if "f" in phases else None
        self.n = at + 1 if "n" in phases else None


class Ring:

    def __init__(self, nc, ctx, name, uses):
        self.banks = [ctx.enter_context(nc.psum_tensor(f"{name}{b}", [P, 512], F32)) for b in range(2)]
        self.full = [ctx.enter_context(nc.semaphore(f"{name}{b}_full")) for b in range(2)]
        self.emptied = [ctx.enter_context(nc.semaphore(f"{name}{b}_emptied")) for b in range(2)]
        self.uses = {kind: [u for u in uses if u[1] in phases] for kind, phases in Part.PHASES.items()}
        assert all(len(u) % 2 == 0 for u in self.uses.values())

    def _where(self, kind, step):
        return [u[0] for u in self.uses[kind]].index(step)

    def _count(self, kind, b, n=None):
        mine = self.uses[kind][:n][b::2] if n is not None else self.uses[kind][b::2]
        return len(mine), sum(u[2] for u in mine)

    def _before(self, part, b, which):
        start, first, body, final = (self._count(kind, b)[which] for kind in ("start", "first", "body", "final"))
        return {
            "start": 0,
            "first": start,
            "body": start + first + (0 if part.i is None else part.i) * body,
            "final": start + first + (GROUPS - 2) * body,
            "last": start + first + (GROUPS - 2) * body + final,
        }[part.kind]

    def _at(self, part, step, which, inclusive):
        n = self._where(part.kind, step)
        return self._before(part, n % 2, which) + self._count(part.kind, n % 2, n + inclusive)[which]

    def bank(self, part, step):
        return self.banks[self._where(part.kind, step) % 2]

    def wait_empty(self, engine, part, step):
        value = self._at(part, step, 1, 0)
        if not (isinstance(value, int) and value == 0):
            engine.wait_ge(self.emptied[self._where(part.kind, step) % 2], value)

    def wait_full(self, engine, part, step):
        engine.wait_ge(self.full[self._where(part.kind, step) % 2], self._at(part, step, 0, 1))

    def wait_read(self, engine, part, step):
        engine.wait_ge(self.emptied[self._where(part.kind, step) % 2], self._at(part, step, 1, 1))

    def wait_read_in_previous(self, engine, part, step):
        tails = set()
        for kind in {"first": ("start",), "body": ("first", "body"), "final": ("body",), "last": ("final",)}[part.kind]:
            n = self._where(kind, step)
            tails.add((n % 2, self._count(kind, n % 2)[1] - self._count(kind, n % 2, n + 1)[1]))
        (b, tail), = tails
        engine.wait_ge(self.emptied[b], self._before(part, b, 1) - tail)

    def full_of(self, part, step):
        return self.full[self._where(part.kind, step) % 2]

    def emptied_of(self, part, step):
        return self.emptied[self._where(part.kind, step) % 2]


def vit_tower(nc, x, tok_w, qkv_w, out_w, ln1_g, ln1_b, ln2_g, ln2_b, wq, bq, wk, bk, wv, bv, wo, bo,
              gate_w, gate_b, w1, b1, w2, b2, out):
    ctx = ExitStack()
    with ctx:
        def sb(name, shape, dt=F32, where=ctx):
            return where.enter_context(nc.sbuf_tensor(name, shape, dt))

        def sem(name):
            return ctx.enter_context(nc.semaphore(name))

        slot_rows = nc.dram_tensor("slot_rows", [SLOT_TILES * P, KEPT], F32, kind="Internal").ap()

        kept_all = sb("kept_all", [P, TILES, KEPT])
        logits_all = sb("logits_all", [P, TILES, EXPERTS])
        bo_row = sb("bo_row", [P, HID])
        gate_b_row = sb("gate_b_row", [P, EXPERTS])
        columns = sb("columns", [P, ROWS])
        identity = sb("identity", [P, P])
        earlier = sb("earlier", [P, P])
        ones = sb("ones", [P, P])
        head_mask = sb("head_mask", [P, HEADS // KH])
        minus_half = sb("minus_half", [P, 2])
        eps = sb("eps", [P, 2])
        wait_carrier = sb("wait_carrier", [P, 1])
        wait_carrier_pool = sb("wait_carrier_pool", [P, 4])
        iota_expert = sb("iota_expert", [P, EXPERTS])
        iota_tile = sb("iota_tile", [P, SLOT_TILES])
        iota_128 = sb("iota_128", [P, TILES])
        slot_of = sb("slot_of", [P, TILES], U32)
        expert_of = sb("expert_of", [P, SLOT_TILES], I32)

        def column(name, k, rows=slice(0, P)):
            return columns[rows, COLUMNS[name] + k:COLUMNS[name] + k + 1]

        tower = ExitStack()
        images_here = ExitStack()
        image_rows = sb("image_rows", [BANDS, PATCH, IMG], where=images_here)
        patch_rows = sb("patch_rows", [BANDS, GRID, PATCH, PATCH], where=images_here)
        images_here.close()
        oT = sb("oT", [P, 2, KO, P], where=tower)
        probs = sb("probs", [P, 2, PAIRS, 2, TOKENS], where=tower)
        features = sb("features", [P, GROUP * FEATURES + 2], where=tower)
        v_sb = sb("v_sb", [P, 2, HD], where=tower)
        tok_w_sb = sb("tok_w_sb", [P, FT, HID], where=tower)
        qk_w = sb("qk_w", [P, KH, PAIRS, 2, P], where=tower)
        v_w = sb("v_w", [P, KH, HD], where=tower)
        out_w_sb = sb("out_w_sb", [P, KO, HID], where=tower)
        raw_here = ExitStack()
        qkv_raw = sb("qkv_raw", [P, KH, 3 * HD], where=raw_here)
        raw_here.close()
        qkT = sb("qkT", [P, PAIRS, 2, GT], where=tower)
        probsT = sb("probsT", [P, HEADS, P], where=tower)
        h1 = sb("h1", [P, 2, HID], where=tower)
        z = sb("z", [P, 2, HID], where=tower)
        zT = sb("zT", [P, KH, GT], where=tower)
        wq_sb = sb("wq_sb", [P, KH, HID], where=tower)
        wk_sb = sb("wk_sb", [P, KH, HID], where=tower)
        wv_sb = sb("wv_sb", [P, KH, HID], where=tower)
        fq = sb("fq", [P, KH, GT], where=tower)
        h2 = sb("h2", [P, 2, HID], where=tower)
        fprobs = sb("fprobs", [P, 2, PAIRS, 2, TOKENS], where=tower)
        empty_here = ExitStack()
        empty_row = sb("empty_row", [P, KEPT], where=empty_here)
        empty_here.close()
        fq_heads = sb("fq_heads", [P, 2, KH, HEADS // KH, TOKENS], where=tower)
        wo_sb = sb("wo_sb", [P, KH, HID], where=tower)
        gate_w_sb = sb("gate_w_sb", [P, KH, EXPERTS], where=tower)
        u = sb("u", [P, 2, HID], where=tower)
        u_bo = sb("u_bo", [P, 2, HID], where=tower)
        z1 = sb("z1", [P, 2, HID], where=tower)
        z2 = z1
        hnT = sb("hnT", [P, KH, GT], where=tower)
        hn2T = hnT
        fkT = sb("fkT", [P, KH, GT], where=tower)
        fv_heads = sb("fv_heads", [P, 2, HEADS, 2 * D2], where=tower)
        fprobsT = sb("fprobsT", [P, HEADS, P], where=tower)
        vectors_here = ExitStack()
        vector_rows = sb("vector_rows", [ROWS, P], where=vectors_here)
        vectors_here.close()
        foT = sb("foT", [P, 2, KH, P], where=tower)
        x2 = sb("x2", [P, 2, HID], where=tower)
        small = {}
        for n in ("a", "u", "1", "2"):
            small[n] = (sb(f"stats_{n}", [P, 2, 6], where=tower), sb(f"moments_{n}", [P, 2, 2], where=tower),
                        sb(f"var_eps_{n}", [P, 2], where=tower), sb(f"rstd_{n}", [P, 2], where=tower))
        soft = {}
        for n in ("c", "f"):
            soft[n] = tuple(sb(f"{what}_{n}", [P, GROUP, PAIRS], where=tower) for what in ("max", "sum", "rsum"))
        tower.close()

        experts = ExitStack()
        expert_w = sb("expert_w", [P, EXPERTS, KH * FFN + KF * HID], where=experts)
        b2_rows = sb("b2_rows", [P, EXPERTS * HID], where=experts)
        slot_in = sb("slot_in", [P, 2, KEPT], where=experts)
        slot_base = sb("slot_base", [P, 2, HID], where=experts)
        slot_token = sb("slot_token", [P, 2], U32, where=experts)
        slot_inT = sb("slot_inT", [P, KH, P], where=experts)
        w1_now = sb("w1_now", [P, 2, KH, FFN], where=experts)
        midT = sb("midT", [P, 2, KF, P], where=experts)
        b1_now = sb("b1_now", [P, 2, KF], where=experts)
        slot_out = sb("slot_out", [P, HID], where=experts)
        r_max = sb("r_max", [P, TILES], where=experts)
        r_cand = sb("r_cand", [P, TILES, EXPERTS], where=experts)
        r_first = sb("r_first", [P, TILES], where=experts)
        chosen = sb("chosen", [P, EXPERTS, TILES], where=experts)
        r_incl = sb("r_incl", [P, EXPERTS, TILES], where=experts)
        r_excl = sb("r_excl", [P, EXPERTS, TILES], where=experts)
        r_work = sb("r_work", [P, EXPERTS, TILES], where=experts)
        r_count = sb("r_count", [P, EXPERTS], where=experts)
        r_tiles = sb("r_tiles", [P, EXPERTS], where=experts)
        r_end = sb("r_end", [P, EXPERTS], where=experts)
        r_shift = sb("r_shift", [P, EXPERTS], where=experts)
        r_slot = sb("r_slot", [P, TILES], where=experts)
        r_ended = sb("r_ended", [P, SLOT_TILES, EXPERTS - 1], where=experts)
        r_expert = sb("r_expert", [P, SLOT_TILES], where=experts)
        experts.close()

        turn = Ring(nc, ctx, "turn", [
            ("hnT", "f", 1), ("fpT00", "f", 2), ("fpT01", "f", 2),
            ("fpT10", "f", 2), ("fpT11", "f", 2), ("pT00", "c", 2), ("pT01", "c", 2), ("pT10", "c", 2),
            ("pT11", "c", 2), ("z2T", "f", 1), ("zT0", "n", 1), ("zT1", "n", 1)])
        proj = Ring(nc, ctx, "proj", [
            ("qk0", "c", 1), ("qk1", "c", 1), ("qk2", "c", 1), ("qk3", "c", 1), ("qk4", "c", 1), ("fqk0", "f", 1),
            ("fqk1", "f", 1), ("fv0", "f", 1), ("fv1", "f", 1), ("qk5", "c", 1), ("qk6", "c", 1), ("qk7", "c", 1),
            ("v00", "c", 1), ("v01", "c", 1), ("v10", "c", 1), ("v11", "c", 1), ("wo0", "f", 1), ("wo1", "f", 1), ("out0", "c", 1),
            ("tok0", "n", 1), ("tok1", "n", 1), ("out1", "c", 1)])
        score = Ring(nc, ctx, "score", [("fs0", "f", 1), ("fs1", "f", 1), ("fs2", "f", 1), ("fs3", "f", 1),
                                        ("s0", "c", 1), ("s1", "c", 1), ("s2", "c", 1), ("s3", "c", 1)])
        mix = Ring(nc, ctx, "mix", [("fo0", "f", 1), ("fo1", "f", 1), ("o00", "c", 1), ("o01", "c", 1),
                                    ("o10", "c", 1), ("o11", "c", 1), ("gate0", "f", 1), ("gate1", "f", 1)])

        consts_made = sem("consts_made")
        vectors_landed = sem("vectors_landed")
        columns_ready = sem("columns_ready")
        columns_turned = sem("columns_turned")
        rows_landed = sem("rows_landed")
        tok_w_landed = sem("tok_w_landed")
        qkv_landed = sem("qkv_landed")
        qkv_sorted = sem("qkv_sorted")
        out_w_landed = sem("out_w_landed")
        small_w_landed = sem("small_w_landed")
        image_landed = sem("image_landed")
        image_used = sem("image_used")
        blocks_zero = sem("blocks_zero")
        fv_heads_zero = sem("fv_heads_zero")
        patch_rows_ready = sem("patch_rows_ready")
        features_landed = sem("features_landed")
        last_image_landed = sem("last_image_landed")
        slots_cleared = sem("slots_cleared")
        norm = {n: {s: sem(f"norm_{n}_{s}") for s in ("stats", "moments", "var_eps", "rstd", "out")}
                for n in ("a", "u", "1", "2")}
        u_bo_ready = sem("u_bo_ready")
        h1_moved = sem("h1_moved")
        fq_heads_ready = sem("fq_heads_ready")
        softmax = {n: {s: sem(f"softmax_{n}_{s}") for s in ("max", "exp", "sum", "rsum", "probs")}
                   for n in ("c", "f")}
        residual_kept = sem("residual_kept")
        normed_kept = sem("normed_kept")
        route = sem("route")
        chosen_ready = sem("chosen_ready")
        ranks_ready = sem("ranks_ready")
        slots_ready = sem("slots_ready")
        scattered = sem("scattered")
        expert_landed = [sem(f"expert_landed{e}") for e in range(EXPERTS)]
        b2_landed = sem("b2_landed")
        experts_resident = sem("experts_resident")
        slot_in_landed = [sem(f"slot_in_landed{n}") for n in range(2)]
        slot_inT_full = sem("slot_inT_full")
        slot_inT_ready = sem("slot_inT_ready")
        w1_copied = [sem(f"w1_copied{n}") for n in range(2)]
        midT_full = [sem(f"midT_full{n}") for n in range(2)]
        midT_ready = [sem(f"midT_ready{n}") for n in range(2)]
        b1_ready = sem("b1_ready")
        slot_out_full = sem("slot_out_full")
        slot_out_ready = sem("slot_out_ready")
        slot_out_stored = sem("slot_out_stored")
        slot_based = sem("slot_based")
        empty_row_made = sem("empty_row_made")

        out_rows = out.rearrange("b t h -> (b t) h")
        expert_w1 = expert_w[:, :, 0:KH * FFN].rearrange("p e (k f) -> p e k f", k=KH)
        expert_w2 = expert_w[:, :, KH * FFN:].rearrange("p e (c h) -> p e c h", c=KF)
        by_token = features[:, 1:1 + GROUP * FEATURES].rearrange("p (n a) -> p n a", a=FOLD)

        def patches_of(n, half):
            at = n * PATCH * PATCH + 1 - half
            return (features[half * TOKENS:(half + 1) * TOKENS, at:at + PATCH * PATCH],
                    patch_rows[n * GRID:(n + 1) * GRID].rearrange("p j r w -> p j (r w)"))

        def of_image(tile, b):
            return tile[:, b // 2, :, b % 2]

        def per_group(per, group, done):
            return group * per + done

        def features_of(group):
            return per_group(FEATURE_LOADS, group, FEATURE_LOADS - FEATURE_LOADS // GROUP)

        block = ctx.enter_context(nc.Block())

        @block.sync
        def _(sync):
            def load_images(g):
                src = x[bass.ds(g * GROUP, GROUP)].rearrange("b c (i r) w -> (b c i) r w", i=GRID)
                sync.dma_start(image_rows[:], src).then_inc(image_landed, 16)

            def load_features(g, channels):
                sync.wait_ge(patch_rows_ready, g + 1)
                for n in channels:
                    for half in range(2):
                        sync.dma_start(*patches_of(n, half)).then_inc(features_landed, 16)

            load_images(0)
            sync.dma_start(tok_w_sb[:], tok_w.rearrange("(t p) h -> p t h", p=P)).then_inc(tok_w_landed, 16)
            for k in range(KH):
                sync.dma_start(qkv_raw[:, k, :], qkv_w[k * P:(k + 1) * P, :]).then_inc(qkv_landed, 16)
            load_features(0, range((GROUP - 1) * CHANNELS))
            sync.dma_start(out_w_sb[:], out_w.rearrange("(c p) h -> p c h", p=P)).then_inc(out_w_landed, 16)
            def next_group(g):
                sync.wait_ge(image_used, g)
                load_images(g)
                load_features(g, range(GROUP * CHANNELS))

            next_group(1)
            sync.wait_ge(empty_row_made, 2)
            sync.dma_start(slot_rows.rearrange("(s p) h -> p s h", p=P),
                           empty_row[:].unsqueeze(1).broadcast_to([P, SLOT_TILES, KEPT])).then_inc(slots_cleared, 16)
            with sync.Fori(2, GROUPS) as g:
                next_group(g)

            def load_expert(e):
                sync.dma_start(expert_w1[:, e], w1[e].rearrange("(k p) f -> p k f", p=P))\
                    .then_inc(expert_landed[e], 16)
                sync.dma_start(expert_w2[:, e], w2[e].rearrange("(c p) h -> p c h", p=P))\
                    .then_inc(expert_landed[e], 16)

            proj.wait_read(sync, Part("final"), "out1")
            for e in range(EXPERTS - 2):
                load_expert(e)
            score.wait_full(sync, Part("last"), "fs3")
            load_expert(EXPERTS - 2)
            for j in range(2):
                mix.wait_read(sync, Part("last"), f"gate{j}")
            sync.wait_ge(normed_kept, TILES)

            def load_slot_tile(s, buffer):
                sync.dma_start(slot_in[:, buffer], slot_rows[bass.ds(s * P, P), :]).then_inc(slot_in_landed[buffer], 16)

            def next_slot_tile(s, buffer):
                sync.wait_ge(slot_inT_full, s + 1)
                sync.wait_ge(slot_based, s + 1)
                load_slot_tile(s + 2, buffer)

            sync.wait_ge(scattered, 16 * TILES)
            load_slot_tile(0, 0)
            sync.dma_start(b2_rows[:], b2.rearrange("e h -> (e h)").partition_broadcast(P)).then_inc(b2_landed, 16)
            load_slot_tile(1, 1)
            load_expert(EXPERTS - 1)
            with sync.Fori(0, (SLOT_TILES - 3) // 2) as pair:
                next_slot_tile(2 * pair, 0)
                next_slot_tile(2 * pair + 1, 1)
            next_slot_tile(SLOT_TILES - 3, 0)

        @block.gpsimd
        def _(pool):
            pool.memset(identity[:], 0.0)
            pool.memset(earlier[:], 1.0)
            pool.memset(head_mask[:], 1.0)
            pool.memset(minus_half[:], -0.5)
            pool.memset(eps[:], EPS)
            pool.memset(ones[:], 1.0)
            pool.iota(iota_expert[:], pattern=[[1, EXPERTS]], base=0, channel_multiplier=0,
                      allow_small_or_imprecise_dtypes=True)
            pool.iota(iota_tile[:], pattern=[[1, SLOT_TILES]], base=0, channel_multiplier=0,
                      allow_small_or_imprecise_dtypes=True)
            pool.iota(iota_128[:], pattern=[[P, TILES]], base=0, channel_multiplier=0,
                      allow_small_or_imprecise_dtypes=True).then_inc(consts_made, 1)
            pool.wait_ge(consts_made, 1)
            pool.affine_select(out=identity[:], in_=identity[:], compare_op=ALU.not_equal, fill=1.0, base=0,
                               pattern=[[-1, P]], channel_multiplier=1)
            pool.affine_select(out=earlier[:], in_=earlier[:], compare_op=ALU.is_gt, fill=0.0, base=0,
                               pattern=[[1, P]], channel_multiplier=-1)
            pool.affine_select(out=head_mask[:], in_=head_mask[:], compare_op=ALU.is_ge, fill=0.0, base=0,
                               pattern=[[-D2, HEADS // KH]], channel_multiplier=1).then_inc(consts_made, 1)
            pool.wait_ge(consts_made, 2)
            pool.affine_select(out=head_mask[:], in_=head_mask[:], compare_op=ALU.is_ge, fill=0.0, base=D2 - 1,
                               pattern=[[D2, HEADS // KH]], channel_multiplier=-1).then_inc(consts_made, 1)
            pool.iota(kept_all[:, :, 2 * HID], pattern=[[P, TILES]], base=0, channel_multiplier=1,
                      allow_small_or_imprecise_dtypes=True)
            pool.memset(empty_row[:, 0:2 * HID], 0.0).then_inc(empty_row_made, 1)
            pool.memset(empty_row[:, 2 * HID:], float(NOBODY)).then_inc(empty_row_made, 1)
            pool.memset(fprobsT[:], 0.0)
            pool.memset(fv_heads[:], 0.0).then_inc(fv_heads_zero, 1)

            pool.wait_ge(patch_rows_ready, 1)
            for n in range((GROUP - 1) * CHANNELS, GROUP * CHANNELS):
                for half in range(2):
                    pool.dma_start(*patches_of(n, half)).then_inc(last_image_landed, 16)

            pool.wait_ge(qkv_landed, 32)
            by_kind = qkv_raw[:].rearrange("p k (m c s) -> p k s m c", m=PAIRS, s=3)
            pool.tensor_copy(v_w[:, 1].rearrange("p (m c) -> p m c", m=PAIRS), by_kind[:, 1, 2]).then_inc(qkv_sorted, 1)

            pool.wait_ge(qkv_sorted, 3)
            pool.memset(probsT[:], 0.0).then_inc(blocks_zero, 1)

            def root(n, group):
                _, moments, var_eps, rstd = small[n]
                pool.wait_ge(norm[n]["moments"], per_group(2, group, 2))
                pool.tensor_tensor(var_eps[:], moments[:, :, 1], eps[:], ALU.add).then_inc(norm[n]["var_eps"], 1)
                pool.wait_ge(norm[n]["var_eps"], per_group(1, group, 1))
                pool.tensor_tensor(rstd[:], var_eps[:], minus_half[:], ALU.pow).then_inc(norm[n]["rstd"], 1)

            def scale_probs(n, tile, b, group):
                pool.wait_ge(softmax[n]["rsum"], per_group(GROUP, group, b + 1))
                rows = of_image(tile, b)
                pool.tensor_tensor(rows, rows, soft[n][2][:, b].unsqueeze(2).broadcast_to([P, PAIRS, TOKENS]),
                                   ALU.mult).then_inc(softmax[n]["probs"], 1)

            def bo_to_u(part):
                pool.wait_ge(norm["u"]["out"], per_group(2, part.f, 2))
                for j in range(2):
                    pool.tensor_tensor(u_bo[:, j], u[:, j], bo_row[:], ALU.add).then_inc(u_bo_ready, 1)

            def queries_by_head(part, images):
                for m in range(KH):
                    proj.wait_read(pool, part, f"fqk{m}")
                for b in images:
                    if b >= 2:
                        score.wait_full(pool, part, f"fs{b - 2}")
                    for m in range(KH):
                        pool.tensor_tensor(
                            fq_heads[:, b % 2, m],
                            fq[:, m, b * TOKENS:(b + 1) * TOKENS].unsqueeze(1).broadcast_to([P, HEADS // KH, TOKENS]),
                            head_mask[:].unsqueeze(2).broadcast_to([P, HEADS // KH, TOKENS]),
                            ALU.mult).then_inc(fq_heads_ready, 1)

            def keep_residual(part):
                for j in range(2):
                    proj.wait_read(pool, part, f"wo{j}")
                    pool.tensor_tensor(kept_all[:, bass.ds(part.f * 2 + j, 1), HID:2 * HID], h2[:, j:j + 1], x2[:, j:j + 1],
                                       ALU.add)\
                        .then_inc(residual_kept, 1)

            def keep_normed(part):
                for j in range(2):
                    pool.wait_ge(norm["2"]["out"], per_group(2, part.f, j + 1))
                    pool.tensor_copy(kept_all[:, bass.ds(part.f * 2 + j, 1), 0:HID], z2[:, j:j + 1]).then_inc(normed_kept, 1)

            def work(part):
                c, f, n = part.c, part.f, part.n
                if f is not None:
                    root("u", f)
                    root("1", f)
                    queries_by_head(part, (0, 1, 2))
                    if c is None:
                        queries_by_head(part, (3,))
                    scale_probs("f", fprobs, 0, f)
                    if c is not None:
                        queries_by_head(part, (3,))
                    scale_probs("f", fprobs, 1, f)
                    if c is not None:
                        bo_to_u(part)
                    scale_probs("f", fprobs, 2, f)
                    scale_probs("f", fprobs, 3, f)
                    if c is None:
                        bo_to_u(part)
                if c is not None:
                    for b in range(GROUP):
                        scale_probs("c", probs, b, c)
                if f is not None:
                    root("2", f)
                    keep_residual(part)
                    keep_normed(part)
                if n is not None:
                    root("a", n)

            work(Part("start"))
            for name, src in (("ln1_g", ln1_g), ("ln1_b", ln1_b), ("ln2_g", ln2_g), ("ln2_b", ln2_b),
                              ("bq", bq), ("bk", bk), ("bv", bv)):
                pool.dma_start(vector_rows[COLUMNS[name]:COLUMNS[name] + KH],
                               src.rearrange("(k p) -> k p", p=P)).then_inc(vectors_landed, 16)
            pool.dma_start(vector_rows[COLUMNS["b1"]:ROWS], b1.rearrange("e (c p) -> (e c) p", p=P))\
                .then_inc(vectors_landed, 16)
            pool.dma_start(bo_row[:], bo.partition_broadcast(P)).then_inc(rows_landed, 16)
            pool.dma_start(gate_b_row[:], gate_b.partition_broadcast(P)).then_inc(rows_landed, 16)
            for tile, src in ((wq_sb, wq), (wk_sb, wk), (wv_sb, wv), (wo_sb, wo), (gate_w_sb, gate_w)):
                pool.dma_start(tile[:], src.rearrange("(k p) h -> p k h", p=P)).then_inc(small_w_landed, 16)
            pool.wait_ge(rows_landed, 32)
            work(Part("first"))
            pool.wait_ge(slots_cleared, 16)
            with pool.Fori(0, GROUPS - 2) as i:
                work(Part("body", i))
            work(Part("final"))
            work(Part("last"))

            for e in range(EXPERTS - 1):
                pool.wait_ge(expert_landed[e], 32)
                pool.sem_inc(experts_resident, 1)

            pool.wait_ge(slots_ready, 1)
            pool.wait_ge(normed_kept, TILES)
            pool.wait_ge(residual_kept, TILES)
            for t in range(TILES):
                to_slots = bass.IndirectOffsetOnAxis(ap=slot_of[:, t:t + 1], axis=0)
                pool.indirect_dma_start(out=slot_rows, out_offset=to_slots, in_=kept_all[:, t], in_offset=None)\
                    .then_inc(scattered, 16)
            pool.wait_ge(slots_ready, 2)

            def base(s, buffer, pair):
                e = pool.value_load(expert_of[0:1, bass.ds(s, 1)], min_val=0, max_val=EXPERTS - 1)
                pool.wait_ge(slot_in_landed[buffer], (pair + 1) * 16)
                pool.tensor_tensor(slot_base[:, buffer], slot_in[:, buffer, HID:2 * HID], b2_rows[:, bass.ds(e * HID, HID)],
                                   ALU.add)
                pool.tensor_copy(slot_token[:, buffer:buffer + 1], slot_in[:, buffer, 2 * HID:]).then_inc(slot_based, 1)

            def store(s, buffer):
                pool.wait_ge(slot_based, s + 1)
                pool.wait_ge(slot_out_ready, s + 1)
                pool.tensor_tensor(wait_carrier_pool[:, buffer:buffer + 1], eps[:, 0:1], eps[:, 0:1], ALU.add)
                pool.indirect_dma_start(out=out_rows,
                                        out_offset=bass.IndirectOffsetOnAxis(ap=slot_token[:, buffer:buffer + 1], axis=0),
                                        in_=slot_out[:], in_offset=None, bounds_check=IMAGES * TOKENS - 1,
                                        oob_is_err=False).then_inc(slot_out_stored, 16)

            pool.wait_ge(b2_landed, 16)
            base(0, 0, 0)
            pool.wait_ge(expert_landed[EXPERTS - 1], 32)
            pool.sem_inc(experts_resident, 1)
            base(1, 1, 0)
            store(0, 0)

            def slot_tile(s, buffer, pair):
                pool.wait_ge(slot_out_stored, 16 * s)
                pool.tensor_tensor(wait_carrier_pool[:, 2 + buffer:3 + buffer], eps[:, 0:1], eps[:, 0:1], ALU.add)
                base(s + 1, 1 - buffer, pair + 1)
                store(s, buffer)

            with pool.Fori(0, (SLOT_TILES - 3) // 2) as pair:
                slot_tile(2 * pair + 1, 1, pair)
                slot_tile(2 * pair + 2, 0, pair)
            slot_tile(SLOT_TILES - 2, 1, (SLOT_TILES - 3) // 2)
            store(SLOT_TILES - 1, 0)
            pool.wait_ge(slot_out_stored, 16 * SLOT_TILES)

        @block.vector
        def _(dve):
            def stats(n, tile, j):
                dve.bn_stats(small[n][0][:, j], tile[:, j]).then_inc(norm[n]["stats"], 1)

            def moments(n, group):
                dve.wait_ge(norm[n]["stats"], per_group(2, group, 2))
                dve.memset(wait_carrier[:], 0.0)
                for j in range(2):
                    dve.bn_aggr(small[n][1][:, j], small[n][0][:, j]).then_inc(norm[n]["moments"], 1)

            def normed(n, dst, src, group):
                dve.wait_ge(norm[n]["rstd"], per_group(1, group, 1))
                for j in range(2):
                    dve.tensor_scalar(dst[:, j], src[:, j], small[n][1][:, j, 0:1], small[n][3][:, j:j + 1],
                                      ALU.subtract, ALU.mult).then_inc(norm[n]["out"], 1)

            def minus_max(n, tile, b, part, step, group):
                score.wait_full(dve, part, step)
                scores = score.bank(part, step)[:].rearrange("p (h t) -> p h t", h=PAIRS)
                dve.tensor_reduce(soft[n][0][:, b], scores, AX_X, ALU.max).then_inc(softmax[n]["max"], 1)
                dve.wait_ge(softmax[n]["max"], per_group(GROUP, group, b + 1))
                dve.tensor_tensor(of_image(tile, b), scores,
                                  soft[n][0][:, b].unsqueeze(2).broadcast_to([P, PAIRS, TOKENS]), ALU.subtract)\
                    .then_inc(score.emptied_of(part, step), 1)

            def row_sums(n, tile, b, group):
                dve.wait_ge(softmax[n]["exp"], per_group(GROUP, group, b + 1))
                dve.tensor_reduce(soft[n][1][:, b], of_image(tile, b), AX_X, ALU.add)\
                    .then_inc(softmax[n]["sum"], 1)
                dve.wait_ge(softmax[n]["sum"], per_group(GROUP, group, b + 1))
                dve.reciprocal(soft[n][2][:, b], soft[n][1][:, b]).then_inc(softmax[n]["rsum"], 1)

            def from_ring(ring, part, step, dst, src):
                ring.wait_full(dve, part, step)
                dve.tensor_copy(dst, src(ring.bank(part, step))).then_inc(ring.emptied_of(part, step), 1)

            def odd_image_blocks(part, steps, dst):
                for g, step in enumerate(steps):
                    turn.wait_full(dve, part, step)
                    src = turn.bank(part, step)[TOKENS:P].rearrange("p (h t) -> p h t", h=8)
                    dve.tensor_copy(dst[TOKENS:P, 8 * g:8 * g + 8, TOKENS:P], src)\
                        .then_inc(turn.emptied_of(part, step), 1)

            def by_patch(g):
                dve.wait_ge(image_landed, 16 * (g + 1))
                dve.tensor_copy(patch_rows[:], image_rows[:].rearrange("p r (j w) -> p j r w", j=GRID))\
                    .then_inc(patch_rows_ready, 1)

            def qk_out(part, m):
                step = f"qk{m}"
                proj.wait_full(dve, part, step)
                bank = proj.bank(part, step)
                dve.tensor_copy(qkT[:, m].rearrange("p s t -> p (s t)"), bank[:]).then_inc(proj.emptied_of(part, step), 1)

            def h2_out(part, j):
                proj.wait_full(dve, part, f"out{j}")
                dve.wait_ge(h1_moved, per_group(1, part.c, 1))
                dve.tensor_tensor(h2[:, j], proj.bank(part, f"out{j}")[:, 0:HID], h2[:, j], ALU.add)\
                    .then_inc(proj.emptied_of(part, f"out{j}"), 1)

            def logits_out(part):
                for j in range(2):
                    mix.wait_full(dve, part, f"gate{j}")
                    dve.tensor_tensor(logits_all[:, bass.ds(part.f * 2 + j, 1)],
                                      mix.bank(part, f"gate{j}")[:, 0:EXPERTS].unsqueeze(1),
                                      gate_b_row[:].unsqueeze(1), ALU.add)\
                        .then_inc(mix.emptied_of(part, f"gate{j}"), 1)

            def work(part):
                c, f, n = part.c, part.f, part.n
                if f is not None:
                    proj.wait_read_in_previous(dve, part, "out1")
                    for j in range(2):
                        stats("u", h2, j)
                    moments("u", f)
                    normed("u", u, h2, f)
                    dve.wait_ge(norm["u"]["out"], per_group(2, f, 2))
                    for j in range(2):
                        stats("1", u, j)
                    moments("1", f)
                if c is not None:
                    qk_out(part, 1)
                if f is not None:
                    normed("1", z1, u, f)
                if c is not None:
                    if n is not None:
                        by_patch(n)
                    qk_out(part, 3)
                if f is not None:
                    proj.wait_full(dve, part, "fqk1")
                    bank = proj.bank(part, "fqk1")
                    dve.tensor_scalar(fq[:, 1], bank[:, 0:GT], column("bq", 1), None, ALU.add)
                    dve.tensor_scalar(fkT[:, 1], bank[:, GT:2 * GT], column("bk", 1), None, ALU.add)\
                        .then_inc(proj.emptied_of(part, "fqk1"), 1)
                if c is not None:
                    qk_out(part, 5)
                if f is not None:
                    minus_max("f", fprobs, 0, part, "fs0", f)
                if f is not None:
                    minus_max("f", fprobs, 1, part, "fs1", f)
                    row_sums("f", fprobs, 0, f)
                if c is not None:
                    qk_out(part, 7)
                if f is not None:
                    row_sums("f", fprobs, 1, f)
                if c is not None:
                    from_ring(proj, part, "v01", v_sb[:, 0, 512:], lambda bank: bank[:])
                if f is not None:
                    if c is not None:
                        odd_image_blocks(part, ("fpT00", "fpT01"), fprobsT)
                    minus_max("f", fprobs, 2, part, "fs2", f)
                    minus_max("f", fprobs, 3, part, "fs3", f)
                    if c is None:
                        odd_image_blocks(part, ("fpT00", "fpT01"), fprobsT)
                if c is not None:
                    if n is not None:
                        dve.wait_ge(features_landed, features_of(n))
                    minus_max("c", probs, 0, part, "s0", c)
                    minus_max("c", probs, 1, part, "s1", c)
                if f is not None:
                    row_sums("f", fprobs, 2, f)
                    row_sums("f", fprobs, 3, f)
                if c is not None:
                    row_sums("c", probs, 0, c)
                    row_sums("c", probs, 1, c)
                    from_ring(proj, part, "v11", v_sb[:, 1, 512:], lambda bank: bank[:])
                if f is not None:
                    odd_image_blocks(part, ("fpT10", "fpT11"), fprobsT)
                if c is not None:
                    minus_max("c", probs, 2, part, "s2", c)
                    minus_max("c", probs, 3, part, "s3", c)
                if f is not None:
                    mix.wait_full(dve, part, "fo1")
                    for k in range(KH):
                        ins = dve.tensor_scalar(foT[:, 1, k], mix.bank(part, "fo1")[:, k * P:(k + 1) * P], column("bv", k),
                                                None, ALU.add)
                    ins.then_inc(mix.emptied_of(part, "fo1"), 1)
                if c is not None:
                    odd_image_blocks(part, ("pT00", "pT01"), probsT)
                    row_sums("c", probs, 2, c)
                    row_sums("c", probs, 3, c)
                if f is not None:
                    for j in range(2):
                        dve.wait_ge(u_bo_ready, per_group(2, f, j + 1))
                        proj.wait_full(dve, part, f"wo{j}")
                        dve.tensor_tensor(x2[:, j], proj.bank(part, f"wo{j}")[:, 0:HID], u_bo[:, j], ALU.add)\
                            .then_inc(proj.emptied_of(part, f"wo{j}"), 1)
                    for j in range(2):
                        proj.wait_read(dve, part, f"wo{j}")
                        stats("2", x2, j)
                    moments("2", f)
                if c is not None:
                    from_ring(mix, part, "o01", oT[:, 0, KO // 2:], lambda bank: bank[:].rearrange("p (a t) -> p a t", t=P))
                    odd_image_blocks(part, ("pT10", "pT11"), probsT)
                if f is not None:
                    normed("2", z2, x2, f)
                if c is not None:
                    h2_out(part, 0)
                    from_ring(mix, part, "o11", oT[:, 1, KO // 2:], lambda bank: bank[:].rearrange("p (a t) -> p a t", t=P))
                if n is not None:
                    if c is not None:
                        dve.wait_ge(h1_moved, per_group(1, c, 1))
                    from_ring(proj, part, "tok1", h1[:, 1], lambda bank: bank[:, 0:HID])
                    for j in range(2):
                        proj.wait_read(dve, part, f"tok{j}")
                        stats("a", h1, j)
                    moments("a", n)
                    normed("a", z, h1, n)
                if c is not None:
                    h2_out(part, 1)
                if f is not None:
                    logits_out(part)

            by_patch(0)
            dve.wait_ge(qkv_landed, 32)
            by_kind = qkv_raw[:].rearrange("p k (m c s) -> p k s m c", m=PAIRS, s=3)
            for s in range(2):
                dve.tensor_copy(qk_w[:, 0, :, s], by_kind[:, 0, s])
            dve.tensor_copy(v_w[:, 0].rearrange("p (m c) -> p m c", m=PAIRS), by_kind[:, 0, 2]).then_inc(qkv_sorted, 1)
            work(Part("start"))
            dve.wait_ge(blocks_zero, 1)
            work(Part("first"))
            dve.wait_ge(columns_turned, 1)
            dve.tensor_copy(columns[:], turn.banks[0][:, 0:ROWS]).then_inc(columns_ready, 1)
            dve.wait_ge(rows_landed, 32)
            dve.wait_ge(columns_ready, 1)
            with dve.Fori(0, GROUPS - 2) as i:
                work(Part("body", i))
            work(Part("final"))
            work(Part("last"))

            steps = [0]

            def then(ins):
                steps[0] += 1
                ins.then_inc(route, 1)
                dve.wait_ge(route, steps[0])

            last = Part("last")
            for j in range(2):
                mix.wait_read(dve, last, f"gate{j}")
            dve.wait_ge(normed_kept, TILES)
            by_tile = [P, TILES, EXPERTS]
            ranks_of = iota_expert[:].unsqueeze(1).broadcast_to(by_tile)
            then(dve.tensor_reduce(r_max[:], logits_all[:], AX_X, ALU.max))
            then(dve.tensor_tensor(r_cand[:], logits_all[:], r_max[:].unsqueeze(2).broadcast_to(by_tile), ALU.is_lt))
            then(dve.scalar_tensor_tensor(r_cand[:], r_cand[:], float(EXPERTS), ranks_of, ALU.mult, ALU.add))
            then(dve.tensor_reduce(r_first[:], r_cand[:], AX_X, ALU.min))
            dve.tensor_tensor(chosen[:].rearrange("p e t -> p t e"), r_first[:].unsqueeze(2).broadcast_to(by_tile),
                              ranks_of, ALU.is_equal).then_inc(chosen_ready, 1)
            dve.wait_ge(ranks_ready, 2)
            ranks = score.banks[0][:, 0:EXPERTS * TILES].rearrange("p (e t) -> p e t", e=EXPERTS)
            totals = score.banks[1][:, 0:EXPERTS * TILES]
            totals_3d = totals.rearrange("p (e t) -> p e t", e=EXPERTS)
            flat = lambda tile: tile[:].rearrange("p e t -> p (e t)")
            then(dve.tensor_tensor_scan(flat(r_incl), ones[:], totals, 0.0, ALU.mult, ALU.add))
            then(dve.tensor_tensor(r_excl[:], r_incl[:], totals_3d, ALU.subtract))
            then(dve.tensor_reduce(r_count[:], totals_3d, AX_X, ALU.add))
            by_expert = [P, EXPERTS, TILES]
            then(dve.tensor_tensor(r_work[:], r_count[:].unsqueeze(2).broadcast_to(by_expert),
                                   iota_128[:].unsqueeze(1).broadcast_to(by_expert), ALU.is_gt))
            then(dve.tensor_reduce(r_tiles[:], r_work[:], AX_X, ALU.add))
            then(dve.tensor_tensor_scan(r_end[:], ones[:, 0:EXPERTS], r_tiles[:], 0.0, ALU.mult, ALU.add))
            then(dve.tensor_tensor(r_shift[:], r_end[:], r_tiles[:], ALU.subtract))
            then(dve.scalar_tensor_tensor(r_shift[:], r_shift[:], float(P), r_excl[:, :, 0], ALU.mult, ALU.subtract))
            then(dve.tensor_tensor(r_work[:], ranks, r_excl[:], ALU.add))
            then(dve.tensor_tensor(r_work[:], r_work[:], r_shift[:].unsqueeze(2).broadcast_to(by_expert), ALU.add))
            then(dve.tensor_tensor(r_work[:], r_work[:], chosen[:], ALU.mult))
            then(dve.tensor_reduce(r_slot[:], r_work[:].rearrange("p e t -> p t e"), AX_X, ALU.add))
            dve.tensor_copy(slot_of[:], r_slot[:]).then_inc(slots_ready, 1)
            by_slot = [P, SLOT_TILES, EXPERTS - 1]
            then(dve.tensor_tensor(r_ended[:], iota_tile[:].unsqueeze(2).broadcast_to(by_slot),
                                   r_end[:, 0:EXPERTS - 1].unsqueeze(1).broadcast_to(by_slot), ALU.is_ge))
            then(dve.tensor_reduce(r_expert[:], r_ended[:], AX_X, ALU.add))
            dve.tensor_copy(expert_of[:], r_expert[:]).then_inc(slots_ready, 1)
            dve.wait_ge(slots_ready, 2)

            def expert(s):
                return dve.value_load(expert_of[0:1, bass.ds(s, 1)], min_val=0, max_val=EXPERTS - 1)

            def rows_in(s):
                turn_bank = turn.banks[0]
                dve.wait_ge(slot_inT_full, s + 1)
                for k in range(KH):
                    ins = dve.tensor_scalar(slot_inT[:, k], turn_bank[:, k * P:(k + 1) * P], column("ln2_g", k),
                                            column("ln2_b", k), ALU.mult, ALU.add)
                ins.then_inc(slot_inT_ready, 1)

            def weights_in(s, buffer, first=False):
                e = expert(s)
                if not first:
                    dve.wait_ge(midT_full[1], s - 1)
                    for n in range(2):
                        dve.wait_ge(midT_ready[n], s - 1)
                dve.wait_ge(experts_resident, e + 1)
                dve.tensor_copy(w1_now[:, buffer:buffer + 1, 0], expert_w[:, bass.ds(e, 1), 0:FFN]).then_inc(w1_copied[0], 1)
                dve.tensor_copy(b1_now[:, buffer], columns[:, bass.ds(e * KF + COLUMNS["b1"], KF)]).then_inc(b1_ready, 1)

            def midT_half(s, buffer):
                dve.wait_ge(midT_full[1], s + 1)
                dve.wait_ge(b1_ready, s + 1)
                for n in range(KF // 2):
                    c = KF // 2 + n
                    ins = dve.tensor_scalar(midT[:, buffer, c], score.banks[1][:, n * P:(n + 1) * P],
                                            b1_now[:, buffer, c:c + 1], 0.0, ALU.add, ALU.max)
                ins.then_inc(midT_ready[1], 1)

            def rows_out(s, buffer, first=False):
                dve.wait_ge(slot_out_full, s + 1)
                dve.wait_ge(slot_based, s + 1)
                if not first:
                    dve.wait_ge(slot_out_stored, s * 16)
                dve.tensor_tensor(slot_out[:], mix.banks[0][:, 0:HID], slot_base[:, buffer], ALU.add)\
                    .then_inc(slot_out_ready, 1)

            def slot_tile(s, buffer, first=False, rows=True, weights=True):
                midT_half(s + 1, 1 - buffer)
                if rows:
                    rows_in(s + 2)
                rows_out(s, buffer, first)
                if weights:
                    weights_in(s + 3, 1 - buffer)

            rows_in(0)
            weights_in(0, 0, first=True)
            weights_in(1, 1, first=True)
            midT_half(0, 0)
            rows_in(1)
            weights_in(2, 0)
            slot_tile(0, 0, first=True)
            with dve.Fori(0, (SLOT_TILES - 5) // 2) as pair:
                slot_tile(2 * pair + 1, 1)
                slot_tile(2 * pair + 2, 0)
            slot_tile(SLOT_TILES - 4, 1)
            slot_tile(SLOT_TILES - 3, 0, weights=False)
            slot_tile(SLOT_TILES - 2, 1, rows=False, weights=False)
            rows_out(SLOT_TILES - 1, 0)

        @block.scalar
        def _(act):
            def from_ring(ring, part, step, dst, src):
                ring.wait_full(act, part, step)
                act.activation(dst, src(ring.bank(part, step)), ACT.Copy).then_inc(ring.emptied_of(part, step), 1)

            def exps(n, tile, b, part, step, scale):
                score.wait_read(act, part, step)
                act.activation(of_image(tile, b), of_image(tile, b), ACT.Exp, scale=scale).then_inc(softmax[n]["exp"], 1)

            def even_image_blocks(part, steps, dst):
                for g, step in enumerate(steps):
                    turn.wait_full(act, part, step)
                    src = turn.bank(part, step)[0:TOKENS].rearrange("p (h t) -> p h t", h=8)
                    act.activation(dst[0:TOKENS, 8 * g:8 * g + 8, 0:TOKENS], src, ACT.Copy)\
                        .then_inc(turn.emptied_of(part, step), 1)

            def qk_out(part, m):
                step = f"qk{m}"
                proj.wait_full(act, part, step)
                bank = proj.bank(part, step)
                act.activation(qkT[:, m].rearrange("p s t -> p (s t)"), bank[:], ACT.Copy)\
                    .then_inc(proj.emptied_of(part, step), 1)

            def work(part):
                c, f, n = part.c, part.f, part.n
                if c is not None:
                    qk_out(part, 0)
                    qk_out(part, 2)
                if f is not None:
                    turn.wait_full(act, part, "hnT")
                    for k in range(KH):
                        ins = act.activation(hnT[:, k], turn.bank(part, "hnT")[:, k * GT:(k + 1) * GT], ACT.Identity,
                                             scale=column("ln1_g", k), bias=column("ln1_b", k))
                    ins.then_inc(turn.emptied_of(part, "hnT"), 1)
                if c is not None:
                    qk_out(part, 4)
                if f is not None:
                    proj.wait_full(act, part, "fqk0")
                    bank = proj.bank(part, "fqk0")
                    act.activation(fq[:, 0], bank[:, 0:GT], ACT.Identity, bias=column("bq", 0))
                    act.activation(fkT[:, 0], bank[:, GT:2 * GT], ACT.Identity, bias=column("bk", 0))\
                        .then_inc(proj.emptied_of(part, "fqk0"), 1)
                    for j in range(2):
                        proj.wait_full(act, part, f"fv{j}")
                        by_pair = proj.bank(part, f"fv{j}")[:, 0:HID].rearrange("p (g s d) -> p g s d", s=2, d=D2)
                        pairs = fv_heads[:, j].rearrange("p (g s) (r d) -> p g s r d", s=2, d=D2)
                        for side in range(2):
                            ins = act.activation(pairs[:, :, side, side], by_pair[:, :, side], ACT.Copy)
                        ins.then_inc(proj.emptied_of(part, f"fv{j}"), 1)
                if f is not None:
                    exps("f", fprobs, 0, part, "fs0", D2 ** -0.5)
                if c is not None:
                    qk_out(part, 6)
                if f is not None:
                    exps("f", fprobs, 1, part, "fs1", D2 ** -0.5)
                if c is not None:
                    from_ring(proj, part, "v00", v_sb[:, 0, 0:512], lambda bank: bank[:])
                if f is not None:
                    if c is not None:
                        even_image_blocks(part, ("fpT00", "fpT01"), fprobsT)
                    exps("f", fprobs, 2, part, "fs2", D2 ** -0.5)
                    exps("f", fprobs, 3, part, "fs3", D2 ** -0.5)
                    if c is None:
                        even_image_blocks(part, ("fpT00", "fpT01"), fprobsT)
                if c is not None:
                    exps("c", probs, 0, part, "s0", D1 ** -0.5)
                    exps("c", probs, 1, part, "s1", D1 ** -0.5)
                if f is not None:
                    mix.wait_full(act, part, "fo0")
                    for k in range(KH):
                        ins = act.activation(foT[:, 0, k], mix.bank(part, "fo0")[:, k * P:(k + 1) * P], ACT.Identity,
                                             bias=column("bv", k))
                    ins.then_inc(mix.emptied_of(part, "fo0"), 1)
                if c is not None:
                    from_ring(proj, part, "v10", v_sb[:, 1, 0:512], lambda bank: bank[:])
                if f is not None:
                    even_image_blocks(part, ("fpT10", "fpT11"), fprobsT)
                if c is not None:
                    exps("c", probs, 2, part, "s2", D1 ** -0.5)
                    exps("c", probs, 3, part, "s3", D1 ** -0.5)
                    even_image_blocks(part, ("pT00", "pT01"), probsT)
                if c is not None:
                    from_ring(mix, part, "o00", oT[:, 0, 0:KO // 2], lambda bank: bank[:].rearrange("p (a t) -> p a t", t=P))
                    even_image_blocks(part, ("pT10", "pT11"), probsT)
                if f is not None:
                    turn.wait_full(act, part, "z2T")
                    for k in range(KH):
                        ins = act.activation(hn2T[:, k], turn.bank(part, "z2T")[:, k * GT:(k + 1) * GT], ACT.Identity,
                                             scale=column("ln2_g", k), bias=column("ln2_b", k))
                    ins.then_inc(turn.emptied_of(part, "z2T"), 1)
                if c is not None:
                    if f is not None:
                        act.wait_ge(residual_kept, per_group(2, f, 2))
                    act.activation(h2[:], h1[:], ACT.Copy).then_inc(h1_moved, 1)
                    from_ring(mix, part, "o10", oT[:, 1, 0:KO // 2], lambda bank: bank[:].rearrange("p (a t) -> p a t", t=P))
                if n is not None:
                    if c is not None:
                        act.wait_ge(h1_moved, per_group(1, c, 1))
                    from_ring(proj, part, "tok0", h1[:, 0], lambda bank: bank[:, 0:HID])
                    for j in range(2):
                        from_ring(turn, part, f"zT{j}", zT[:, :, j * P:(j + 1) * P],
                                  lambda bank: bank[:, 0:HID].rearrange("p (k t) -> p k t", k=KH))

            act.wait_ge(qkv_landed, 32)
            by_kind = qkv_raw[:].rearrange("p k (m c s) -> p k s m c", m=PAIRS, s=3)
            act.activation(qk_w[:, 1, :, 0], by_kind[:, 1, 0], ACT.Copy)
            act.activation(qk_w[:, 1, :, 1], by_kind[:, 1, 1], ACT.Copy).then_inc(qkv_sorted, 1)
            work(Part("start"))
            act.wait_ge(blocks_zero, 1)
            work(Part("first"))
            act.wait_ge(columns_ready, 1)
            act.wait_ge(fv_heads_zero, 1)
            with act.Fori(0, GROUPS - 2) as i:
                work(Part("body", i))
            work(Part("final"))
            work(Part("last"))

            act.wait_ge(slots_ready, 2)

            def weights_in(s, buffer, first=False):
                e = act.value_load(expert_of[0:1, bass.ds(s, 1)], min_val=0, max_val=EXPERTS - 1)
                if not first:
                    act.wait_ge(midT_full[1], s - 1)
                act.wait_ge(experts_resident, e + 1)
                act.activation(w1_now[:, buffer:buffer + 1, 1], expert_w[:, bass.ds(e, 1), FFN:2 * FFN], ACT.Copy)\
                    .then_inc(w1_copied[1], 1)

            def midT_half(s, buffer):
                act.wait_ge(midT_full[0], s + 1)
                act.wait_ge(b1_ready, s + 1)
                for c in range(KF // 2):
                    ins = act.activation(midT[:, buffer, c], score.banks[0][:, c * P:(c + 1) * P], ACT.Relu,
                                         bias=b1_now[:, buffer, c:c + 1])
                ins.then_inc(midT_ready[0], 1)

            weights_in(0, 0, first=True)
            weights_in(1, 1, first=True)
            midT_half(0, 0)
            weights_in(2, 0)
            with act.Fori(0, (SLOT_TILES - 3) // 2) as pair:
                midT_half(2 * pair + 1, 1)
                weights_in(2 * pair + 3, 1)
                midT_half(2 * pair + 2, 0)
                weights_in(2 * pair + 4, 0)
            midT_half(SLOT_TILES - 2, 1)
            midT_half(SLOT_TILES - 1, 0)

        @block.tensor
        def _(pe):
            def group_of(out_ap, pairs):
                for n, (lhsT, rhs) in enumerate(pairs):
                    ins = pe.matmul(out_ap, lhsT, rhs, start=(n == 0), stop=(n == len(pairs) - 1))
                return ins

            def carry_wait(bank):
                pe.matmul(bank[0:32, 0:2], identity[:, 0:32], identity[:, 0:2], start=True, stop=True)

            def tokens(part):
                if part.kind == "start":
                    pe.wait_ge(last_image_landed, FEATURE_LOADS // GROUP)
                pe.wait_ge(features_landed, features_of(part.n))
                for j in range(2):
                    proj.wait_empty(pe, part, f"tok{j}")
                    group_of(proj.bank(part, f"tok{j}")[:, 0:HID],
                             [(by_token[:, j * P:(j + 1) * P, 2 * t], tok_w_sb[:, t]) for t in range(FT)])\
                        .then_inc(proj.full_of(part, f"tok{j}"), 1)

            def turn_rows(part, step, rows, ready, count):
                turn.wait_empty(pe, part, step)
                for j in range(2):
                    pe.wait_ge(ready, per_group(2, count, j + 1))
                    for k in range(KH):
                        ins = pe.transpose(turn.bank(part, step)[:, k * GT + j * P:k * GT + (j + 1) * P],
                                           rows[:, j, k * P:(k + 1) * P], identity[:])
                ins.then_inc(turn.full_of(part, step), 1)

            def turn_z(part):
                for j in range(2):
                    pe.wait_ge(norm["a"]["out"], per_group(2, part.n, j + 1))
                    turn.wait_empty(pe, part, f"zT{j}")
                    for k in range(KH):
                        ins = pe.transpose(turn.bank(part, f"zT{j}")[:, k * P:(k + 1) * P], z[:, j, k * P:(k + 1) * P],
                                           identity[:])
                        if (j, k) == (0, 0):
                            ins.then_inc(image_used, 1)
                    ins.then_inc(turn.full_of(part, f"zT{j}"), 1)

            def qk(part, m):
                step = f"qk{m}"
                if m == 0:
                    for j in range(2):
                        turn.wait_read_in_previous(pe, part, f"zT{j}")
                proj.wait_empty(pe, part, step)
                for s in range(2):
                    ins = group_of(proj.bank(part, step)[:, s * GT:(s + 1) * GT],
                                   [(qk_w[:, k, m, s], zT[:, k]) for k in range(KH)])
                ins.then_inc(proj.full_of(part, step), 1)

            def values(part, j, half):
                step = f"v{j}{half}"
                proj.wait_empty(pe, part, step)
                group_of(proj.bank(part, step)[:],
                         [(zT[:, k, j * P:(j + 1) * P], v_w[:, k, half * 512:(half + 1) * 512]) for k in range(KH)])\
                    .then_inc(proj.full_of(part, step), 1)

            def scores(part, b):
                if b == 0:
                    proj.wait_read(pe, part, "qk6")
                    proj.wait_read(pe, part, "qk7")
                step = f"s{b}"
                score.wait_empty(pe, part, step)
                carry_wait(score.bank(part, step))
                for m in range(PAIRS):
                    for rows in (slice(0, D1), slice(D1, 2 * D1)):
                        ins = pe.matmul(score.bank(part, step)[rows, m * TOKENS:(m + 1) * TOKENS],
                                        qkT[rows, m, 0, b * TOKENS:(b + 1) * TOKENS],
                                        qkT[rows, m, 1, b * TOKENS:(b + 1) * TOKENS], start=True, stop=True)
                ins.then_inc(score.full_of(part, step), 1)

            def fscores(part, b):
                pe.wait_ge(fq_heads_ready, per_group(GROUP * KH, part.f, KH * (b + 1)))
                step = f"fs{b}"
                score.wait_empty(pe, part, step)
                for m in range(KH):
                    for g in range(PAIRS // KH):
                        at = (m * PAIRS // KH + g) * TOKENS
                        ins = pe.matmul(score.bank(part, step)[:, at:at + TOKENS],
                                        fq_heads[:, b % 2, m, 2 * g:2 * g + 2].rearrange("p h t -> p (h t)"),
                                        fkT[:, m, b * TOKENS:(b + 1) * TOKENS], start=True, stop=True)
                ins.then_inc(score.full_of(part, step), 1)

            def turn_probs(part, n, tile, j, group):
                pe.wait_ge(softmax[n]["probs"], per_group(GROUP, group, 2 * j + 2))
                for g in range(2):
                    step = f"{'f' if n == 'f' else ''}pT{j}{g}"
                    turn.wait_empty(pe, part, step)
                    for q in range(4):
                        m = 4 * g + q
                        ins = pe.transpose(turn.bank(part, step)[:, q * P:(q + 1) * P],
                                           tile[:, j, m].rearrange("p b t -> p (b t)"), identity[:])
                    ins.then_inc(turn.full_of(part, step), 1)

            def mix_values(part, j):
                for g in range(2):
                    turn.wait_read(pe, part, f"pT{j}{g}")
                    proj.wait_read(pe, part, f"v{j}{g}")
                for g in range(2):
                    step = f"o{j}{g}"
                    mix.wait_empty(pe, part, step)
                    for n in range(8):
                        h = 8 * g + n
                        rows = slice(h % 2 * D1, (h % 2 + 1) * D1)
                        ins = pe.matmul(mix.bank(part, step)[rows, n // 2 * P:(n // 2 + 1) * P],
                                        v_sb[:, j, h * D1:(h + 1) * D1], probsT[:, h], start=True, stop=True)
                    ins.then_inc(mix.full_of(part, step), 1)

            def fmix_values(part, j):
                for g in range(2):
                    turn.wait_read(pe, part, f"fpT{j}{g}")
                proj.wait_read(pe, part, f"fv{j}")
                step = f"fo{j}"
                mix.wait_empty(pe, part, step)
                for h in range(HEADS):
                    k, at = divmod(h * D2, P)
                    at -= at % (2 * D2)
                    ins = pe.matmul(mix.bank(part, step)[at:at + 2 * D2, k * P:(k + 1) * P], fv_heads[:, j, h],
                                    fprobsT[:, h], start=(h % 2 == 0), stop=(h % 2 == 1))
                ins.then_inc(mix.full_of(part, step), 1)

            def fout(part, j):
                mix.wait_read(pe, part, f"fo{j}")
                proj.wait_empty(pe, part, f"wo{j}")
                group_of(proj.bank(part, f"wo{j}")[:, 0:HID], [(foT[:, j, k], wo_sb[:, k]) for k in range(KH)])\
                    .then_inc(proj.full_of(part, f"wo{j}"), 1)

            def out_proj(part, j):
                for g in range(2):
                    mix.wait_read(pe, part, f"o{j}{g}")
                proj.wait_empty(pe, part, f"out{j}")
                group_of(proj.bank(part, f"out{j}")[:, 0:HID], [(oT[:, j, k], out_w_sb[:, k]) for k in range(KO)])\
                    .then_inc(proj.full_of(part, f"out{j}"), 1)

            def fqkv(part):
                turn.wait_read(pe, part, "hnT")
                for m in range(KH):
                    proj.wait_empty(pe, part, f"fqk{m}")
                    for s, weights in enumerate((wq_sb, wk_sb)):
                        ins = group_of(proj.bank(part, f"fqk{m}")[:, s * GT:(s + 1) * GT],
                                       [(weights[:, k, m * P:(m + 1) * P], hnT[:, k]) for k in range(KH)])
                    ins.then_inc(proj.full_of(part, f"fqk{m}"), 1)
                for j in range(2):
                    proj.wait_empty(pe, part, f"fv{j}")
                    group_of(proj.bank(part, f"fv{j}")[:, 0:HID],
                             [(hnT[:, k, j * P:(j + 1) * P], wv_sb[:, k]) for k in range(KH)])\
                        .then_inc(proj.full_of(part, f"fv{j}"), 1)

            def gate(part):
                turn.wait_read(pe, part, "z2T")
                for j in range(2):
                    mix.wait_empty(pe, part, f"gate{j}")
                    group_of(mix.bank(part, f"gate{j}")[:, 0:EXPERTS],
                             [(hn2T[:, k, j * P:(j + 1) * P], gate_w_sb[:, k]) for k in range(KH)])\
                        .then_inc(mix.full_of(part, f"gate{j}"), 1)

            def work(part):
                c, f, n = part.c, part.f, part.n
                if c is not None:
                    for m in range(4):
                        qk(part, m)
                if f is not None:
                    turn_rows(part, "hnT", z1, norm["1"]["out"], f)
                if c is not None:
                    qk(part, 4)
                if f is not None:
                    fqkv(part)
                if c is not None:
                    qk(part, 5)
                if f is not None:
                    for m in range(KH):
                        proj.wait_read(pe, part, f"fqk{m}")
                    fscores(part, 0)
                if c is not None:
                    qk(part, 6)
                if f is not None:
                    fscores(part, 1)
                if c is not None:
                    qk(part, 7)
                    values(part, 0, 0)
                    values(part, 0, 1)
                if f is not None:
                    if c is None:
                        fscores(part, 2)
                        fscores(part, 3)
                    if c is not None:
                        fscores(part, 2)
                    turn_probs(part, "f", fprobs, 0, f)
                    if c is not None:
                        fscores(part, 3)
                if c is not None:
                    scores(part, 0)
                    values(part, 1, 0)
                    scores(part, 1)
                if f is not None:
                    fmix_values(part, 0)
                if c is not None:
                    values(part, 1, 1)
                    scores(part, 2)
                if f is not None:
                    turn_probs(part, "f", fprobs, 1, f)
                if c is not None:
                    scores(part, 3)
                if f is not None:
                    fmix_values(part, 1)
                if c is not None:
                    turn_probs(part, "c", probs, 0, c)
                if f is not None:
                    fout(part, 0)
                    fout(part, 1)
                if c is not None:
                    mix_values(part, 0)
                    turn_probs(part, "c", probs, 1, c)
                    if part.kind == "first":
                        pe.wait_ge(out_w_landed, 16)
                    out_proj(part, 0)
                if f is not None:
                    turn_rows(part, "z2T", z2, norm["2"]["out"], f)
                if c is not None:
                    mix_values(part, 1)
                if n is not None:
                    tokens(part)
                if c is not None:
                    out_proj(part, 1)
                if n is not None:
                    turn_z(part)
                if f is not None:
                    gate(part)

            pe.wait_ge(consts_made, 3)
            pe.wait_ge(tok_w_landed, 16)
            work(Part("start"))
            pe.wait_ge(qkv_sorted, 3)
            first = Part("first")
            work(first)
            for g in range(2):
                turn.wait_read(pe, first, f"zT{g}")
            pe.wait_ge(vectors_landed, 128)
            pe.transpose(turn.banks[0][:, 0:ROWS], vector_rows[:], identity[0:ROWS, 0:ROWS]).then_inc(columns_turned, 1)
            pe.wait_ge(columns_ready, 1)
            pe.wait_ge(small_w_landed, 80)
            with pe.Fori(0, GROUPS - 2) as i:
                work(Part("body", i))
            work(Part("final"))
            work(Part("last"))

            pe.wait_ge(chosen_ready, 1)
            flat = chosen[:].rearrange("p e t -> p (e t)")
            pe.matmul(score.banks[0][:, 0:EXPERTS * TILES], earlier[:], flat, start=True, stop=True).then_inc(ranks_ready, 1)
            pe.matmul(score.banks[1][:, 0:EXPERTS * TILES], ones[:], flat, start=True, stop=True).then_inc(ranks_ready, 1)
            pe.wait_ge(slots_ready, 2)

            def expert(s):
                return pe.value_load(expert_of[0:1, bass.ds(s, 1)], min_val=0, max_val=EXPERTS - 1)

            def turn_in(s, buffer, pair):
                pe.wait_ge(slot_in_landed[buffer], (pair + 1) * 16)
                for k in range(KH):
                    ins = pe.transpose(turn.banks[0][:, k * P:(k + 1) * P], slot_in[:, buffer, k * P:(k + 1) * P],
                                       identity[:])
                ins.then_inc(slot_inT_full, 1)

            def up(s, buffer, first=False):
                pe.wait_ge(slot_inT_ready, s + 1)
                for n in range(2):
                    pe.wait_ge(w1_copied[n], s + 1)
                for half in range(2):
                    if not first:
                        pe.wait_ge(midT_ready[half], s)
                    for n in range(KF // 2):
                        at = (half * KF // 2 + n) * P
                        ins = group_of(score.banks[half][:, n * P:(n + 1) * P],
                                       [(w1_now[:, buffer, k, at:at + P], slot_inT[:, k]) for k in range(KH)])
                    ins.then_inc(midT_full[half], 1)

            def down(s, buffer, first=False):
                e = expert(s)
                for half in range(2):
                    pe.wait_ge(midT_ready[half], s + 1)
                if not first:
                    pe.wait_ge(slot_out_ready, s)
                group_of(mix.banks[0][:, 0:HID],
                         [(midT[:, buffer, c], expert_w[:, bass.ds(e, 1), KH * FFN + c * HID:KH * FFN + (c + 1) * HID])
                          for c in range(KF)]).then_inc(slot_out_full, 1)

            turn_in(0, 0, 0)
            up(0, 0, first=True)
            turn_in(1, 1, 0)

            def slot_tile(s, buffer, pair, first=False):
                up(s + 1, 1 - buffer)
                turn_in(s + 2, buffer, pair + 1)
                down(s, buffer, first)

            slot_tile(0, 0, 0, first=True)
            with pe.Fori(0, (SLOT_TILES - 3) // 2) as pair:
                slot_tile(2 * pair + 1, 1, pair)
                slot_tile(2 * pair + 2, 0, pair + 1)
            up(SLOT_TILES - 1, 0)
            down(SLOT_TILES - 2, 1)
            down(SLOT_TILES - 1, 0)


_INS = ["x", "L0_tok_W", "L0_attn_W_qkv", "L0_attn_W_out", "L0_ffn_ln1_g", "L0_ffn_ln1_b", "L0_ffn_ln2_g",
        "L0_ffn_ln2_b", "L0_ffn_wq", "L0_ffn_bq", "L0_ffn_wk", "L0_ffn_bk", "L0_ffn_wv", "L0_ffn_bv", "L0_ffn_wo",
        "L0_ffn_bo", "L0_ffn_gate_w", "L0_ffn_gate_b", "L0_ffn_w1", "L0_ffn_b1", "L0_ffn_w2", "L0_ffn_b2"]


def kernel(**inputs):
    import numpy as np
    import concourse.bacc as bacc
    from concourse.bass_utils import run_bass_kernel_spmd

    nc = bacc.Bacc("TRN2", target_bir_lowering=False, num_devices=1)
    arrays, args = {}, []
    for name in _INS:
        a = np.ascontiguousarray(inputs[name])
        arrays[f"in_{name}"] = a
        args.append(nc.dram_tensor(f"in_{name}", a.shape, mybir.dt.from_np(a.dtype), kind="ExternalInput").ap())
    args.append(nc.dram_tensor("tower_out", (IMAGES, TOKENS, HID), F32, kind="ExternalOutput").ap())
    vit_tower(nc, *args)
    r = run_bass_kernel_spmd(nc, [arrays], core_ids=[0])
    return r.results[0]["tower_out"]
```
